# Optimizing a Trainium2 kernel written in Bass

```python
import numpy as np
import jax
import jax.numpy as jnp

def _softmax(x, axis=-1):
    return jax.nn.softmax(x, axis=axis)

def _gelu(x):
    return jax.nn.gelu(x, approximate=True)

def _silu(x):
    return jax.nn.silu(x)

def _sigmoid(x):
    return jax.nn.sigmoid(x)

def _layernorm(x, axis=-1, eps=1e-05):
    m = jnp.mean(x, axis=axis, keepdims=True)
    v = jnp.var(x, axis=axis, keepdims=True)
    return (x - m) / jnp.sqrt(v + eps)

def _scatter_add(tgt, idx, src, axis=0):
    return tgt.at[idx].add(src)

def _segment_sum(src, seg, n):
    return jax.ops.segment_sum(src, seg, n)
kernel_name = 'mk_xattn_ffn_d1_seqx_r2_c568e7'

def setup_inputs(seed: int=0):
    np.random.seed(seed)
    _w = jnp.asarray

    def _rec_inputs():
        import jax
        import jax.numpy as jnp
        _rk = jax.random.key(seed)
        x = -0.0002928 + 1 * jax.random.normal(jax.random.fold_in(_rk, 1), (8, 512, 512), jnp.float32)
        _lenS = 512 - jax.random.randint(jax.random.fold_in(_rk, 7), (8,), 0, max(1, 512 // 4) + 1, jnp.int32)
        _lenS2 = 512 - jax.random.randint(jax.random.fold_in(_rk, 8), (8,), 0, max(1, 512 // 4) + 1, jnp.int32)
        _ctx_1024P = jax.random.normal(jax.random.fold_in(_rk, 11), (8, 16, 512), jnp.float32)
        _ctx_1024c = jax.random.dirichlet(jax.random.fold_in(_rk, 511), 0.3 * jnp.ones((16,), jnp.float32), (8, 512))
        _ctx_1024t = jnp.einsum('bsk,bkd->bsd', _ctx_1024c, _ctx_1024P)
        _ctx_1024t = _ctx_1024t * jax.lax.rsqrt(jnp.mean(jnp.square(_ctx_1024t)) + 1e-12) * 0.953939
        ctx_1024 = -1.39393e-06 + 0.999914 * (_ctx_1024t + 0.3 * jax.random.normal(jax.random.fold_in(_rk, 611), (8, 512, 512), jnp.float32))
        return (x, ctx_1024)
    x, ctx_1024 = _rec_inputs()

    def _L0_xattn_setup():
        import jax, jax.numpy as jnp
        import numpy as np
        import math
        EMBED_DIM = 512
        NUM_HEADS = 16
        HEAD_DIM = EMBED_DIM // NUM_HEADS
        ROPE_BASE = 10000.0

        def _rope_cache(seq_len, dim, dtype=jnp.float32):
            inv_freq = 1.0 / ROPE_BASE ** (jnp.arange(0, dim, 2, dtype=jnp.float32) / dim)
            t = jnp.arange(seq_len, dtype=jnp.float32)
            freqs = t[:, None] * inv_freq[None, :]
            emb = jnp.concatenate([freqs, freqs], axis=-1)
            return (jnp.cos(emb).astype(dtype), jnp.sin(emb).astype(dtype))

        def _rotate_half(x):
            x1, x2 = jnp.split(x, 2, axis=-1)
            return jnp.concatenate([-x2, x1], axis=-1)
        key = jax.random.key(seed)
        ks = jax.random.split(key, 12)
        B, S, E = (2, 1024, EMBED_DIM)
        s = 1.0 / math.sqrt(E)
        inp = {'query': jax.random.normal(ks[0], (B, S, E), jnp.float32), 'key': jax.random.normal(ks[1], (B, S, E), jnp.float32), 'value': jax.random.normal(ks[2], (B, S, E), jnp.float32), 'Wq': jax.random.normal(ks[3], (E, E), jnp.float32) * s, 'bq': jnp.zeros((E,), jnp.float32), 'Wk': jax.random.normal(ks[4], (E, E), jnp.float32) * s, 'bk': jnp.zeros((E,), jnp.float32), 'Wv': jax.random.normal(ks[5], (E, E), jnp.float32) * s, 'bv': jnp.zeros((E,), jnp.float32), 'Wo': jax.random.normal(ks[6], (E, E), jnp.float32) * s, 'bo': jnp.zeros((E,), jnp.float32)}
        return inp
    _L0_xattn_all = _L0_xattn_setup()
    _L0_xattn_in = {k: v for k, v in _L0_xattn_all.items() if k in ('Wq', 'bq', 'Wk', 'bk', 'Wv', 'bv', 'Wo', 'bo')}
    del _L0_xattn_all

    def _L0_ffn_setup():
        import jax, jax.numpy as jnp
        import numpy as np
        BLOCK = 32
        W_BITS = 4
        ACT_BITS = 16

        def act_qdq(x):
            qmax = 2.0 ** (ACT_BITS - 1) - 1.0
            scale = jnp.maximum(jnp.max(jnp.abs(x)) / qmax, 1e-12)
            return jnp.clip(jnp.round(x / scale), -qmax - 1.0, qmax) * scale

        def fixed_qdq_u16(x):
            scale = 1.0 / 65536.0
            return jnp.clip(jnp.round(x / scale), 0.0, 65535.0) * scale

        def lpbq_dequant(w):
            O, I = w.shape
            qmax = 2.0 ** (W_BITS - 1) - 1.0
            wb = w.reshape(O, I // BLOCK, BLOCK)
            s = jnp.maximum(jnp.max(jnp.abs(wb), axis=-1, keepdims=True) / qmax, 1e-12)
            wq = jnp.clip(jnp.round(wb / s), -qmax - 1.0, qmax) * s
            return wq.reshape(O, I)
        key = jax.random.key(seed)
        k1, k2, k3, k4 = jax.random.split(key, 4)
        B, S, H, I = (2, 2048, 512, 1536)
        x = jax.random.normal(k1, (B, S, H), jnp.float32)
        w_gate = jax.random.normal(k2, (I, H), jnp.float32) * 0.02
        w_up = jax.random.normal(k3, (I, H), jnp.float32) * 0.02
        w_down = jax.random.normal(k4, (H, I), jnp.float32) * 0.02
        return {'x': x, 'w_gate': w_gate, 'w_up': w_up, 'w_down': w_down}
    _L0_ffn_all = _L0_ffn_setup()
    _L0_ffn_in = {k: v for k, v in _L0_ffn_all.items() if k in ('w_gate', 'w_up', 'w_down')}
    del _L0_ffn_all
    return {'x': x, 'ctx_1024': ctx_1024, 'L0_xattn_Wq': _L0_xattn_in['Wq'], 'L0_xattn_bq': _L0_xattn_in['bq'], 'L0_xattn_Wk': _L0_xattn_in['Wk'], 'L0_xattn_bk': _L0_xattn_in['bk'], 'L0_xattn_Wv': _L0_xattn_in['Wv'], 'L0_xattn_bv': _L0_xattn_in['bv'], 'L0_xattn_Wo': _L0_xattn_in['Wo'], 'L0_xattn_bo': _L0_xattn_in['bo'], 'L0_ffn_w_gate': _L0_ffn_in['w_gate'], 'L0_ffn_w_up': _L0_ffn_in['w_up'], 'L0_ffn_w_down': _L0_ffn_in['w_down']}

def reference(x, ctx_1024, L0_xattn_Wq, L0_xattn_bq, L0_xattn_Wk, L0_xattn_bk, L0_xattn_Wv, L0_xattn_bv, L0_xattn_Wo, L0_xattn_bo, L0_ffn_w_gate, L0_ffn_w_up, L0_ffn_w_down):
    import jax
    import jax.numpy as jnp

    def _L0_xattn_ref(query, key, value, Wq, bq, Wk, bk, Wv, bv, Wo, bo):
        import jax, jax.numpy as jnp
        import numpy as np
        import math
        EMBED_DIM = 512
        NUM_HEADS = 16
        HEAD_DIM = EMBED_DIM // NUM_HEADS
        ROPE_BASE = 10000.0

        def _rope_cache(seq_len, dim, dtype=jnp.float32):
            inv_freq = 1.0 / ROPE_BASE ** (jnp.arange(0, dim, 2, dtype=jnp.float32) / dim)
            t = jnp.arange(seq_len, dtype=jnp.float32)
            freqs = t[:, None] * inv_freq[None, :]
            emb = jnp.concatenate([freqs, freqs], axis=-1)
            return (jnp.cos(emb).astype(dtype), jnp.sin(emb).astype(dtype))

        def _rotate_half(x):
            x1, x2 = jnp.split(x, 2, axis=-1)
            return jnp.concatenate([-x2, x1], axis=-1)
        B, S, E = query.shape
        H, D = (NUM_HEADS, HEAD_DIM)

        def proj(x, W, b):
            return (x @ W.T + b).reshape(B, -1, H, D).transpose(0, 2, 1, 3)
        q = proj(query, Wq, bq)
        k = proj(key, Wk, bk)
        v = proj(value, Wv, bv)
        cos, sin = _rope_cache(S, D, q.dtype)
        cos = cos[None, None]
        sin = sin[None, None]
        q = q * cos + _rotate_half(q) * sin
        k = k * cos + _rotate_half(k) * sin
        scale = 1.0 / math.sqrt(D)
        scores = jnp.einsum('bhsd,bhtd->bhst', q, k) * scale
        causal = jnp.triu(jnp.ones((S, S), bool), k=1)
        scores = jnp.where(causal[None, None], -jnp.inf, scores)
        attn = jax.nn.softmax(scores, axis=-1)
        out = jnp.einsum('bhst,bhtd->bhsd', attn, v)
        out = out.transpose(0, 2, 1, 3).reshape(B, S, E)
        return out @ Wo.T + bo

    def _L0_ffn_ref(x, w_gate, w_up, w_down):
        import jax, jax.numpy as jnp
        import numpy as np
        BLOCK = 32
        W_BITS = 4
        ACT_BITS = 16

        def act_qdq(x):
            qmax = 2.0 ** (ACT_BITS - 1) - 1.0
            scale = jnp.maximum(jnp.max(jnp.abs(x)) / qmax, 1e-12)
            return jnp.clip(jnp.round(x / scale), -qmax - 1.0, qmax) * scale

        def fixed_qdq_u16(x):
            scale = 1.0 / 65536.0
            return jnp.clip(jnp.round(x / scale), 0.0, 65535.0) * scale

        def lpbq_dequant(w):
            O, I = w.shape
            qmax = 2.0 ** (W_BITS - 1) - 1.0
            wb = w.reshape(O, I // BLOCK, BLOCK)
            s = jnp.maximum(jnp.max(jnp.abs(wb), axis=-1, keepdims=True) / qmax, 1e-12)
            wq = jnp.clip(jnp.round(wb / s), -qmax - 1.0, qmax) * s
            return wq.reshape(O, I)
        x = act_qdq(x)
        up = act_qdq(x @ lpbq_dequant(w_up).T)
        gate = act_qdq(x @ lpbq_dequant(w_gate).T)
        sig = fixed_qdq_u16(jax.nn.sigmoid(gate))
        gate = act_qdq(gate * sig)
        o = act_qdq(gate * up)
        return o @ lpbq_dequant(w_down).T
    x = x + _L0_xattn_ref(_layernorm(x, axis=-1), ctx_1024, ctx_1024, L0_xattn_Wq, L0_xattn_bq, L0_xattn_Wk, L0_xattn_bk, L0_xattn_Wv, L0_xattn_bv, L0_xattn_Wo, L0_xattn_bo)
    x = x + _L0_ffn_ref(_layernorm(x, axis=-1), L0_ffn_w_gate, L0_ffn_w_up, L0_ffn_w_down)
    return x

_drawn_inputs = setup_inputs


def setup_inputs(seed=0):
    import zlib

    import numpy as np

    out = dict(_drawn_inputs(seed))
    spreads = {'L0_xattn_bq': (0.0, 0.468),
     'L0_xattn_bk': (0.0, 0.8),
     'L0_xattn_bv': (0.0, 0.1),
     'L0_xattn_bo': (0.0, 0.1)}
    factors = {}
    for name, (base, spread) in spreads.items():
        noise = np.random.default_rng([zlib.crc32(name.encode()), seed]).standard_normal(out[name].shape)
        drawn = base * np.exp(spread * noise) if base else spread * noise
        out[name] = jnp.asarray(drawn.astype(out[name].dtype))
    for name, factor in factors.items():
        out[name] = (out[name] * factor).astype(out[name].dtype)
    return out
```

```python
from contextlib import ExitStack

import concourse.bass as bass
import numpy as np
from concourse import mybir
from concourse.alu_op_type import AluOpType as ALU

F32, F16, BF16 = mybir.dt.float32, mybir.dt.float16, mybir.dt.bfloat16
I16, U16 = mybir.dt.int16, mybir.dt.uint16
ACT = mybir.ActivationFunctionType
AXX = mybir.AxisListType.X

P = 128
B, S, E = 8, 512, 512
H, D = 16, 32
I = 1536
C = E // P
ST = S // P
HG = P // D
IC = I // P
BLOCK = 32
EPS = 1e-5
TINY = 1e-12
QMAX_W, QMAX_A = 7.0, 32767.0

X_UP = 16.0
W_UP = 256.0
QK_UP = 8.0
PROJ_DOWN = 1.0 / (X_UP * W_UP)
M_DOWN = 64.0
EXP_SCALE = 1.0 / (float(np.sqrt(D)) * QK_UP * QK_UP)
MASKED = -float(2.0 ** 100)
ROLE_Q = ("hi", "lo", "hi")
ROLE_K = ("hi", "hi", "lo")
KROWS = 3 * D
MROWS = KROWS + 2

PAIRS_LOOPED = 2


class Count:

    def __init__(self, sem):
        self.sem, self.n, self.turn, self.growth = sem, 0, None, 0

    def value(self, back=0):
        assert self.turn is None or self.n > back
        return self.n - back if self.turn is None else self.turn * self.growth + (self.n - back)

    def up(self, k=1):
        self.n += k
        return self.value()

    def enter(self, turn, growth):
        self.turn, self.growth, self.entered = turn, growth, self.n

    def leave(self, turns):
        assert self.n - self.entered == self.growth, (self.sem, self.n - self.entered, self.growth)
        self.turn, self.n = None, self.n + (turns - 1) * self.growth


def wait(eng, count_or_sem, value=None, past=None):
    sem = count_or_sem.sem if isinstance(count_or_sem, Count) else count_or_sem
    if value is None:
        value = count_or_sem.value()
    if not isinstance(value, int) or value > 0:
        eng.wait_ge(sem, value)
        if past and not isinstance(value, int):
            eng.sem_inc(past, 1)


class Batch:

    def __init__(self, c, turn=None):
        self.c, self.turn, self.par = c, turn, c % 2

    def index(self):
        return self.c if self.turn is None else self.turn * 2 + self.c

    def step(self, k):
        return Batch(self.c + k, self.turn)


def weight_stage(nc, wf, attn_w, wf_parts, wa_parts):
    N = 3 * IC // 2
    NB = 2 * 512 // BLOCK
    with ExitStack() as ctx:
        def sb(n, s, d):
            return ctx.enter_context(nc.sbuf_tensor("w_" + n, s, d))

        raw = [sb(f"raw{k}", [P, 2, 512], F32) for k in range(2)]
        top = sb("top", [P, 2, NB], F32)
        inv = sb("inv", [P, 2, NB], F32)
        ints = sb("ints", [P, 2, 2 * 512], I16)
        deq = [sb(f"deq{k}", [P, 2, 512], F32) for k in range(2)]
        parts = [sb(f"parts{k}", [P, 2, 2, 512], F16) for k in range(2)]
        ident = sb("ident", [P, P], F32)
        aw = [sb(f"aw{k}", [P, C, E], F32) for k in range(2)]
        ap = [sb(f"ap{k}", [P, 2, C, E], F16) for k in range(2)]
        bank = [ctx.enter_context(nc.psum_tensor(f"w_bank{k}", [P, 2, 512], F32)) for k in range(2)]

        def sem(n):
            return ctx.enter_context(nc.semaphore("w_" + n))

        s_in = [sem(f"in{k}") for k in range(2)]
        s_out = [sem(f"out{k}") for k in range(2)]
        s_q = sem("quant")
        s_t = sem("transposed")
        s_hi = sem("hi")
        s_lo = sem("lo")
        s_ain = [sem(f"ain{k}") for k in range(2)]
        s_ahi, s_alo = sem("ahi"), sem("alo")
        s_aout = [sem(f"aout{k}") for k in range(2)]
        s_id = sem("id")

        with nc.Block() as block:
            @block.sync
            def _(sp):
                def load(k, n):
                    sp.dma_start(raw[k][:], wf[n].rearrange("k p c -> p k c")).then_inc(s_in[k], 16)

                def store(k, n):
                    sp.wait_ge(s_lo, n + 1)
                    sp.dma_start(wf_parts[n].rearrange("k p a c -> p k a c"), parts[k][:]).then_inc(s_out[k], 16)

                for m in range(4):
                    k = m % 2
                    if m >= 2:
                        sp.wait_ge(s_alo, m - 1)
                    sp.dma_start(aw[k][:], attn_w[m]).then_inc(s_ain[k], 16)
                load(0, 0)
                load(1, 1)
                for m in range(4):
                    sp.wait_ge(s_alo, m + 1)
                    sp.dma_start(wa_parts[m], ap[m % 2][:]).then_inc(s_aout[m % 2], 16)
                with sp.Fori(0, N // 2 - 1) as i:
                    for k in range(2):
                        n = i * 2 + k
                        sp.wait_ge(s_q, n * 5 + 4)
                        load(k, n + 2)
                        store(k, n)
                for k in range(2):
                    store(k, N - 2 + k)
                for k in range(2):
                    sp.wait_ge(s_out[k], 16 * (N // 2))
                    sp.wait_ge(s_aout[k], 32)

            @block.gpsimd
            def _(pool):
                pool.memset(ident[:], 0.0).then_inc(s_id, 1)
                pool.wait_ge(s_id, 1)
                pool.affine_select(out=ident[:], in_=ident[:], compare_op=ALU.not_equal, fill=1.0, base=0,
                                   pattern=[[-1, P]], channel_multiplier=1).then_inc(s_id, 1)

            @block.scalar
            def _(act):
                for m in range(4):
                    act.wait_ge(s_ain[m % 2], 16 * (m // 2 + 1))
                    if m >= 2:
                        act.wait_ge(s_aout[m % 2], 16)
                    act.activation(ap[m % 2][:, 0], aw[m % 2][:], ACT.Copy, scale=W_UP).then_inc(s_ahi, 1)

                def pair(k, n, first):
                    act.wait_ge(s_t, n + 1)
                    if not first:
                        act.wait_ge(s_out[k], n * 8 - k * 8)
                    act.activation(parts[k][:, :, 0], bank[k][:], ACT.Copy, scale=W_UP).then_inc(s_hi, 1)

                pair(0, 0, True)
                pair(1, 1, True)
                with act.Fori(1, N // 2) as i:
                    for k in range(2):
                        pair(k, i * 2 + k, False)

            @block.vector
            def _(dve):
                for m in range(4):
                    dve.wait_ge(s_ahi, m + 1)
                    dve.scalar_tensor_tensor(ap[m % 2][:, 1], aw[m % 2][:], W_UP, ap[m % 2][:, 0],
                                             ALU.mult, ALU.subtract).then_inc(s_alo, 1)

                def quantise(k, n):
                    dve.wait_ge(s_in[k], n * 8 - k * 8 + 16)
                    blocks = raw[k][:].rearrange("p k (b c) -> p (k b) c", c=BLOCK)
                    dve.tensor_reduce(top[:, k], blocks, AXX, ALU.max, apply_absolute_value=True).then_inc(s_q, 1)
                    dve.wait_ge(s_q, n * 5 + 1)
                    dve.tensor_scalar(top[:, k], top[:, k], 1.0 / QMAX_W, TINY, ALU.mult, ALU.max).then_inc(s_q, 1)
                    dve.wait_ge(s_q, n * 5 + 2)
                    dve.reciprocal(inv[:, k], top[:, k]).then_inc(s_q, 1)
                    dve.wait_ge(s_q, n * 5 + 3)
                    q = ints[:, k].rearrange("p (b c) -> p b c", c=BLOCK)
                    dve.tensor_tensor(q, blocks, inv[:, k].unsqueeze(2).to_broadcast([P, NB, BLOCK]),
                                      ALU.mult).then_inc(s_q, 1)
                    dve.wait_ge(s_q, n * 5 + 4)
                    w = deq[k][:].rearrange("p k (b c) -> p (k b) c", c=BLOCK)
                    dve.tensor_tensor(w, q, top[:, k].unsqueeze(2).to_broadcast([P, NB, BLOCK]),
                                      ALU.mult).then_inc(s_q, 1)

                def low(k, n):
                    dve.wait_ge(s_hi, n + 1)
                    dve.scalar_tensor_tensor(parts[k][:, :, 1], bank[k][:], W_UP, parts[k][:, :, 0],
                                             ALU.mult, ALU.subtract).then_inc(s_lo, 1)

                quantise(0, 0)
                quantise(1, 1)
                low(0, 0)
                with dve.Fori(1, N // 2) as i:
                    quantise(0, i * 2)
                    low(1, i * 2 - 1)
                    quantise(1, i * 2 + 1)
                    low(0, i * 2)
                low(1, N - 1)

            @block.tensor
            def _(pe):
                pe.wait_ge(s_id, 2)

                def pair(k, n, first):
                    pe.wait_ge(s_q, n * 5 + 5)
                    if not first:
                        pe.wait_ge(s_lo, n - 1)
                    for t in range(2):
                        for c in range(C):
                            cols = slice(c * P, (c + 1) * P)
                            last = pe.transpose(bank[k][:, t, cols], deq[k][:, t, cols], ident[:])
                    last.then_inc(s_t, 1)

                pair(0, 0, True)
                pair(1, 1, True)
                with pe.Fori(1, N // 2) as i:
                    for k in range(2):
                        pair(k, i * 2 + k, False)


def attention_stage(nc, x, ctxT, wa_parts, biases, rope, x1, xn2T, peak):
    with ExitStack() as ctx:
        def sb(n, s, d):
            return ctx.enter_context(nc.sbuf_tensor("a_" + n, s, d))

        def sem(n):
            return ctx.enter_context(nc.semaphore("a_" + n))

        W = {m: sb("W" + m, [P, 2, C, E], F16) for m in "qkvo"}
        b_q, b_k, b_v = (sb("b" + m, [P, C], F32) for m in "qkv")
        b_o = sb("bo", [P, E], F32)
        cos, sin = sb("cos", [P, S], F32), sb("sin", [P, S], F32)
        xt = sb("xt", [P, ST, E], F32)
        ct = sb("ct", [P, C, S], F32)
        sum1 = [ct[:, k] for k in range(2)]
        resid = ct[:, 2]
        xp = sb("xp", [P, 2, C, S], F16)
        cp = sb("cp", [P, 2, C, S], F16)
        tmp = sb("tmp", [P, 4, S], F32)
        rot = sb("rot", [P, 2, S], F32)
        qkp = sb("qkp", [P, 2, C, S], F16)
        qs = [sb(f"qs{k}", [P, C, HG, S], F16) for k in range(2)]
        ks = [sb(f"ks{k}", [P, C, HG, S], F16) for k in range(2)]
        v = sb("v", [P, ST, E], F32)
        pt = sb("pt", [P, 10, S], F32)
        rden, att = sb("rden", [P, S], F32), sb("att", [P, S], F32)
        aop = [sb(f"aop{k}", [P, 2, C, S], F16) for k in range(2)]
        mx = sb("mx", [P, ST, HG], F32)
        mp = sb("mp", [P, ST, 2, HG], F16)
        mrow = sb("mrow", [2 * HG, S], F16)
        stats, mv = sb("stats", [P, ST, 6], F32), sb("mv", [P, ST, 2], F32)
        rstd, power = sb("rstd", [P, ST], F32), sb("power", [P, ST], F32)
        stats2, mv2, rstd2 = sb("stats2", [P, ST, 6], F32), sb("mv2", [P, ST, 2], F32), sb("rstd2", [P, ST], F32)
        peak_b = sb("peakb", [P, ST], F32)
        ident = sb("ident", [P, P], F32)
        ident16, identb = sb("ident16", [P, P], F16), sb("identb", [P, P], BF16)
        mask_s, mask_t = sb("mask_s", [P, P], BF16), sb("mask_t", [P, P], BF16)
        ones = sb("ones", [P, D], F32)

        def ps(n, d=F32):
            return ctx.enter_context(nc.psum_tensor("a_" + n, [P, 512], d))

        proj = [ps(f"proj{k}") for k in range(2)]
        sc = [ps(f"sc{k}") for k in range(2)]
        sct = [ps(f"sct{k}") for k in range(2)]
        ps_o, ps_d = ps("o"), ps("d")

        s_const = sem("const")
        s_w = sem("w")
        s_dc = sem("dve_const")
        s_x, s_c = sem("x_in"), sem("c_in")
        s_ln = sem("ln_stats")
        s_rstd = sem("ln_rstd")
        s_xn = sem("xn")
        s_chi, s_clo = sem("c_hi"), sem("c_lo")
        s_full = sem("proj_full")
        s_evac = sem("proj_evac")
        s_rot = sem("rotated")
        s_cos, s_mul = sem("times_cos"), sem("rot_times_sin")
        s_sum = sem("rope_sum")
        s_hi, s_lo = sem("hi"), sem("lo")
        s_kst, s_qst = sem("k_stacked"), sem("q_stacked")
        s_sfull, s_sread = sem("sc_full"), sem("sc_read")
        s_m = sem("m_parts")
        s_min = sem("m_placed")
        s_tfull, s_exp = sem("sct_full"), sem("exp")
        s_pv, s_pvread, s_norm = sem("pv"), sem("pv_read"), sem("norm")
        s_aohi, s_aolo = sem("ao_hi"), sem("ao_lo")
        s_res, s_resb = sem("resid_in"), sem("resid_bias")
        s_x1, s_ln2, s_rstd2, s_xn2, s_peak = sem("x1"), sem("ln2_stats"), sem("ln2_rstd"), sem("xn2"), sem("peak")
        s_x1out = [sem(f"x1_out{k}") for k in range(2)]
        s_xn2out = sem("xn2_out")

        growth = {
            s_x: 32, s_c: 32, s_ln: 16, s_rstd: 4, s_xn: 8, s_chi: 2, s_clo: 2, s_full: 48, s_evac: 48,
            s_rot: 16, s_cos: 16, s_mul: 16, s_sum: 16, s_hi: 24, s_lo: 24, s_kst: 384, s_qst: 384,
            s_sfull: 88, s_sread: 88, s_m: 16, s_min: 256, s_tfull: 80, s_exp: 80, s_pv: 8, s_pvread: 16,
            s_norm: 16, s_aohi: 8, s_aolo: 8, s_res: 128, s_resb: 8, s_x1: 8, s_ln2: 16, s_rstd2: 16,
            s_xn2: 8, s_peak: 10, s_x1out[0]: 64, s_x1out[1]: 64, s_xn2out: 32,
        }

        def run(eng, counts, turn):
            turn(Batch(-1), False, True)
            turn(Batch(0), False, True)
            turn(Batch(1), True, True)
            with eng.Fori(0, PAIRS_LOOPED) as i:
                for c in counts:
                    c.enter(i, growth[c.sem])
                turn(Batch(2, i), True, True)
                turn(Batch(3, i), True, True)
            for c in counts:
                c.leave(PAIRS_LOOPED)
            turn(Batch(6), True, True)
            turn(Batch(7), True, False)
            turn(Batch(8), True, False)

        def order(b, has_prev, has_next):
            here, n, p = 0 <= b.c < B, b.step(1), b.step(-1)
            for step in (
                ("load", n), ("exp", b, 0), ("norm_x", n), ("c_parts", n), ("pv", b, 0), ("scores", b, 1),
                ("x", n), ("ao_norm", b, 0), ("rows", b, 1), ("out", p, (0, 1)), ("ao_parts", b, 0),
                ("exp", b, 1), ("out", p, (2, 3)), ("pv", b, 1), ("out_end", p), ("scores", b, 2),
                ("k", n, (0, 1)), ("rows", b, 2), ("ao_norm", b, 1), ("k", n, (2, 3)),
                ("exp", b, 2), ("k_end", n), ("ao_parts", b, 1), ("xn2", p), ("q", n, (0,)), ("pv", b, 2),
                ("scores", b, 3), ("q", n, (1, 2)),
                ("rows", b, 3), ("ao_norm", b, 2), ("q", n, (3,)),
                ("exp", b, 3), ("q_end", n), ("ao_parts", b, 2), ("pv", b, 3), ("v", n, (0, 1, 2)),
                ("ao_norm", b, 3), ("scores", n, 0), ("ao_parts", b, 3), ("v", n, (3,)), ("rows", n, 0),
            ):
                if step[1] is b and here or step[1] is n and has_next or step[1] is p and has_prev:
                    yield step

        def heads_blocks(pair, transposed):
            a, z = 2 * pair, 2 * pair + 1
            if transposed:
                return [[(a, 0, 0)], [(a, 1, 0), (a, 3, 384)], [(z, 0, 0)], [(z, 1, 0), (z, 3, 384)],
                        [(a, 2, 0), (z, 2, 256)]]
            return [[(a, 3, 0)], [(a, 2, 0), (a, 0, 384)], [(z, 3, 0)], [(z, 2, 0), (z, 0, 384)],
                    [(a, 1, 0), (z, 1, 256)]]

        def stack(sp, dst, src, roles, s):
            for j in range(HG):
                for r, role in enumerate(roles):
                    sp.dma_start(dst[r * D:(r + 1) * D, :, j, :],
                                 src[j * D:(j + 1) * D, 0 if role == "hi" else 1, :, :]).then_inc(s, 16)
        s_past = {e: sem(f"past_{e}") for e in ("sp", "pool", "dve", "act")}

        with nc.Block() as block:
            @block.sync
            def _(sp):
                def sp_wait(*what):
                    wait(sp, *what, past=s_past["sp"])

                for n, m in enumerate("qkvo"):
                    sp.dma_start(W[m][:], wa_parts[n]).then_inc(s_w, 16)
                for dst, src in ((b_q, biases[0]), (b_k, biases[1]), (b_v, biases[2])):
                    sp.dma_start(dst[:], src).then_inc(s_w, 16)
                sp.dma_start(b_o[:], biases[3]).then_inc(s_w, 16)
                sp.dma_start(cos[:], rope[0]).then_inc(s_w, 16)
                sp.dma_start(sin[:], rope[1]).then_inc(s_w, 16)
                full, sread, x1c, lo = (Count(s) for s in (s_full, s_sread, s_x1, s_lo))
                evac, clo = Count(s_evac), Count(s_clo)
                x1out, xn2out = [Count(s) for s in s_x1out], Count(s_xn2out)
                counts = [full, sread, x1c, lo, evac, clo, *x1out, xn2out]

                def turn(b, has_prev, has_next):
                    for kind, t, *arg in order(b, has_prev, has_next):
                        if kind == "load":
                            sp_wait(full)
                            for c in x1out:
                                sp_wait(c)
                            sp_wait(xn2out)
                            sp.dma_start(xt[:], x[t.index()].rearrange("(s p) e -> p s e", p=P)).then_inc(s_x, 16)
                            sp_wait(clo)
                            sp.dma_start(ct[:], ctxT[t.index()].rearrange("(c p) t -> p c t", p=P)).then_inc(s_c, 16)
                        elif kind == "c_parts":
                            clo.up()
                        elif kind == "x":
                            full.up(4), evac.up(4), lo.up(4)
                        elif kind in "kqv":
                            full.up(len(arg[0])), evac.up(len(arg[0]))
                            if kind != "v":
                                lo.up(len(arg[0]))
                        elif kind == "k_end":
                            sp_wait(lo)
                            stack(sp, ks[t.par], qkp, ROLE_K, s_kst)
                        elif kind == "q_end":
                            sp_wait(lo)
                            stack(sp, qs[t.par], qkp, ROLE_Q, s_qst)
                        elif kind == "scores":
                            sread.up(10)
                        elif kind == "rows":
                            sp_wait(s_sread, sread.up())
                            for part in range(2):
                                sp.dma_start(qs[t.par][KROWS + part:KROWS + part + 1, arg[0], :, :],
                                             mrow[part * HG:(part + 1) * HG, :]).then_inc(s_min, 16)
                        elif kind == "out":
                            full.up(len(arg[0])), evac.up(len(arg[0]))
                            for st in arg[0]:
                                if st == 0:
                                    sp_wait(clo)
                                    sp_wait(xn2out)
                                sp_wait(x1c)
                                rows = slice(st * P, (st + 1) * P)
                                sp.dma_start(resid, x[t.index(), rows, :]).then_inc(s_res, 16)
                                sp_wait(s_x1, x1c.up())
                                sp.dma_start(x1[t.index(), rows, :], sum1[st % 2]).then_inc(s_x1out[st % 2], 16)
                                x1out[st % 2].up(16)
                        elif kind == "xn2":
                            full.up(ST)
                            sp_wait(s_evac, evac.up(ST))
                            sp.dma_start(xn2T[t.index()], ct[:]).then_inc(s_xn2out, 16)
                            xn2out.up(16)

                run(sp, counts, turn)
                for c in x1out:
                    sp_wait(c)
                sp_wait(xn2out)

            @block.gpsimd
            def _(pool):
                def pool_wait(*what):
                    wait(pool, *what, past=s_past["pool"])

                pool.memset(power[:], -0.5).then_inc(s_const, 1)
                pool.memset(ident[:], 0.0).then_inc(s_const, 1)
                pool.memset(ident16[:], 0.0).then_inc(s_const, 1)
                pool.memset(identb[:], 0.0).then_inc(s_const, 1)
                pool.memset(mask_s[:], 0.0).then_inc(s_const, 1)
                pool.memset(mask_t[:], 0.0).then_inc(s_const, 1)
                pool.memset(ones[:], 1.0).then_inc(s_const, 1)
                pool.wait_ge(s_const, 7)
                for t in (ident, ident16, identb):
                    pool.affine_select(out=t[:], in_=t[:], compare_op=ALU.not_equal, fill=1.0, base=0,
                                       pattern=[[-1, P]], channel_multiplier=1).then_inc(s_const, 1)
                pool.affine_select(out=mask_s[:], in_=mask_s[:], compare_op=ALU.is_ge, fill=MASKED, base=0,
                                   pattern=[[-1, P]], channel_multiplier=1).then_inc(s_const, 1)
                pool.affine_select(out=mask_t[:], in_=mask_t[:], compare_op=ALU.is_ge, fill=MASKED, base=0,
                                   pattern=[[1, P]], channel_multiplier=-1).then_inc(s_const, 1)
                pool.wait_ge(s_w, 160)
                ln, rotc, rstdc, res, ln2, rstd2c, xn1 = (
                    Count(s) for s in (s_ln, s_rot, s_rstd, s_res, s_ln2, s_rstd2, s_xn))
                counts = [ln, rotc, rstdc, res, ln2, rstd2c, xn1]

                def turn(b, has_prev, has_next):
                    for kind, t, *arg in order(b, has_prev, has_next):
                        if kind == "norm_x":
                            pool_wait(s_ln, ln.up(8))
                            pool_wait(xn1)
                            pool.tensor_scalar(rstd[:], mv[:, :, 1], EPS, None, ALU.add).then_inc(s_rstd, 1)
                            pool_wait(s_rstd, rstdc.up())
                            pool.tensor_tensor(rstd[:], rstd[:], power[:], ALU.pow).then_inc(s_rstd, 1)
                            rstdc.up()
                            xn1.up(4)
                        elif kind in "kq":
                            for eo in arg[0]:
                                pool_wait(s_rot, rotc.up())
                                pool.tensor_tensor(rot[:, eo % 2], rot[:, eo % 2], sin[:], ALU.mult).then_inc(s_mul, 1)
                        elif kind == "out":
                            for st in arg[0]:
                                pool_wait(s_res, res.up(16))
                                pool.tensor_tensor(resid, resid, b_o[:], ALU.add).then_inc(s_resb, 1)
                                pool_wait(s_ln2, ln2.up(2))
                                pool.tensor_scalar(rstd2[:, st:st + 1], mv2[:, st, 1:2], EPS, None,
                                                   ALU.add).then_inc(s_rstd2, 1)
                                pool_wait(s_rstd2, rstd2c.up())
                                pool.tensor_tensor(rstd2[:, st:st + 1], rstd2[:, st:st + 1], power[:, 0:1],
                                                   ALU.pow).then_inc(s_rstd2, 1)
                                rstd2c.up()

                run(pool, counts, turn)

            @block.scalar
            def _(act):
                full, lo, xn2c, clo = (Count(s) for s in (s_full, s_lo, s_xn2, s_clo))
                tfull, pv, c_in, summ, norm, aolo = (Count(s) for s in (s_tfull, s_pv, s_c, s_sum, s_norm, s_aolo))
                kst, qst = Count(s_kst), Count(s_qst)
                x1out, xn2out = [Count(s) for s in s_x1out], Count(s_xn2out)
                counts = [full, lo, xn2c, clo, tfull, pv, c_in, summ, norm, aolo, kst, qst, *x1out, xn2out]
                act.wait_ge(s_w, 160)
                act.wait_ge(s_dc, 4)

                def high(item):
                    wait(act, s_sum, summ.up())
                    act.activation(qkp[:, 0, item], tmp[:, item], ACT.Copy).then_inc(s_hi, 1)

                def turn(b, has_prev, has_next):
                    for kind, t, *arg in order(b, has_prev, has_next):
                        if kind == "c_parts":
                            wait(act, s_c, c_in.up(16))
                            act.activation(cp[:, 0], ct[:], ACT.Copy, scale=X_UP).then_inc(s_chi, 1)
                            clo.up()
                        elif kind == "x":
                            for ec in range(C):
                                wait(act, s_full, full.up())
                                wait(act, s_lo, lo.value(3))
                                act.activation(xp[:, 0, ec], proj[ec % 2][:], ACT.Copy, scale=X_UP).then_inc(s_hi, 1)
                                act.activation(tmp[:, ec], proj[ec % 2][:], ACT.Copy, scale=X_UP).then_inc(s_evac, 1)
                                lo.up()
                        elif kind in "kq":
                            bias = b_k if kind == "k" else b_q
                            for eo in arg[0]:
                                wait(act, s_full, full.up())
                                wait(act, s_lo, lo.value(3))
                                act.activation(tmp[:, eo], proj[eo % 2][:], ACT.Identity, bias=bias[:, eo:eo + 1],
                                               scale=PROJ_DOWN * QK_UP).then_inc(s_evac, 1)
                                lo.up()
                                if eo == 2:
                                    wait(act, qst if kind == "k" else kst)
                                if eo >= 2:
                                    high(eo - 2)
                        elif kind in ("k_end", "q_end"):
                            high(2)
                            high(3)
                            (kst if kind == "k_end" else qst).up(192)
                        elif kind == "v":
                            for tb in arg[0]:
                                wait(act, s_full, full.up())
                                act.activation(v[:, tb], proj[tb % 2][:], ACT.Copy, scale=PROJ_DOWN * X_UP).then_inc(s_evac, 1)
                        elif kind == "exp":
                            for u in range(10):
                                wait(act, s_tfull, tfull.up())
                                if u == 0:
                                    wait(act, pv)
                                act.activation(pt[:, u], sct[u % 2][:], ACT.Exp, scale=EXP_SCALE).then_inc(s_exp, 1)
                        elif kind == "pv":
                            wait(act, s_pv, pv.up())
                            wait(act, aolo)
                            act.activation(att[:], ps_o[:], ACT.Copy).then_inc(s_pvread, 1)
                            act.activation(rden[:], ps_d[:], ACT.Copy).then_inc(s_pvread, 1)
                        elif kind == "ao_parts":
                            g = arg[0]
                            wait(act, s_norm, norm.up(2))
                            act.activation(aop[t.par][:, 0, g], att[:], ACT.Identity,
                                           bias=b_v[:, g:g + 1]).then_inc(s_aohi, 1)
                            aolo.up()
                        elif kind == "out":
                            for st in arg[0]:
                                wait(act, s_full, full.up())
                                wait(act, clo)
                                if st == 0:
                                    wait(act, xn2out)
                                wait(act, x1out[st % 2])
                                if st >= 2:
                                    wait(act, s_xn2, xn2c.value(1))
                                act.activation(sum1[st % 2], proj[st % 2][:], ACT.Copy,
                                               scale=PROJ_DOWN).then_inc(s_evac, 1)
                                x1out[st % 2].up(16)
                                xn2c.up()
                        elif kind == "xn2":
                            for st in range(ST):
                                wait(act, s_full, full.up())
                                for c in x1out:
                                    wait(act, c)
                                act.activation(ct[:, st], proj[st % 2][:], ACT.Copy).then_inc(s_evac, 1)
                            xn2out.up(16)

                run(act, counts, turn)

            @block.vector
            def _(dve):
                x_in, rstdc, ln, xn = Count(s_x), Count(s_rstd), Count(s_ln), Count(s_xn)
                hi, evac, mul, summ, rotc = Count(s_hi), Count(s_evac), Count(s_mul), Count(s_sum), Count(s_rot)
                chi, lo, sfull, sread, mc, minn = (Count(s) for s in (s_chi, s_lo, s_sfull, s_sread, s_m, s_min))
                pvr, norm, aohi, resb = Count(s_pvread), Count(s_norm), Count(s_aohi), Count(s_resb)
                cosc, aolo = Count(s_cos), Count(s_aolo)
                x1c, ln2, rstd2c, xn2c, pk = Count(s_x1), Count(s_ln2), Count(s_rstd2), Count(s_xn2), Count(s_peak)
                counts = [x_in, rstdc, ln, xn, hi, evac, mul, summ, rotc, chi, lo, sfull, sread, mc, minn,
                          pvr, norm, aohi, resb, x1c, ln2, rstd2c, xn2c, pk, aolo, cosc]
                dve.memset(peak[:], 0.0).then_inc(s_dc, 1)
                for k in range(2):
                    dve.memset(ks[k][KROWS:P, :, :, :], M_DOWN)
                dve.wait_ge(s_w, 160)
                for t, up in ((b_q, QK_UP), (b_k, QK_UP), (b_v, X_UP)):
                    dve.tensor_scalar(t[:], t[:], up, None, ALU.mult).then_inc(s_dc, 1)

                def rotate(item):
                    wait(dve, s_evac, evac.up())
                    wait(dve, summ, past=s_past["dve"])
                    dve.stream_shuffle(rot[:, item % 2], tmp[:, item % 4],
                                       [(d + D // 2) % D for d in range(D)]).then_inc(s_rot, 1)
                    rotc.up()
                    wait(dve, s_rot, rotc.value())
                    dve.tensor_tensor(tmp[:, item % 4], tmp[:, item % 4], cos[:], ALU.mult).then_inc(s_cos, 1)

                def rope_sum(item):
                    wait(dve, s_cos, cosc.up())
                    wait(dve, s_mul, mul.up())
                    dve.tensor_tensor(tmp[:, item % 4], tmp[:, item % 4], rot[:, item % 2], ALU.add).then_inc(s_sum, 1)
                    summ.up()

                def low(item, dst):
                    wait(dve, s_hi, hi.up())
                    dve.tensor_tensor(dst[:, 1, item % 4], tmp[:, item % 4], dst[:, 0, item % 4],
                                      ALU.subtract).then_inc(s_lo, 1)
                    lo.up()

                def norm_x1(st):
                    wait(dve, s_rstd2, rstd2c.up(2))
                    dve.tensor_scalar(xt[:, st], sum1[st % 2], mv2[:, st, 0:1], rstd2[:, st:st + 1],
                                      ALU.subtract, ALU.mult).then_inc(s_xn2, 1)
                    xn2c.up()

                def top_x1(st):
                    wait(dve, s_xn2, xn2c.value())
                    wait(dve, s_peak, pk.value())
                    dve.tensor_reduce(peak_b[:, st:st + 1], xt[:, st], AXX, ALU.max,
                                      apply_absolute_value=True).then_inc(s_peak, 1)
                    pk.up()

                def turn(b, has_prev, has_next):
                    for kind, t, *arg in order(b, has_prev, has_next):
                        if kind == "norm_x":
                            wait(dve, s_x, x_in.up(16))
                            wait(dve, xn)
                            for st in range(ST):
                                dve.bn_stats(stats[:, st], xt[:, st]).then_inc(s_ln, 1)
                            for st in range(ST):
                                wait(dve, s_ln, ln.up(), past=s_past["dve"])
                                dve.bn_aggr(mv[:, st], stats[:, st]).then_inc(s_ln, 1)
                            ln.up(4)
                            wait(dve, s_rstd, rstdc.up(2))
                            for st in range(ST):
                                dve.tensor_scalar(xt[:, st], xt[:, st], mv[:, st, 0:1], rstd[:, st:st + 1],
                                                  ALU.subtract, ALU.mult).then_inc(s_xn, 1)
                            xn.up(4)
                        elif kind == "c_parts":
                            wait(dve, s_chi, chi.up())
                            dve.scalar_tensor_tensor(cp[:, 1], ct[:], X_UP, cp[:, 0], ALU.mult,
                                                     ALU.subtract).then_inc(s_clo, 1)
                        elif kind == "x":
                            for ec in range(C):
                                wait(dve, s_evac, evac.up())
                                low(ec, xp)
                        elif kind in "kq":
                            for eo in arg[0]:
                                rotate(eo)
                                if eo > 0:
                                    rope_sum(eo - 1)
                                if eo > 1:
                                    low(eo - 2, qkp)
                        elif kind in ("k_end", "q_end"):
                            rope_sum(3)
                            low(2, qkp)
                            low(3, qkp)
                        elif kind == "v":
                            evac.up(len(arg[0]))
                        elif kind == "xn2":
                            evac.up(4)
                        elif kind == "scores":
                            wait(dve, mc)
                            for pair in range(2):
                                for blocks in heads_blocks(pair, False):
                                    wait(dve, s_sfull, sfull.up())
                                    bank = sc[(sfull.n - 1) % 2]
                                    if blocks[0][1] == 1:
                                        last = dve.tensor_reduce(mx[:, 1, 2 * pair:2 * pair + 2],
                                                                 bank[:].rearrange("p (j t) -> p j t", j=2), AXX, ALU.max)
                                    else:
                                        for j, sbt, col in blocks:
                                            last = dve.tensor_reduce(mx[:, sbt, j:j + 1],
                                                                     bank[:, col:col + (sbt + 1) * P], AXX, ALU.max)
                                    last.then_inc(s_sread, 1)
                                    sread.up()
                            wait(dve, sread)
                            dve.tensor_scalar(mp[:, :, 0], mx[:], -1.0 / M_DOWN, None, ALU.mult).then_inc(s_m, 1)
                            wait(dve, s_m, mc.up())
                            dve.scalar_tensor_tensor(mp[:, :, 1], mx[:], -1.0 / M_DOWN, mp[:, :, 0],
                                                     ALU.mult, ALU.subtract).then_inc(s_m, 1)
                            mc.up()
                        elif kind == "rows":
                            wait(dve, s_sfull, sfull.up())
                            wait(dve, minn)
                            bank = sc[(sfull.n - 1) % 2]
                            dve.tensor_copy(mrow[:], bank[0:2 * HG, 0:S // 2].bitcast(F16)).then_inc(s_sread, 1)
                            sread.up()
                            minn.up(32)
                        elif kind == "ao_norm":
                            wait(dve, s_pvread, pvr.up(2))
                            dve.reciprocal(rden[:], rden[:]).then_inc(s_norm, 1)
                            wait(dve, s_norm, norm.up())
                            dve.tensor_tensor(att[:], att[:], rden[:], ALU.mult).then_inc(s_norm, 1)
                            norm.up()
                        elif kind == "ao_parts":
                            g = arg[0]
                            wait(dve, s_aohi, aohi.up())
                            dve.scalar_tensor_tensor(aop[t.par][:, 1, g], att[:], b_v[:, g:g + 1], aop[t.par][:, 0, g],
                                                     ALU.add, ALU.subtract).then_inc(s_aolo, 1)
                            aolo.up()
                        elif kind == "out":
                            for st in arg[0]:
                                wait(dve, s_evac, evac.up())
                                wait(dve, s_resb, resb.up())
                                dve.tensor_tensor(sum1[st % 2], sum1[st % 2], resid, ALU.add).then_inc(s_x1, 1)
                                wait(dve, s_x1, x1c.up())
                                wait(dve, xn2c)
                                dve.bn_stats(stats2[:, st], sum1[st % 2]).then_inc(s_ln2, 1)
                                wait(dve, s_ln2, ln2.up(), past=s_past["dve"])
                                dve.bn_aggr(mv2[:, st], stats2[:, st]).then_inc(s_ln2, 1)
                                ln2.up()
                                if st > 0:
                                    top_x1(st - 1)
                                norm_x1(st)
                        elif kind == "out_end":
                            top_x1(3)
                            wait(dve, pk)
                            dve.tensor_tensor(peak[:], peak[:], peak_b[:], ALU.max).then_inc(s_peak, 1)
                            pk.up()

                run(dve, counts, turn)
                wait(dve, pk)

            @block.tensor
            def _(pe):
                evac, xn, lo, clo, kst, qst = (Count(s) for s in (s_evac, s_xn, s_lo, s_clo, s_kst, s_qst))
                sread, mc, minn, exp, pvr, aolo, xn2c = (Count(s) for s in (s_sread, s_m, s_min, s_exp, s_pvread, s_aolo, s_xn2))
                counts = [evac, xn, lo, clo, kst, qst, sread, mc, minn, exp, pvr, aolo, xn2c]
                pe.wait_ge(s_const, 12)
                pe.wait_ge(s_w, 160)
                pe.wait_ge(s_dc, 4)

                def next_bank():
                    evac.up()
                    wait(pe, s_evac, evac.value(2))
                    return proj[(evac.n - 1) % 2]

                def product(bank, left, right):
                    n = 0
                    for c in range(C):
                        for a, z in ((0, 0), (0, 1), (1, 0)):
                            last = pe.matmul(bank[:], left(a, c), right(z, c), start=n == 0, stop=n == 3 * C - 1)
                            n += 1
                    last.then_inc(s_full, 1)

                def turn(b, has_prev, has_next):
                    for kind, t, *arg in order(b, has_prev, has_next):
                        if kind == "x":
                            wait(pe, s_xn, xn.up(4))
                            for ec in range(C):
                                bank = next_bank()
                                for st in range(ST):
                                    last = pe.transpose(bank[:, st * P:(st + 1) * P], xt[:, st, ec * P:(ec + 1) * P], ident[:])
                                last.then_inc(s_full, 1)
                            lo.up(4)
                        elif kind == "k":
                            if arg[0][0] == 0:
                                wait(pe, s_clo, clo.up())
                            for eo in arg[0]:
                                cols = slice(eo * P, (eo + 1) * P)
                                product(next_bank(), lambda a, c: W["k"][:, a, c, cols], lambda z, c: cp[:, z, c])
                            lo.up(len(arg[0]))
                        elif kind == "q":
                            if arg[0][0] == 0:
                                wait(pe, s_lo, lo.value(4))
                            for eo in arg[0]:
                                cols = slice(eo * P, (eo + 1) * P)
                                product(next_bank(), lambda a, c: W["q"][:, a, c, cols], lambda z, c: xp[:, z, c])
                            lo.up(len(arg[0]))
                        elif kind == "v":
                            for tb in arg[0]:
                                cols = slice(tb * P, (tb + 1) * P)
                                product(next_bank(), lambda a, c: cp[:, a, c, cols], lambda z, c: W["v"][:, z, c])
                        elif kind == "scores":
                            g = arg[0]
                            if g == 0:
                                wait(pe, s_kst, kst.up(192))
                                wait(pe, s_qst, qst.up(192))
                            for pair in range(2):
                                for blocks in heads_blocks(pair, False):
                                    sread.up()
                                    wait(pe, s_sread, sread.value(2))
                                    bank = sc[(sread.n - 1) % 2]
                                    for j, sbt, col in blocks:
                                        w = (sbt + 1) * P
                                        pe.matmul(bank[:, col:col + w], qs[t.par][0:KROWS, g, j, sbt * P:w],
                                                  ks[t.par][0:KROWS, g, j, 0:w], start=True, stop=False)
                                        last = pe.matmul(bank[:, col + w - P:col + w], identb[:], mask_s[:],
                                                         start=False, stop=True)
                                    last.then_inc(s_sfull, 1)
                        elif kind == "rows":
                            wait(pe, s_m, mc.up(2))
                            sread.up()
                            wait(pe, s_sread, sread.value(2))
                            bank = sc[(sread.n - 1) % 2]
                            for st in range(ST):
                                last = pe.transpose(bank[0:2 * HG, st * P // 2:(st + 1) * P // 2].bitcast(F16),
                                                    mp[:, st].rearrange("p a j -> p (a j)"), ident16[:])
                            last.then_inc(s_sfull, 1)
                        elif kind == "exp":
                            g = arg[0]
                            wait(pe, s_min, minn.up(32))
                            for pair in range(2):
                                for blocks in heads_blocks(pair, True):
                                    exp.up()
                                    wait(pe, s_exp, exp.value(2))
                                    bank = sct[(exp.n - 1) % 2]
                                    for j, tb, col in blocks:
                                        w = S - tb * P
                                        pe.matmul(bank[:, col:col + w], ks[t.par][0:MROWS, g, j, tb * P:(tb + 1) * P],
                                                  qs[t.par][0:MROWS, g, j, tb * P:S], start=True, stop=False)
                                        last = pe.matmul(bank[:, col:col + P], identb[:], mask_t[:],
                                                         start=False, stop=True)
                                    last.then_inc(s_tfull, 1)
                        elif kind == "pv":
                            g = arg[0]
                            wait(pe, exp)
                            wait(pe, pvr)
                            where = {}
                            for pair in range(2):
                                for u, blocks in enumerate(heads_blocks(pair, True)):
                                    for j, tb, col in blocks:
                                        where[j, tb] = (pair * 5 + u, col)
                            for tb in range(ST):
                                w = S - tb * P
                                for dst in (ps_o, ps_d):
                                    for j in range(HG):
                                        u, col = where[j, tb]
                                        head = (HG * g + j) * D
                                        left = v[:, tb, head:head + D] if dst is ps_o else ones[:]
                                        last = pe.matmul(dst[j * D:(j + 1) * D, tb * P:S], left, pt[:, u, col:col + w],
                                                         start=tb == 0, stop=tb == ST - 1)
                            last.then_inc(s_pv, 1)
                            pvr.up(2)
                        elif kind == "ao_parts":
                            aolo.up()
                        elif kind == "out":
                            if arg[0][0] == 0:
                                wait(pe, aolo)
                            for st in arg[0]:
                                cols = slice(st * P, (st + 1) * P)
                                product(next_bank(), lambda a, c: aop[t.par][:, a, c, cols], lambda z, c: W["o"][:, z, c])
                        elif kind == "xn2":
                            wait(pe, s_xn2, xn2c.up(4))
                            for st in range(ST):
                                bank = next_bank()
                                for ec in range(C):
                                    last = pe.transpose(bank[:, ec * P:(ec + 1) * P], xt[:, st, ec * P:(ec + 1) * P], ident[:])
                                last.then_inc(s_full, 1)

                run(pe, counts, turn)


T = B
PIECES = 3
CH = IC // PIECES
CW = PIECES * S
RING = 4
RMAX = bass.bass_isa.ReduceOp.max
(X_MAX, X_S, X_INV, X_UNIT, G_MAX, G_S, G_INV, U_MAX, U_S, U_INV, F_MAX, F_UNIT, F_S, F_INV,
 O_MAX, O_UNIT, O_S, O_MUL, TOP, TMP, N_SCALARS) = range(21)


def tiles_in_pairs(eng, counts, growth, turn):
    turn(0, False)
    with eng.Fori(0, T // 2 - 2) as i:
        for c in counts:
            c.enter(i, growth[c.sem])
        turn(i * 2 + 2, False)
    for c in counts:
        c.leave(T // 2 - 2)
    turn(T - 2, True)


def three_pass_product(pe, bank, chunks, left, right):
    n = 0
    for c in range(chunks):
        for a, z in ((0, 0), (0, 1), (1, 0)):
            last = pe.matmul(bank, left(a, c), right(z, c), start=n == 0, stop=n == 3 * chunks - 1)
            n += 1
    return last


class Scalars:

    def __init__(self, dve, table, sem):
        self.dve, self.table, self.sem, self.n = dve, table, sem, 0

    def col(self, k):
        return self.table[:, k:k + 1]

    def after(self, ins):
        ins.then_inc(self.sem, 1)
        self.n += 1
        self.dve.wait_ge(self.sem, self.n)

    def quantisation(self, top, unit, scale, inverse):
        dve, col = self.dve, self.col
        if unit is None:
            self.after(dve.tensor_scalar(col(scale), col(top), 1.0 / QMAX_A, TINY, ALU.mult, ALU.max))
            self.after(dve.reciprocal(col(inverse), col(scale)))
            return
        self.after(dve.tensor_scalar(col(TMP), col(top), col(unit), 1.0 / QMAX_A, ALU.mult, ALU.mult))
        self.after(dve.tensor_scalar(col(scale), col(TMP), TINY, None, ALU.max))
        self.after(dve.reciprocal(col(TMP), col(scale)))
        self.after(dve.tensor_tensor(col(inverse), col(TMP), col(unit), ALU.mult))


def gate_stage(nc, wf_parts, xn2T, x_int, g_raw, table, peak_x, peak_g):
    with ExitStack() as ctx:
        def sb(n, s, d):
            return ctx.enter_context(nc.sbuf_tensor("g_" + n, s, d))

        def sem(n):
            return ctx.enter_context(nc.semaphore("g_" + n))

        w = sb("w", [P, IC, 2, C, P], F16)
        xn = [sb(f"xn{k}", [P, ST, C * P], F32) for k in range(2)]
        xi = [sb(f"xi{k}", [P, C, S], I16) for k in range(2)]
        xp = [sb(f"xp{k}", [P, 2, C, S], F16) for k in range(2)]
        stage = [sb(f"stage{k}", [P, PIECES, S], F32) for k in range(2)]
        top = sb("top", [P, 2 * CH], F32)
        bank = [ctx.enter_context(nc.psum_tensor(f"g_bank{k}", [P, S], F32)) for k in range(RING)]
        s_w, s_ready, s_max, s_sc = sem("w"), sem("ready"), sem("max"), sem("scalars")
        s_x = [sem(f"x{k}") for k in range(2)]
        s_xst = [sem(f"xst{k}") for k in range(2)]
        s_int, s_hi, s_lo = sem("int"), sem("hi"), sem("lo")
        s_full, s_evac, s_top, s_peak = sem("full"), sem("evac"), sem("top"), sem("peak")
        s_st = [sem(f"st{k}") for k in range(2)]
        growth = {s_int: 2, s_hi: 2, s_lo: 2, s_full: 2 * IC, s_evac: 2 * IC, s_top: 2 * CH, s_peak: 1,
                  **{s: 16 for s in s_x + s_xst}, **{s: 16 * CH for s in s_st}}
        s_past = {e: sem(f"past_{e}") for e in ("sp", "pool", "dve", "act")}

        with nc.Block() as block:
            @block.sync
            def _(sp):
                def sp_wait(*what):
                    wait(sp, *what, past=s_past["sp"])

                ints, lo, evac, full = Count(s_int), Count(s_lo), Count(s_evac), Count(s_full)

                def load(k, t):
                    sp_wait(s_int, ints.value(1))
                    ints.up()
                    sp.dma_start(xn[k][:], xn2T[t]).then_inc(s_x[k], 16)

                load(0, 0)
                load(1, 1)
                for ic in range(0, IC, PIECES):
                    sp.dma_start(w[:, ic:ic + PIECES].rearrange("p k a c n -> p k (a c n)"),
                                 wf_parts[ic:ic + PIECES].rearrange("k p a n -> p k (a n)")).then_inc(s_w, 16)

                def turn(t, last):
                    for k in range(2):
                        sp_wait(s_lo, lo.up())
                        sp.dma_start(x_int[t + k], xp[k][:]).then_inc(s_xst[k], 16)
                        for c in range(CH):
                            sp_wait(s_evac, evac.up(PIECES))
                            sp.dma_start(g_raw[t + k, c], stage[c % 2][:].rearrange("p a n -> p (a n)")
                                         ).then_inc(s_st[c % 2], 16)
                            if c == 0 and not last:
                                load(k, t + k + 2)

                tiles_in_pairs(sp, [ints, lo, evac], growth, turn)
                for k in range(2):
                    sp.wait_ge(s_st[k], 16 * CH * T // 2)
                    sp.wait_ge(s_xst[k], 16 * T // 2)

            @block.gpsimd
            def _(pool):
                pool.wait_ge(s_ready, 1)
                pool.partition_all_reduce(table[:, X_MAX:X_MAX + 1], table[:, TOP:TOP + 1], P, RMAX).then_inc(s_max, 1)

            @block.scalar
            def _(act):
                ints, full, xst, st, tops = (Count(s_int), Count(s_full), [Count(s) for s in s_xst],
                                             [Count(s) for s in s_st], Count(s_top))

                def turn(t, last):
                    for k in range(2):
                        wait(act, s_int, ints.up())
                        wait(act, s_full, full.value(IC))
                        wait(act, xst[k])
                        xst[k].up(16)
                        act.activation(xp[k][:, 0], xi[k][:], ACT.Copy).then_inc(s_hi, 1)
                        for c in range(CH):
                            wait(act, st[c % 2])
                            wait(act, s_top, tops.value(1))
                            st[c % 2].up(16)
                            tops.up()
                            for j in range(PIECES):
                                wait(act, s_full, full.up())
                                act.activation(stage[c % 2][:, j], bank[(c * PIECES + j) % RING][:],
                                               ACT.Copy).then_inc(s_evac, 1)

                tiles_in_pairs(act, [ints, full, *xst, *st, tops], growth, turn)

            @block.vector
            def _(dve):
                sc = Scalars(dve, table, s_sc)
                x, hi, ints, evac, tops, peak, lo = ([Count(s) for s in s_x], Count(s_hi), Count(s_int), Count(s_evac),
                                                     Count(s_top), Count(s_peak), Count(s_lo))
                sc.after(dve.memset(peak_g[:], 0.0))
                dve.tensor_reduce(sc.col(TOP), peak_x[:], AXX, ALU.max).then_inc(s_ready, 1)
                dve.wait_ge(s_max, 1)
                sc.quantisation(X_MAX, None, X_S, X_INV)
                sc.after(dve.tensor_scalar(sc.col(X_UNIT), sc.col(X_S), 1.0 / W_UP, None, ALU.mult))

                def turn(t, last):
                    wait(dve, peak)
                    for k in range(2):
                        wait(dve, s_x[k], x[k].up(16))
                        wait(dve, s_lo, lo.value(1))
                        dve.tensor_scalar(xi[k][:].rearrange("p c (s n) -> p c s n", s=ST),
                                          xn[k][:].rearrange("p s (c n) -> p c s n", c=C),
                                          sc.col(X_INV), None, ALU.mult).then_inc(s_int, 1)
                        wait(dve, s_hi, hi.up())
                        dve.tensor_tensor(xp[k][:, 1], xi[k][:], xp[k][:, 0], ALU.subtract).then_inc(s_lo, 1)
                        lo.up()
                        for c in range(CH):
                            wait(dve, s_evac, evac.up(PIECES))
                            n = k * CH + c
                            dve.tensor_reduce(top[:, n:n + 1], stage[c % 2][:].rearrange("p a n -> p (a n)"), AXX,
                                              ALU.max, apply_absolute_value=True).then_inc(s_top, 1)
                            tops.up()
                    wait(dve, tops)
                    dve.tensor_tensor(peak_g[:], peak_g[:], top[:], ALU.max).then_inc(s_peak, 1)
                    peak.up()

                tiles_in_pairs(dve, [*x, hi, evac, tops, peak, lo], growth, turn)
                wait(dve, peak)

            @block.tensor
            def _(pe):
                lo, evac = Count(s_lo), Count(s_evac)

                def turn(t, last):
                    for k in range(2):
                        wait(pe, s_lo, lo.up())
                        for ic in range(IC):
                            if isinstance(t, int) and k == 0 and ic % PIECES == 0:
                                pe.wait_ge(s_w, 16 * CH)
                            evac.up()
                            wait(pe, s_evac, evac.value(RING))
                            three_pass_product(pe, bank[ic % RING][:], C, lambda a, c: w[:, ic, a, c],
                                               lambda z, c: xp[k][:, z, c]).then_inc(s_full, 1)

                tiles_in_pairs(pe, [lo, evac], growth, turn)


def up_stage(nc, wf_parts, x_int, g_raw, u_raw, table, peak_g, peak_u, peak_f, gq):
    with ExitStack() as ctx:
        def sb(n, s, d):
            return ctx.enter_context(nc.sbuf_tensor("u_" + n, s, d))

        def sem(n):
            return ctx.enter_context(nc.semaphore("u_" + n))

        w = sb("w", [P, IC, 2, C, P], F16)
        xp = [sb(f"xp{k}", [P, 2, C, S], F16) for k in range(2)]
        stage = [sb(f"stage{k}", [P, PIECES, S], F32) for k in range(2)]
        raw = [sb(f"raw{k}", [P, CW], F32) for k in range(2)]
        sig = [sb(f"sig{k}", [P, CW], F32) for k in range(2)]
        sigq = sb("sigq", [P, CW], U16)
        top = sb("top", [P, 2, 2 * CH], F32)
        bank = [ctx.enter_context(nc.psum_tensor(f"u_bank{k}", [P, S], F32)) for k in range(RING)]
        s_w, s_ready, s_max, s_sc, s_set = sem("w"), sem("ready"), sem("max"), sem("scalars"), sem("set")
        s_x = [sem(f"x{k}") for k in range(2)]
        s_g = [sem(f"g{k}") for k in range(2)]
        s_st = [sem(f"st{k}") for k in range(2)]
        s_full, s_evac, s_top, s_peak = sem("full"), sem("evac"), sem("top"), sem("peak")
        s_gq, s_sig, s_sigq, s_f, s_ftop = sem("gq"), sem("sig"), sem("sigq"), sem("f"), sem("ftop")
        growth = {s_full: 2 * IC, s_evac: 2 * IC, s_top: 2 * CH, s_peak: 2, s_gq: 2 * CH, s_sig: 2 * CH,
                  s_sigq: 2 * CH, s_f: 2 * CH, s_ftop: 2 * CH,
                  **{s: 16 for s in s_x}, **{s: 16 * CH for s in s_st + s_g}}
        s_past = {e: sem(f"past_{e}") for e in ("sp", "pool", "dve", "act")}

        with nc.Block() as block:
            @block.sync
            def _(sp):
                def sp_wait(*what):
                    wait(sp, *what, past=s_past["sp"])

                for ic in range(0, IC, PIECES):
                    sp.dma_start(w[:, ic:ic + PIECES].rearrange("p k a c n -> p k (a c n)"),
                                 wf_parts[IC + ic:IC + ic + PIECES].rearrange("k p a n -> p k (a n)")).then_inc(s_w, 16)
                full, evac, gqc = Count(s_full), Count(s_evac), Count(s_gq)

                def turn(t, last):
                    for k in range(2):
                        sp_wait(s_full, full.value(IC))
                        full.up(IC)
                        sp.dma_start(xp[k][:], x_int[t + k]).then_inc(s_x[k], 16)
                        for c in range(CH):
                            sp_wait(s_gq, gqc.value(1))
                            gqc.up()
                            sp.dma_start(raw[c % 2][:], g_raw[t + k, c]).then_inc(s_g[c % 2], 16)
                            sp_wait(s_evac, evac.up(PIECES))
                            sp.dma_start(u_raw[t + k, c], stage[c % 2][:].rearrange("p a n -> p (a n)")
                                         ).then_inc(s_st[c % 2], 16)

                tiles_in_pairs(sp, [full, evac, gqc], growth, turn)
                for k in range(2):
                    sp.wait_ge(s_st[k], 16 * CH * T // 2)

            @block.gpsimd
            def _(pool):
                pool.wait_ge(s_ready, 1)
                pool.partition_all_reduce(table[:, G_MAX:G_MAX + 1], table[:, TOP:TOP + 1], P, RMAX).then_inc(s_max, 1)

            @block.scalar
            def _(act):
                full, tops, ftop, gqc = Count(s_full), Count(s_top), Count(s_ftop), Count(s_gq)
                st, g = [Count(s) for s in s_st], [Count(s) for s in s_g]
                act.wait_ge(s_set, 1)

                def turn(t, last):
                    for k in range(2):
                        for c in range(CH):
                            wait(act, st[c % 2])
                            wait(act, s_top, tops.value(1))
                            st[c % 2].up(16)
                            tops.up()
                            wait(act, s_g[c % 2], g[c % 2].up(16), past=s_past["act"])
                            ints = gq[:, t + k, c]
                            act.activation(ints, raw[c % 2][:], ACT.Copy,
                                           scale=table[:, G_INV:G_INV + 1]).then_inc(s_gq, 1)
                            for j in range(PIECES):
                                wait(act, s_full, full.up())
                                act.activation(stage[c % 2][:, j], bank[(c * PIECES + j) % RING][:],
                                               ACT.Copy).then_inc(s_evac, 1)
                            wait(act, s_gq, gqc.up())
                            wait(act, s_ftop, ftop.value(1), past=s_past["act"])
                            ftop.up()
                            act.activation(sig[c % 2][:], ints, ACT.Sigmoid,
                                           scale=table[:, G_S:G_S + 1]).then_inc(s_sig, 1)

                tiles_in_pairs(act, [full, tops, ftop, gqc, *st, *g], growth, turn)

            @block.vector
            def _(dve):
                sc = Scalars(dve, table, s_sc)
                evac, tops, peak, sigc, sigqc, f, ftop = (
                    Count(s) for s in (s_evac, s_top, s_peak, s_sig, s_sigq, s_f, s_ftop))
                sc.after(dve.memset(peak_u[:], 0.0))
                sc.after(dve.memset(peak_f[:], 0.0))
                dve.tensor_reduce(sc.col(TOP), peak_g[:], AXX, ALU.max).then_inc(s_ready, 1)
                dve.wait_ge(s_max, 1)
                sc.quantisation(G_MAX, X_UNIT, G_S, G_INV)
                dve.tensor_scalar(sc.col(F_UNIT), sc.col(G_S), 1.0 / 65536.0, None, ALU.mult).then_inc(s_set, 1)

                def turn(t, last):
                    wait(dve, peak)
                    for k in range(2):
                        for c in range(CH):
                            n = k * CH + c
                            wait(dve, s_evac, evac.up(PIECES))
                            dve.tensor_reduce(top[:, 0, n:n + 1], stage[c % 2][:].rearrange("p a n -> p (a n)"), AXX,
                                              ALU.max, apply_absolute_value=True).then_inc(s_top, 1)
                            tops.up()
                            wait(dve, s_sig, sigc.up())
                            wait(dve, f)
                            dve.tensor_scalar(sigq[:], sig[c % 2][:], 65536.0, None, ALU.mult).then_inc(s_sigq, 1)
                            wait(dve, s_sigq, sigqc.up())
                            dve.tensor_tensor(sig[c % 2][:], gq[:, t + k, c], sigq[:], ALU.mult).then_inc(s_f, 1)
                            wait(dve, s_f, f.up())
                            dve.tensor_reduce(top[:, 1, n:n + 1], sig[c % 2][:], AXX, ALU.max,
                                              apply_absolute_value=True).then_inc(s_ftop, 1)
                            ftop.up()
                    wait(dve, ftop)
                    dve.tensor_tensor(peak_u[:], peak_u[:], top[:, 0], ALU.max).then_inc(s_peak, 1)
                    dve.tensor_tensor(peak_f[:], peak_f[:], top[:, 1], ALU.max).then_inc(s_peak, 1)
                    peak.up(2)

                tiles_in_pairs(dve, [evac, tops, peak, sigc, sigqc, f, ftop], growth, turn)
                wait(dve, peak)

            @block.tensor
            def _(pe):
                x, evac = [Count(s) for s in s_x], Count(s_evac)
                pe.wait_ge(s_w, 16 * CH)

                def turn(t, last):
                    for k in range(2):
                        wait(pe, s_x[k], x[k].up(16))
                        for ic in range(IC):
                            evac.up()
                            wait(pe, s_evac, evac.value(RING))
                            three_pass_product(pe, bank[ic % RING][:], C, lambda a, c: w[:, ic, a, c],
                                               lambda z, c: xp[k][:, z, c]).then_inc(s_full, 1)

                tiles_in_pairs(pe, [*x, evac], growth, turn)


def peak_stage(nc, u_raw, table, peak_u, peak_f, peak_o, gq):
    with ExitStack() as ctx:
        def sb(n, s, d):
            return ctx.enter_context(nc.sbuf_tensor("p_" + n, s, d))

        def sem(n):
            return ctx.enter_context(nc.semaphore("p_" + n))

        sig = [sb(f"sig{k}", [P, CW], F32) for k in range(2)]
        sigq = [sb(f"sigq{k}", [P, CW], U16) for k in range(2)]
        raw = [sb(f"raw{k}", [P, CW], F32) for k in range(2)]
        uq = [sb(f"uq{k}", [P, CW], I16) for k in range(2)]
        prod = [sb(f"prod{k}", [P, CW], F32) for k in range(2)]
        top = sb("top", [P, 2 * CH], F32)
        s_ready, s_max, s_sc, s_set = sem("ready"), sem("max"), sem("scalars"), sem("set")
        s_u = [sem(f"u{k}") for k in range(2)]
        s_sig, s_sigq, s_f, s_fq, s_uq, s_o, s_top, s_peak = (
            sem(n) for n in ("sig", "sigq", "f", "fq", "uq", "o", "top", "peak"))
        growth = {**{s: 2 * CH for s in (s_sig, s_sigq, s_f, s_fq, s_uq, s_o, s_top)}, s_peak: 1,
                  **{s: 16 * CH for s in s_u}}
        s_past = {e: sem(f"past_{e}") for e in ("sp", "pool", "dve", "act")}

        with nc.Block() as block:
            @block.sync
            def _(sp):
                def sp_wait(*what):
                    wait(sp, *what, past=s_past["sp"])

                uqc = Count(s_uq)

                def turn(t, last):
                    for k in range(2):
                        for c in range(CH):
                            sp_wait(s_uq, uqc.value(1))
                            uqc.up()
                            sp.dma_start(raw[c % 2][:], u_raw[t + k, c]).then_inc(s_u[c % 2], 16)

                tiles_in_pairs(sp, [uqc], growth, turn)

            @block.gpsimd
            def _(pool):
                pool.wait_ge(s_ready, 1)
                pool.partition_all_reduce(table[:, U_MAX:U_MAX + 1], table[:, TOP:TOP + 1], P, RMAX).then_inc(s_max, 1)
                pool.wait_ge(s_ready, 2)
                pool.partition_all_reduce(table[:, F_MAX:F_MAX + 1], table[:, TOP:TOP + 1], P, RMAX).then_inc(s_max, 1)

            @block.scalar
            def _(act):
                f, fq, o, u, sigqc, sig_c = Count(s_f), Count(s_fq), Count(s_o), [Count(s) for s in s_u], Count(s_sigq), Count(s_sig)
                act.wait_ge(s_set, 1)

                def turn(t, last):
                    for k in range(2):
                        for c in range(CH):
                            here = gq[:, t + k, c]
                            wait(act, s_fq, fq.value(1), past=s_past["act"])
                            act.activation(sig[c % 2][:], here, ACT.Sigmoid,
                                           scale=table[:, G_S:G_S + 1]).then_inc(s_sig, 1)
                            wait(act, s_u[c % 2], u[c % 2].up(16))
                            wait(act, s_o, o.value(1))
                            o.up()
                            act.activation(uq[c % 2][:], raw[c % 2][:], ACT.Copy,
                                           scale=table[:, U_INV:U_INV + 1]).then_inc(s_uq, 1)
                            wait(act, s_f, f.up(), past=s_past["act"])
                            act.activation(here, sig[c % 2][:], ACT.Copy,
                                           scale=table[:, F_INV:F_INV + 1]).then_inc(s_fq, 1)
                            fq.up()

                tiles_in_pairs(act, [f, fq, o, *u], growth, turn)

            @block.vector
            def _(dve):
                sc = Scalars(dve, table, s_sc)
                sc.after(dve.memset(peak_o[:], 0.0))
                dve.tensor_reduce(sc.col(TOP), peak_u[:], AXX, ALU.max).then_inc(s_ready, 1)
                dve.wait_ge(s_max, 1)
                sc.quantisation(U_MAX, X_UNIT, U_S, U_INV)
                dve.tensor_reduce(sc.col(TOP), peak_f[:], AXX, ALU.max).then_inc(s_ready, 1)
                dve.wait_ge(s_max, 2)
                sc.quantisation(F_MAX, F_UNIT, F_S, F_INV)
                dve.tensor_tensor(sc.col(O_UNIT), sc.col(F_S), sc.col(U_S), ALU.mult).then_inc(s_set, 1)
                sigc, f, fq, uqc, o, tops, peak, sigqc = (
                    Count(s) for s in (s_sig, s_f, s_fq, s_uq, s_o, s_top, s_peak, s_sigq))

                def turn(t, last):
                    wait(dve, peak)
                    for k in range(2):
                        for c in range(CH):
                            n = k * CH + c
                            wait(dve, s_sig, sigc.up())
                            wait(dve, s_f, f.value(1))
                            dve.tensor_scalar(sigq[c % 2][:], sig[c % 2][:], 65536.0, None, ALU.mult).then_inc(s_sigq, 1)
                            wait(dve, s_sigq, sigqc.up())
                            dve.tensor_tensor(sig[c % 2][:], gq[:, t + k, c], sigq[c % 2][:], ALU.mult).then_inc(s_f, 1)
                            f.up()
                            wait(dve, s_fq, fq.up())
                            wait(dve, s_uq, uqc.up())
                            wait(dve, s_top, tops.value(1))
                            dve.tensor_tensor(prod[c % 2][:], gq[:, t + k, c], uq[c % 2][:], ALU.mult).then_inc(s_o, 1)
                            wait(dve, s_o, o.up())
                            dve.tensor_reduce(top[:, n:n + 1], prod[c % 2][:], AXX, ALU.max,
                                              apply_absolute_value=True).then_inc(s_top, 1)
                            tops.up()
                    wait(dve, tops)
                    dve.tensor_tensor(peak_o[:], peak_o[:], top[:], ALU.max).then_inc(s_peak, 1)
                    peak.up()

                tiles_in_pairs(dve, [sigc, f, fq, uqc, o, tops, peak, sigqc], growth, turn)
                wait(dve, peak)


def down_stage(nc, wf_parts, u_raw, x1, out, table, peak_o, gq):
    with ExitStack() as ctx:
        def sb(n, s, d):
            return ctx.enter_context(nc.sbuf_tensor("d_" + n, s, d))

        def sem(n):
            return ctx.enter_context(nc.semaphore("d_" + n))

        w = sb("w", [P, IC, 2, C, P], F16)
        raw = [sb(f"raw{k}", [P, CW], F32) for k in range(2)]
        uq = sb("uq", [P, CW], I16)
        oi = [sb(f"oi{k}", [P, CW], I16) for k in range(2)]
        op = sb("op", [P, CH, 2, PIECES, S], F16)
        res = [sb(f"res{k}", [P, E], F32) for k in range(2)]
        bank = [ctx.enter_context(nc.psum_tensor(f"d_bank{k}", [P, E], F32)) for k in range(8)]
        s_w, s_ready, s_max, s_sc, s_set = sem("w"), sem("ready"), sem("max"), sem("scalars"), sem("set")
        s_u = [sem(f"u{k}") for k in range(2)]
        s_r = [sem(f"r{k}") for k in range(2)]
        s_out = [sem(f"out{k}") for k in range(2)]
        s_uq, s_oi, s_hi, s_lo, s_pass, s_full, s_y = (sem(n) for n in ("uq", "oi", "hi", "lo", "pass", "full", "y"))
        growth = {**{s: 2 * CH for s in (s_uq, s_oi, s_hi, s_lo)}, s_pass: 2 * (CH - 1), s_full: 2 * ST, s_y: 2 * ST,
                  **{s: 16 * CH for s in s_u}, **{s: 16 * ST for s in s_r + s_out}}
        s_past = {e: sem(f"past_{e}") for e in ("sp", "pool", "dve", "act")}

        with nc.Block() as block:
            @block.sync
            def _(sp):
                def sp_wait(*what):
                    wait(sp, *what, past=s_past["sp"])

                uqc, y = Count(s_uq), Count(s_y)
                out_c = [Count(s) for s in s_out]

                def chunks(t):
                    for c in range(CH):
                        sp_wait(s_uq, uqc.value(1))
                        uqc.up()
                        sp.dma_start(raw[c % 2][:], u_raw[t, c]).then_inc(s_u[c % 2], 16)
                        if c == 0 and isinstance(t, int) and t == 0:
                            for ic in range(0, IC, PIECES):
                                sp.dma_start(w[:, ic:ic + PIECES].rearrange("p k a c n -> p k (a c n)"),
                                             wf_parts[2 * IC + ic:2 * IC + ic + PIECES].rearrange("k p a n -> p k (a n)")
                                             ).then_inc(s_w, 16)

                def rows(t):
                    for st in range(ST):
                        sp_wait(out_c[st % 2])
                        out_c[st % 2].up(16)
                        sp.dma_start(res[st % 2][:], x1[t, st * P:(st + 1) * P, :]).then_inc(s_r[st % 2], 16)
                        sp_wait(s_y, y.up())
                        sp.dma_start(out[t, st * P:(st + 1) * P, :], res[st % 2][:]).then_inc(s_out[st % 2], 16)

                def turn(t, last):
                    for k in range(2):
                        if not (last and k):
                            chunks(t + k + 1)
                        rows(t + k)

                chunks(0)
                tiles_in_pairs(sp, [uqc, y, *out_c], growth, turn)
                for c in out_c:
                    sp_wait(c)

            @block.gpsimd
            def _(pool):
                pool.wait_ge(s_ready, 1)
                pool.partition_all_reduce(table[:, O_MAX:O_MAX + 1], table[:, TOP:TOP + 1], P, RMAX).then_inc(s_max, 1)

            @block.scalar
            def _(act):
                u, oi_c, passed, full = [Count(s) for s in s_u], Count(s_oi), Count(s_pass), Count(s_full)

                def turn(t, last):
                    for k in range(2):
                        for c in range(CH):
                            wait(act, s_u[c % 2], u[c % 2].up(16))
                            wait(act, oi_c)
                            act.activation(uq[:], raw[c % 2][:], ACT.Copy,
                                           scale=table[:, U_INV:U_INV + 1]).then_inc(s_uq, 1)
                            wait(act, s_oi, oi_c.up())
                            if c < CH - 1:
                                wait(act, s_pass, passed.value(CH - 2))
                                passed.up()
                            else:
                                wait(act, full)
                                full.up(ST)
                            act.activation(op[:, c, 0].rearrange("p a n -> p (a n)"), oi[c % 2][:],
                                           ACT.Copy).then_inc(s_hi, 1)

                tiles_in_pairs(act, [*u, oi_c, passed, full], growth, turn)

            @block.vector
            def _(dve):
                sc = Scalars(dve, table, s_sc)
                dve.tensor_reduce(sc.col(TOP), peak_o[:], AXX, ALU.max).then_inc(s_ready, 1)
                dve.wait_ge(s_max, 1)
                sc.quantisation(O_MAX, O_UNIT, O_S, O_MUL)
                sc.after(dve.tensor_scalar(sc.col(O_S), sc.col(O_S), 1.0 / W_UP, None, ALU.mult))
                uqc, hi, lo, full, r, y = (Count(s_uq), Count(s_hi), Count(s_lo), Count(s_full),
                                           [Count(s) for s in s_r], Count(s_y))

                def chunks(t):
                    for c in range(CH):
                        wait(dve, s_uq, uqc.up())
                        wait(dve, s_lo, lo.value(1))
                        dve.scalar_tensor_tensor(oi[c % 2][:], gq[:, t, c], sc.col(O_MUL), uq[:],
                                                 ALU.mult, ALU.mult).then_inc(s_oi, 1)
                        wait(dve, s_hi, hi.up())
                        dve.tensor_tensor(op[:, c, 1].rearrange("p a n -> p (a n)"), oi[c % 2][:],
                                          op[:, c, 0].rearrange("p a n -> p (a n)"), ALU.subtract).then_inc(s_lo, 1)
                        lo.up()

                def rows(t):
                    for st in range(ST):
                        wait(dve, s_full, full.up())
                        wait(dve, s_r[st % 2], r[st % 2].up(16))
                        dve.scalar_tensor_tensor(res[st % 2][:], bank[(full.n - 1) % 8][:], sc.col(O_S),
                                                 res[st % 2][:], ALU.mult, ALU.add).then_inc(s_y, 1)
                        y.up()

                def turn(t, last):
                    for k in range(2):
                        if not (last and k):
                            chunks(t + k + 1)
                        rows(t + k)

                chunks(0)
                tiles_in_pairs(dve, [uqc, hi, lo, full, *r, y], growth, turn)

            @block.tensor
            def _(pe):
                lo, y = Count(s_lo), Count(s_y)
                pe.wait_ge(s_w, 16 * CH)

                def turn(t, last):
                    for k in range(2):
                        banks = [bank[k * ST + st] for st in range(ST)]
                        wait(pe, s_y, y.value(ST))
                        y.up(ST)
                        for c in range(CH):
                            wait(pe, s_lo, lo.up())
                            for st in range(ST):
                                cols = slice(st * P, (st + 1) * P)
                                for j in range(PIECES):
                                    ic = c * PIECES + j
                                    rows_of = slice(ic // C * C, ic // C * C + C)
                                    for a, z in ((0, 0), (0, 1), (1, 0)):
                                        last = pe.matmul(banks[st][:].rearrange("p (r n) -> p r n", r=C),
                                                         op[:, c, a, j, cols], w[:, rows_of, z, ic % C, :],
                                                         start=(c, j, a, z) == (0, 0, 0, 0),
                                                         stop=(c, j, a) == (CH - 1, PIECES - 1, 1))
                                if c == CH - 1:
                                    last.then_inc(s_full, 1)
                                elif st == ST - 1:
                                    last.then_inc(s_pass, 1)

                tiles_in_pairs(pe, [lo, y], growth, turn)


def block_program(nc, x, ctxT, wf, attn_w, b_qkv, b_o, rope, out):
    def scratch(name, shape, dtype):
        return nc.dram_tensor("scratch_" + name, shape, dtype, kind="Internal").ap()

    wf_parts = scratch("wf_parts", [3 * IC, P, 2, 512], F16)
    wa_parts = scratch("wa_parts", [4, P, 2, C, E], F16)
    x1 = scratch("x1", [B, S, E], F32)
    xn2T = scratch("xn2T", [B, P, ST, C * P], F32)
    x_int = scratch("x_int", [T, P, 2, C, S], F16)
    g_raw = scratch("g_raw", [T, CH, P, CW], F32)
    u_raw = scratch("u_raw", [T, CH, P, CW], F32)
    with ExitStack() as ctx:
        def sb(name, shape, dtype):
            return ctx.enter_context(nc.sbuf_tensor(name, shape, dtype))

        peak_x = sb("peak_x", [P, ST], F32)
        weight_stage(nc, wf.rearrange("(n k) p c -> n k p c", k=2), attn_w,
                     wf_parts.rearrange("(n k) p a c -> n k p a c", k=2), wa_parts)
        attention_stage(nc, x, ctxT, wa_parts, [b_qkv[0], b_qkv[1], b_qkv[2], b_o], rope, x1, xn2T, peak_x)
        table = sb("scalars", [P, N_SCALARS], F32)
        peak_g, peak_u, peak_f, peak_o = (sb(f"peak_{n}", [P, 2 * CH], F32) for n in "gufo")
        gate_stage(nc, wf_parts, xn2T, x_int, g_raw, table, peak_x, peak_g)
        gq = sb("gq", [P, T, CH, CW], I16)
        up_stage(nc, wf_parts, x_int, g_raw, u_raw, table, peak_g, peak_u, peak_f, gq)
        peak_stage(nc, u_raw, table, peak_u, peak_f, peak_o, gq)
        down_stage(nc, wf_parts, u_raw, x1, out, table, peak_o, gq)


def rope_tables():
    inv = (np.float32(1.0) / np.float32(10000.0) ** (np.arange(0, D, 2, dtype=np.float32) / np.float32(D))).astype(np.float32)
    angle = inv[:, None] * np.arange(S, dtype=np.float32)[None, :]
    cos, sin = np.cos(angle), np.sin(angle)
    return np.stack([np.tile(cos, (2 * HG, 1)), np.tile(np.concatenate([-sin, sin]), (HG, 1))]).astype(np.float32)


def kernel(**inputs):
    import concourse.bacc as bacc
    from concourse.bass_utils import run_bass_kernel_spmd

    a = {k: np.asarray(v) for k, v in inputs.items()}
    down = a["L0_ffn_w_down"].reshape(C, P, IC // C, 512).transpose(2, 0, 1, 3).reshape(IC, P, 512)
    arrays = {
        "in_x": a["x"],
        "in_ctxT": a["ctx_1024"].transpose(0, 2, 1),
        "in_wf": np.concatenate([a["L0_ffn_w_gate"].reshape(IC, P, E), a["L0_ffn_w_up"].reshape(IC, P, E), down]),
        "in_attn_w": np.stack([a[f"L0_xattn_W{m}"].T.reshape(C, P, E).transpose(1, 0, 2) for m in "qkvo"]),
        "in_b_qkv": np.stack([a[f"L0_xattn_b{m}"].reshape(C, P).T for m in "qkv"]),
        "in_b_o": np.broadcast_to(a["L0_xattn_bo"], (P, E)),
        "in_rope": rope_tables(),
    }
    arrays = {k: np.ascontiguousarray(v) for k, v in arrays.items()}
    nc = bacc.Bacc("TRN2", target_bir_lowering=False, num_devices=1)
    args = [nc.dram_tensor(k, v.shape, mybir.dt.from_np(v.dtype), kind="ExternalInput").ap() for k, v in arrays.items()]
    out = nc.dram_tensor("out", (B, S, E), F32, kind="ExternalOutput").ap()
    block_program(nc, *args, out)
    result = run_bass_kernel_spmd(nc, [arrays], core_ids=[0])
    return result.results[0]["out"]
```

```python
from contextlib import ExitStack

import concourse.bass as bass
import numpy as np
from concourse import mybir
from concourse.alu_op_type import AluOpType as ALU

F32, F16, BF16 = mybir.dt.float32, mybir.dt.float16, mybir.dt.bfloat16
I16, U16 = mybir.dt.int16, mybir.dt.uint16
ACT = mybir.ActivationFunctionType
AXX = mybir.AxisListType.X

P = 128
B, S, E = 8, 512, 512
H, D = 16, 32
I = 1536
C = E // P
ST = S // P
HG = P // D
IC = I // P
BLOCK = 32
EPS = 1e-5
TINY = 1e-12
QMAX_W, QMAX_A = 7.0, 32767.0

X_UP = 16.0
W_UP = 256.0
QK_UP = 8.0
PROJ_DOWN = 1.0 / (X_UP * W_UP)
M_DOWN = 64.0
EXP_SCALE = 1.0 / (float(np.sqrt(D)) * QK_UP * QK_UP)
MASKED = -float(2.0 ** 100)
ROLE_Q = ("hi", "lo", "hi")
ROLE_K = ("hi", "hi", "lo")
KROWS = 3 * D
MROWS = KROWS + 2

PAIRS_LOOPED = 2


class Count:

    def __init__(self, sem):
        self.sem, self.n, self.turn, self.growth = sem, 0, None, 0

    def value(self, back=0):
        assert self.turn is None or self.n > back
        return self.n - back if self.turn is None else self.turn * self.growth + (self.n - back)

    def up(self, k=1):
        self.n += k
        return self.value()

    def enter(self, turn, growth):
        self.turn, self.growth, self.entered = turn, growth, self.n

    def leave(self, turns):
        assert self.n - self.entered == self.growth, (self.sem, self.n - self.entered, self.growth)
        self.turn, self.n = None, self.n + (turns - 1) * self.growth


def wait(eng, count_or_sem, value=None, past=None):
    sem = count_or_sem.sem if isinstance(count_or_sem, Count) else count_or_sem
    if value is None:
        value = count_or_sem.value()
    if not isinstance(value, int) or value > 0:
        eng.wait_ge(sem, value)
        if past and not isinstance(value, int):
            eng.sem_inc(past, 1)


class Batch:

    def __init__(self, c, turn=None):
        self.c, self.turn, self.par = c, turn, c % 2

    def index(self):
        return self.c if self.turn is None else self.turn * 2 + self.c

    def step(self, k):
        return Batch(self.c + k, self.turn)


def weight_stage(nc, wf, attn_w, wf_parts, wa_parts):
    N = IC // 2
    NB = 2 * 512 // BLOCK
    with ExitStack() as ctx:
        def sb(n, s, d):
            return ctx.enter_context(nc.sbuf_tensor("w_" + n, s, d))

        raw = [sb(f"raw{k}", [P, 2, 512], F32) for k in range(2)]
        top = sb("top", [P, 2, NB], F32)
        inv = sb("inv", [P, 2, NB], F32)
        ints = sb("ints", [P, 2, 2 * 512], I16)
        deq = [sb(f"deq{k}", [P, 2, 512], F32) for k in range(2)]
        parts = [sb(f"parts{k}", [P, 2, 2, 512], F16) for k in range(2)]
        ident = sb("ident", [P, P], F32)
        aw = [sb(f"aw{k}", [P, C, E], F32) for k in range(2)]
        ap = [sb(f"ap{k}", [P, 2, C, E], F16) for k in range(2)]
        bank = [ctx.enter_context(nc.psum_tensor(f"w_bank{k}", [P, 2, 512], F32)) for k in range(2)]

        def sem(n):
            return ctx.enter_context(nc.semaphore("w_" + n))

        s_in = [sem(f"in{k}") for k in range(2)]
        s_out = [sem(f"out{k}") for k in range(2)]
        s_q = sem("quant")
        s_t = sem("transposed")
        s_hi = sem("hi")
        s_lo = sem("lo")
        s_ain = [sem(f"ain{k}") for k in range(2)]
        s_ahi, s_alo = sem("ahi"), sem("alo")
        s_aout = [sem(f"aout{k}") for k in range(2)]
        s_id = sem("id")

        with nc.Block() as block:
            @block.sync
            def _(sp):
                def load(k, n):
                    sp.dma_start(raw[k][:], wf[n].rearrange("k p c -> p k c")).then_inc(s_in[k], 16)

                def store(k, n):
                    sp.wait_ge(s_lo, n + 1)
                    sp.dma_start(wf_parts[n].rearrange("k p a c -> p k a c"), parts[k][:]).then_inc(s_out[k], 16)

                for m in range(4):
                    k = m % 2
                    if m >= 2:
                        sp.wait_ge(s_alo, m - 1)
                    sp.dma_start(aw[k][:], attn_w[m]).then_inc(s_ain[k], 16)
                load(0, 0)
                load(1, 1)
                for m in range(4):
                    sp.wait_ge(s_alo, m + 1)
                    sp.dma_start(wa_parts[m], ap[m % 2][:]).then_inc(s_aout[m % 2], 16)
                with sp.Fori(0, N // 2 - 1) as i:
                    for k in range(2):
                        n = i * 2 + k
                        sp.wait_ge(s_q, n * 5 + 4)
                        load(k, n + 2)
                        store(k, n)
                for k in range(2):
                    store(k, N - 2 + k)
                for k in range(2):
                    sp.wait_ge(s_out[k], 16 * (N // 2))
                    sp.wait_ge(s_aout[k], 32)

            @block.gpsimd
            def _(pool):
                pool.memset(ident[:], 0.0).then_inc(s_id, 1)
                pool.wait_ge(s_id, 1)
                pool.affine_select(out=ident[:], in_=ident[:], compare_op=ALU.not_equal, fill=1.0, base=0,
                                   pattern=[[-1, P]], channel_multiplier=1).then_inc(s_id, 1)

            @block.scalar
            def _(act):
                for m in range(4):
                    act.wait_ge(s_ain[m % 2], 16 * (m // 2 + 1))
                    if m >= 2:
                        act.wait_ge(s_aout[m % 2], 16)
                    act.activation(ap[m % 2][:, 0], aw[m % 2][:], ACT.Copy, scale=W_UP).then_inc(s_ahi, 1)

                def pair(k, n, first):
                    act.wait_ge(s_t, n + 1)
                    if not first:
                        act.wait_ge(s_out[k], n * 8 - k * 8)
                    act.activation(parts[k][:, :, 0], bank[k][:], ACT.Copy, scale=W_UP).then_inc(s_hi, 1)

                pair(0, 0, True)
                pair(1, 1, True)
                with act.Fori(1, N // 2) as i:
                    for k in range(2):
                        pair(k, i * 2 + k, False)

            @block.vector
            def _(dve):
                for m in range(4):
                    dve.wait_ge(s_ahi, m + 1)
                    dve.scalar_tensor_tensor(ap[m % 2][:, 1], aw[m % 2][:], W_UP, ap[m % 2][:, 0],
                                             ALU.mult, ALU.subtract).then_inc(s_alo, 1)

                def quantise(k, n):
                    dve.wait_ge(s_in[k], n * 8 - k * 8 + 16)
                    blocks = raw[k][:].rearrange("p k (b c) -> p (k b) c", c=BLOCK)
                    dve.tensor_reduce(top[:, k], blocks, AXX, ALU.max, apply_absolute_value=True).then_inc(s_q, 1)
                    dve.wait_ge(s_q, n * 5 + 1)
                    dve.tensor_scalar(top[:, k], top[:, k], 1.0 / QMAX_W, TINY, ALU.mult, ALU.max).then_inc(s_q, 1)
                    dve.wait_ge(s_q, n * 5 + 2)
                    dve.reciprocal(inv[:, k], top[:, k]).then_inc(s_q, 1)
                    dve.wait_ge(s_q, n * 5 + 3)
                    q = ints[:, k].rearrange("p (b c) -> p b c", c=BLOCK)
                    dve.tensor_tensor(q, blocks, inv[:, k].unsqueeze(2).to_broadcast([P, NB, BLOCK]),
                                      ALU.mult).then_inc(s_q, 1)
                    dve.wait_ge(s_q, n * 5 + 4)
                    w = deq[k][:].rearrange("p k (b c) -> p (k b) c", c=BLOCK)
                    dve.tensor_tensor(w, q, top[:, k].unsqueeze(2).to_broadcast([P, NB, BLOCK]),
                                      ALU.mult).then_inc(s_q, 1)

                def low(k, n):
                    dve.wait_ge(s_hi, n + 1)
                    dve.scalar_tensor_tensor(parts[k][:, :, 1], bank[k][:], W_UP, parts[k][:, :, 0],
                                             ALU.mult, ALU.subtract).then_inc(s_lo, 1)

                quantise(0, 0)
                quantise(1, 1)
                low(0, 0)
                with dve.Fori(1, N // 2) as i:
                    quantise(0, i * 2)
                    low(1, i * 2 - 1)
                    quantise(1, i * 2 + 1)
                    low(0, i * 2)
                low(1, N - 1)

            @block.tensor
            def _(pe):
                pe.wait_ge(s_id, 2)

                def pair(k, n, first):
                    pe.wait_ge(s_q, n * 5 + 5)
                    if not first:
                        pe.wait_ge(s_lo, n - 1)
                    for t in range(2):
                        for c in range(C):
                            cols = slice(c * P, (c + 1) * P)
                            last = pe.transpose(bank[k][:, t, cols], deq[k][:, t, cols], ident[:])
                    last.then_inc(s_t, 1)

                pair(0, 0, True)
                pair(1, 1, True)
                with pe.Fori(1, N // 2) as i:
                    for k in range(2):
                        pair(k, i * 2 + k, False)


def attention_stage(nc, x, ctxT, wa_parts, biases, rope, x1, xn2T, peak):
    with ExitStack() as ctx:
        def sb(n, s, d):
            return ctx.enter_context(nc.sbuf_tensor("a_" + n, s, d))

        def sem(n):
            return ctx.enter_context(nc.semaphore("a_" + n))

        W = {m: sb("W" + m, [P, 2, C, E], F16) for m in "qkvo"}
        b_q, b_k, b_v = (sb("b" + m, [P, C], F32) for m in "qkv")
        b_o = sb("bo", [P, E], F32)
        cos, sin = sb("cos", [P, S], F32), sb("sin", [P, S], F32)
        xt = sb("xt", [P, ST, E], F32)
        ct = sb("ct", [P, C, S], F32)
        sum1 = [ct[:, k] for k in range(2)]
        resid = [ct[:, 2 + k] for k in range(2)]
        xp = sb("xp", [P, 2, C, S], F16)
        cp = sb("cp", [P, 2, C, S], F16)
        tmp = sb("tmp", [P, 4, S], F32)
        rot = sb("rot", [P, 2, S], F32)
        qkp = sb("qkp", [P, 2, C, S], F16)
        qs = [sb(f"qs{k}", [P, C, HG, S], F16) for k in range(2)]
        ks = [sb(f"ks{k}", [P, C, HG, S], F16) for k in range(2)]
        v = sb("v", [P, ST, E], F32)
        pt = sb("pt", [P, 10, S], F32)
        rden, att = sb("rden", [P, S], F32), sb("att", [P, S], F32)
        aop = [sb(f"aop{k}", [P, 2, C, S], F16) for k in range(2)]
        mx = sb("mx", [P, ST, HG], F32)
        mp = sb("mp", [P, ST, 2, HG], F16)
        mrow = sb("mrow", [2 * HG, S], F16)
        stats, mv = sb("stats", [P, ST, 6], F32), sb("mv", [P, ST, 2], F32)
        rstd, power = sb("rstd", [P, ST], F32), sb("power", [P, ST], F32)
        stats2, mv2, rstd2 = sb("stats2", [P, ST, 6], F32), sb("mv2", [P, ST, 2], F32), sb("rstd2", [P, ST], F32)
        peak_b = sb("peakb", [P, ST], F32)
        ident = sb("ident", [P, P], F32)
        ident16, identb = sb("ident16", [P, P], F16), sb("identb", [P, P], BF16)
        mask_s, mask_t = sb("mask_s", [P, P], BF16), sb("mask_t", [P, P], BF16)
        ones = sb("ones", [P, D], F32)

        def ps(n, d=F32):
            return ctx.enter_context(nc.psum_tensor("a_" + n, [P, 512], d))

        proj = [ps(f"proj{k}") for k in range(2)]
        sc = [ps(f"sc{k}") for k in range(2)]
        sct = [ps(f"sct{k}") for k in range(2)]
        ps_o, ps_d = ps("o"), ps("d")

        s_const = sem("const")
        s_w = sem("w")
        s_dc = sem("dve_const")
        s_x, s_c = sem("x_in"), sem("c_in")
        s_ln = sem("ln_stats")
        s_rstd = sem("ln_rstd")
        s_xn = sem("xn")
        s_chi, s_clo = sem("c_hi"), sem("c_lo")
        s_full = sem("proj_full")
        s_evac = sem("proj_evac")
        s_rot = sem("rotated")
        s_cos, s_mul = sem("times_cos"), sem("rot_times_sin")
        s_sum = sem("rope_sum")
        s_hi, s_lo = sem("hi"), sem("lo")
        s_kst, s_qst = sem("k_stacked"), sem("q_stacked")
        s_sfull, s_sread = sem("sc_full"), sem("sc_read")
        s_m = sem("m_parts")
        s_min = sem("m_placed")
        s_tfull, s_exp = sem("sct_full"), sem("exp")
        s_pv, s_pvread, s_norm = sem("pv"), sem("pv_read"), sem("norm")
        s_aohi, s_aolo = sem("ao_hi"), sem("ao_lo")
        s_res, s_resb = [sem(f"resid_in{k}") for k in range(2)], sem("resid_bias")
        s_x1, s_ln2, s_rstd2, s_xn2, s_peak = sem("x1"), sem("ln2_stats"), sem("ln2_rstd"), sem("xn2"), sem("peak")
        s_x1out = [sem(f"x1_out{k}") for k in range(2)]
        s_xn2out = sem("xn2_out")

        growth = {
            s_x: 32, s_c: 32, s_ln: 16, s_rstd: 4, s_xn: 8, s_chi: 2, s_clo: 2, s_full: 48, s_evac: 48,
            s_rot: 16, s_cos: 16, s_mul: 16, s_sum: 16, s_hi: 24, s_lo: 24, s_kst: 384, s_qst: 384,
            s_sfull: 88, s_sread: 88, s_m: 16, s_min: 256, s_tfull: 80, s_exp: 80, s_pv: 8, s_pvread: 16,
            s_norm: 16, s_aohi: 8, s_aolo: 8, s_res[0]: 64, s_res[1]: 64, s_resb: 8, s_x1: 8, s_ln2: 16, s_rstd2: 16,
            s_xn2: 8, s_peak: 10, s_x1out[0]: 64, s_x1out[1]: 64, s_xn2out: 32,
        }

        def run(eng, counts, turn):
            turn(Batch(-2), False, False)
            turn(Batch(-1), False, True)
            turn(Batch(0), False, True)
            turn(Batch(1), True, True)
            with eng.Fori(0, PAIRS_LOOPED) as i:
                for c in counts:
                    c.enter(i, growth[c.sem])
                turn(Batch(2, i), True, True)
                turn(Batch(3, i), True, True)
            for c in counts:
                c.leave(PAIRS_LOOPED)
            turn(Batch(6), True, True)
            turn(Batch(7), True, False)
            turn(Batch(8), True, False)

        def order(b, has_prev, has_next):
            here, n, p, nn = 0 <= b.c < B, b.step(1), b.step(-1), b.step(2)
            has_next_but_one = b.turn is not None or b.c + 2 < B
            for step in (
                ("exp", b, 0), ("norm_x", n), ("c_parts", n), ("pv", b, 0), ("scores", b, 1),
                ("x", n), ("ao_norm", b, 0), ("rows", b, 1), ("out", p, (0, 1)), ("ao_parts", b, 0),
                ("exp", b, 1), ("out", p, (2, 3)), ("pv", b, 1), ("out_end", p), ("scores", b, 2),
                ("k", n, (0,)), ("rows", b, 2), ("k", n, (1,)), ("ao_norm", b, 1), ("k", n, (2, 3)),
                ("exp", b, 2), ("k_end", n), ("ao_parts", b, 1), ("xn2", p), ("load", nn), ("q", n, (0,)),
                ("pv", b, 2), ("scores", b, 3), ("q", n, (1,)), ("rows", b, 3), ("q", n, (2,)),
                ("ao_norm", b, 2), ("q", n, (3,)),
                ("exp", b, 3), ("q_end", n), ("ao_parts", b, 2), ("pv", b, 3), ("v", n, (0, 1)),
                ("ao_norm", b, 3), ("scores", n, 0), ("v", n, (2,)), ("rows", n, 0), ("ao_parts", b, 3),
                ("v", n, (3,)),
            ):
                if (step[1] is b and here or step[1] is n and has_next or step[1] is p and has_prev
                        or step[1] is nn and has_next_but_one):
                    yield step

        def heads_blocks(pair, transposed):
            a, z = 2 * pair, 2 * pair + 1
            if transposed:
                return [[(a, 0, 0)], [(a, 1, 0), (a, 3, 384)], [(z, 0, 0)], [(z, 1, 0), (z, 3, 384)],
                        [(a, 2, 0), (z, 2, 256)]]
            return [[(a, 3, 0)], [(a, 2, 0), (a, 0, 384)], [(z, 3, 0)], [(z, 2, 0), (z, 0, 384)],
                    [(a, 1, 0), (z, 1, 256)]]

        def stack(sp, dst, src, roles, s):
            for j in range(HG):
                for r, role in enumerate(roles):
                    sp.dma_start(dst[r * D:(r + 1) * D, :, j, :],
                                 src[j * D:(j + 1) * D, 0 if role == "hi" else 1, :, :]).then_inc(s, 16)
        s_past = {e: sem(f"past_{e}") for e in ("sp", "pool", "dve", "act")}

        with nc.Block() as block:
            @block.sync
            def _(sp):
                def sp_wait(*what):
                    wait(sp, *what, past=s_past["sp"])

                for n, m in enumerate("qkvo"):
                    sp.dma_start(W[m][:], wa_parts[n]).then_inc(s_w, 16)
                for dst, src in ((b_q, biases[0]), (b_k, biases[1]), (b_v, biases[2])):
                    sp.dma_start(dst[:], src).then_inc(s_w, 16)
                sp.dma_start(b_o[:], biases[3]).then_inc(s_w, 16)
                sp.dma_start(cos[:], rope[0]).then_inc(s_w, 16)
                sp.dma_start(sin[:], rope[1]).then_inc(s_w, 16)
                full, sread, x1c, lo = (Count(s) for s in (s_full, s_sread, s_x1, s_lo))
                evac, clo = Count(s_evac), Count(s_clo)
                x1out, xn2out = [Count(s) for s in s_x1out], Count(s_xn2out)
                counts = [full, sread, x1c, lo, evac, clo, *x1out, xn2out]

                def load_resid(t, st):
                    sp_wait(x1c)
                    sp.dma_start(resid[st % 2], x[t.index(), st * P:(st + 1) * P, :]).then_inc(s_res[st % 2], 16)

                def turn(b, has_prev, has_next):
                    for kind, t, *arg in order(b, has_prev, has_next):
                        if kind == "load":
                            sp_wait(full)
                            for c in x1out:
                                sp_wait(c)
                            sp_wait(xn2out)
                            sp.dma_start(xt[:], x[t.index()].rearrange("(s p) e -> p s e", p=P)).then_inc(s_x, 16)
                            sp_wait(clo)
                            sp.dma_start(ct[:], ctxT[t.index()].rearrange("(c p) t -> p c t", p=P)).then_inc(s_c, 16)
                        elif kind == "c_parts":
                            clo.up()
                        elif kind == "x":
                            full.up(4), evac.up(4), lo.up(4)
                        elif kind in "kqv":
                            full.up(len(arg[0])), evac.up(len(arg[0]))
                            if kind != "v":
                                lo.up(len(arg[0]))
                        elif kind == "k_end":
                            sp_wait(lo)
                            stack(sp, ks[t.par], qkp, ROLE_K, s_kst)
                        elif kind == "q_end":
                            sp_wait(lo)
                            stack(sp, qs[t.par], qkp, ROLE_Q, s_qst)
                        elif kind == "scores":
                            sread.up(10)
                        elif kind == "rows":
                            sp_wait(s_sread, sread.up())
                            for part in range(2):
                                sp.dma_start(qs[t.par][KROWS + part:KROWS + part + 1, arg[0], :, :],
                                             mrow[part * HG:(part + 1) * HG, :]).then_inc(s_min, 16)
                        elif kind == "out":
                            full.up(len(arg[0])), evac.up(len(arg[0]))
                            if arg[0][0] == 0:
                                sp_wait(clo)
                                sp_wait(xn2out)
                                load_resid(t, 0)
                                load_resid(t, 1)
                            for st in arg[0]:
                                sp_wait(s_x1, x1c.up())
                                sp.dma_start(x1[t.index(), st * P:(st + 1) * P, :], sum1[st % 2]
                                             ).then_inc(s_x1out[st % 2], 16)
                                x1out[st % 2].up(16)
                                if st < 2:
                                    load_resid(t, st + 2)
                        elif kind == "xn2":
                            full.up(ST)
                            sp_wait(s_evac, evac.up(ST))
                            sp.dma_start(xn2T[t.index()], ct[:]).then_inc(s_xn2out, 16)
                            xn2out.up(16)

                run(sp, counts, turn)
                for c in x1out:
                    sp_wait(c)
                sp_wait(xn2out)

            @block.gpsimd
            def _(pool):
                def pool_wait(*what):
                    wait(pool, *what, past=s_past["pool"])

                pool.memset(power[:], -0.5).then_inc(s_const, 1)
                pool.memset(ident[:], 0.0).then_inc(s_const, 1)
                pool.memset(ident16[:], 0.0).then_inc(s_const, 1)
                pool.memset(identb[:], 0.0).then_inc(s_const, 1)
                pool.memset(mask_s[:], 0.0).then_inc(s_const, 1)
                pool.memset(mask_t[:], 0.0).then_inc(s_const, 1)
                pool.memset(ones[:], 1.0).then_inc(s_const, 1)
                pool.wait_ge(s_const, 7)
                for t in (ident, ident16, identb):
                    pool.affine_select(out=t[:], in_=t[:], compare_op=ALU.not_equal, fill=1.0, base=0,
                                       pattern=[[-1, P]], channel_multiplier=1).then_inc(s_const, 1)
                pool.affine_select(out=mask_s[:], in_=mask_s[:], compare_op=ALU.is_ge, fill=MASKED, base=0,
                                   pattern=[[-1, P]], channel_multiplier=1).then_inc(s_const, 1)
                pool.affine_select(out=mask_t[:], in_=mask_t[:], compare_op=ALU.is_ge, fill=MASKED, base=0,
                                   pattern=[[1, P]], channel_multiplier=-1).then_inc(s_const, 1)
                pool.wait_ge(s_w, 160)
                ln, rotc, rstdc, ln2, rstd2c, xn1 = (
                    Count(s) for s in (s_ln, s_rot, s_rstd, s_ln2, s_rstd2, s_xn))
                res = [Count(s) for s in s_res]
                counts = [ln, rotc, rstdc, *res, ln2, rstd2c, xn1]

                def resid_bias(st):
                    pool_wait(s_res[st % 2], res[st % 2].up(16))
                    pool.tensor_tensor(resid[st % 2], resid[st % 2], b_o[:], ALU.add).then_inc(s_resb, 1)

                def turn(b, has_prev, has_next):
                    for kind, t, *arg in order(b, has_prev, has_next):
                        if kind == "norm_x":
                            pool_wait(s_ln, ln.up(8))
                            pool_wait(xn1)
                            pool.tensor_scalar(rstd[:], mv[:, :, 1], EPS, None, ALU.add).then_inc(s_rstd, 1)
                            pool_wait(s_rstd, rstdc.up())
                            pool.tensor_tensor(rstd[:], rstd[:], power[:], ALU.pow).then_inc(s_rstd, 1)
                            rstdc.up()
                            xn1.up(4)
                        elif kind in "kq":
                            for eo in arg[0]:
                                pool_wait(s_rot, rotc.up())
                                pool.tensor_tensor(rot[:, eo % 2], rot[:, eo % 2], sin[:], ALU.mult).then_inc(s_mul, 1)
                        elif kind == "out":
                            if arg[0][0] == 0:
                                resid_bias(0)
                                resid_bias(1)
                            for st in arg[0]:
                                pool_wait(s_ln2, ln2.up(2))
                                pool.tensor_scalar(rstd2[:, st:st + 1], mv2[:, st, 1:2], EPS, None,
                                                   ALU.add).then_inc(s_rstd2, 1)
                                pool_wait(s_rstd2, rstd2c.up())
                                pool.tensor_tensor(rstd2[:, st:st + 1], rstd2[:, st:st + 1], power[:, 0:1],
                                                   ALU.pow).then_inc(s_rstd2, 1)
                                rstd2c.up()
                                if st < 2:
                                    resid_bias(st + 2)

                run(pool, counts, turn)

            @block.scalar
            def _(act):
                full, lo, xn2c, clo = (Count(s) for s in (s_full, s_lo, s_xn2, s_clo))
                tfull, pv, c_in, summ, norm, aolo = (Count(s) for s in (s_tfull, s_pv, s_c, s_sum, s_norm, s_aolo))
                kst, qst = Count(s_kst), Count(s_qst)
                x1out, xn2out = [Count(s) for s in s_x1out], Count(s_xn2out)
                counts = [full, lo, xn2c, clo, tfull, pv, c_in, summ, norm, aolo, kst, qst, *x1out, xn2out]
                act.wait_ge(s_w, 160)
                act.wait_ge(s_dc, 4)

                def high(item):
                    wait(act, s_sum, summ.up())
                    act.activation(qkp[:, 0, item], tmp[:, item], ACT.Copy).then_inc(s_hi, 1)

                def turn(b, has_prev, has_next):
                    for kind, t, *arg in order(b, has_prev, has_next):
                        if kind == "c_parts":
                            wait(act, s_c, c_in.up(16))
                            act.activation(cp[:, 0], ct[:], ACT.Copy, scale=X_UP).then_inc(s_chi, 1)
                            clo.up()
                        elif kind == "x":
                            for ec in range(C):
                                wait(act, s_full, full.up())
                                wait(act, s_lo, lo.value(3))
                                act.activation(xp[:, 0, ec], proj[ec % 2][:], ACT.Copy, scale=X_UP).then_inc(s_hi, 1)
                                act.activation(tmp[:, ec], proj[ec % 2][:], ACT.Copy, scale=X_UP).then_inc(s_evac, 1)
                                lo.up()
                        elif kind in "kq":
                            bias = b_k if kind == "k" else b_q
                            for eo in arg[0]:
                                wait(act, s_full, full.up())
                                wait(act, s_lo, lo.value(3))
                                act.activation(tmp[:, eo], proj[eo % 2][:], ACT.Identity, bias=bias[:, eo:eo + 1],
                                               scale=PROJ_DOWN * QK_UP).then_inc(s_evac, 1)
                                lo.up()
                                if eo == 2:
                                    wait(act, qst if kind == "k" else kst)
                                if eo >= 2:
                                    high(eo - 2)
                        elif kind in ("k_end", "q_end"):
                            high(2)
                            high(3)
                            (kst if kind == "k_end" else qst).up(192)
                        elif kind == "v":
                            for tb in arg[0]:
                                wait(act, s_full, full.up())
                                act.activation(v[:, tb], proj[tb % 2][:], ACT.Copy, scale=PROJ_DOWN * X_UP).then_inc(s_evac, 1)
                        elif kind == "exp":
                            for u in range(10):
                                wait(act, s_tfull, tfull.up())
                                if u == 0:
                                    wait(act, pv)
                                act.activation(pt[:, u], sct[u % 2][:], ACT.Exp, scale=EXP_SCALE).then_inc(s_exp, 1)
                        elif kind == "pv":
                            wait(act, s_pv, pv.up())
                            wait(act, aolo)
                            act.activation(att[:], ps_o[:], ACT.Copy).then_inc(s_pvread, 1)
                            act.activation(rden[:], ps_d[:], ACT.Copy).then_inc(s_pvread, 1)
                        elif kind == "ao_parts":
                            g = arg[0]
                            wait(act, s_norm, norm.up(2))
                            act.activation(aop[t.par][:, 0, g], att[:], ACT.Identity,
                                           bias=b_v[:, g:g + 1]).then_inc(s_aohi, 1)
                            aolo.up()
                        elif kind == "out":
                            for st in arg[0]:
                                wait(act, s_full, full.up())
                                wait(act, clo)
                                if st == 0:
                                    wait(act, xn2out)
                                wait(act, x1out[st % 2])
                                if st >= 2:
                                    wait(act, s_xn2, xn2c.value(1))
                                act.activation(sum1[st % 2], proj[st % 2][:], ACT.Copy,
                                               scale=PROJ_DOWN).then_inc(s_evac, 1)
                                x1out[st % 2].up(16)
                                xn2c.up()
                        elif kind == "xn2":
                            for st in range(ST):
                                wait(act, s_full, full.up())
                                for c in x1out:
                                    wait(act, c)
                                act.activation(ct[:, st], proj[st % 2][:], ACT.Copy).then_inc(s_evac, 1)
                            xn2out.up(16)

                run(act, counts, turn)

            @block.vector
            def _(dve):
                x_in, rstdc, ln, xn = Count(s_x), Count(s_rstd), Count(s_ln), Count(s_xn)
                hi, evac, mul, summ, rotc = Count(s_hi), Count(s_evac), Count(s_mul), Count(s_sum), Count(s_rot)
                chi, lo, sfull, sread, mc, minn = (Count(s) for s in (s_chi, s_lo, s_sfull, s_sread, s_m, s_min))
                pvr, norm, aohi, resb = Count(s_pvread), Count(s_norm), Count(s_aohi), Count(s_resb)
                cosc, aolo = Count(s_cos), Count(s_aolo)
                x1c, ln2, rstd2c, xn2c, pk = Count(s_x1), Count(s_ln2), Count(s_rstd2), Count(s_xn2), Count(s_peak)
                counts = [x_in, rstdc, ln, xn, hi, evac, mul, summ, rotc, chi, lo, sfull, sread, mc, minn,
                          pvr, norm, aohi, resb, x1c, ln2, rstd2c, xn2c, pk, aolo, cosc]
                dve.memset(peak[:], 0.0).then_inc(s_dc, 1)
                for k in range(2):
                    dve.memset(ks[k][KROWS:P, :, :, :], M_DOWN)
                dve.wait_ge(s_w, 160)
                for t, up in ((b_q, QK_UP), (b_k, QK_UP), (b_v, X_UP)):
                    dve.tensor_scalar(t[:], t[:], up, None, ALU.mult).then_inc(s_dc, 1)

                def rotate(item):
                    wait(dve, s_evac, evac.up())
                    wait(dve, summ, past=s_past["dve"])
                    dve.stream_shuffle(rot[:, item % 2], tmp[:, item % 4],
                                       [(d + D // 2) % D for d in range(D)]).then_inc(s_rot, 1)
                    rotc.up()
                    wait(dve, s_rot, rotc.value())
                    dve.tensor_tensor(tmp[:, item % 4], tmp[:, item % 4], cos[:], ALU.mult).then_inc(s_cos, 1)

                def rope_sum(item):
                    wait(dve, s_cos, cosc.up())
                    wait(dve, s_mul, mul.up())
                    dve.tensor_tensor(tmp[:, item % 4], tmp[:, item % 4], rot[:, item % 2], ALU.add).then_inc(s_sum, 1)
                    summ.up()

                def low(item, dst):
                    wait(dve, s_hi, hi.up())
                    dve.tensor_tensor(dst[:, 1, item % 4], tmp[:, item % 4], dst[:, 0, item % 4],
                                      ALU.subtract).then_inc(s_lo, 1)
                    lo.up()

                def norm_x1(st):
                    wait(dve, s_rstd2, rstd2c.up(2))
                    dve.tensor_scalar(xt[:, st], sum1[st % 2], mv2[:, st, 0:1], rstd2[:, st:st + 1],
                                      ALU.subtract, ALU.mult).then_inc(s_xn2, 1)
                    xn2c.up()

                def top_x1(st):
                    wait(dve, s_xn2, xn2c.value())
                    wait(dve, s_peak, pk.value())
                    dve.tensor_reduce(peak_b[:, st:st + 1], xt[:, st], AXX, ALU.max,
                                      apply_absolute_value=True).then_inc(s_peak, 1)
                    pk.up()

                def turn(b, has_prev, has_next):
                    for kind, t, *arg in order(b, has_prev, has_next):
                        if kind == "norm_x":
                            wait(dve, s_x, x_in.up(16))
                            wait(dve, xn)
                            for st in range(ST):
                                dve.bn_stats(stats[:, st], xt[:, st]).then_inc(s_ln, 1)
                            for st in range(ST):
                                wait(dve, s_ln, ln.up(), past=s_past["dve"])
                                dve.bn_aggr(mv[:, st], stats[:, st]).then_inc(s_ln, 1)
                            ln.up(4)
                            wait(dve, s_rstd, rstdc.up(2))
                            for st in range(ST):
                                dve.tensor_scalar(xt[:, st], xt[:, st], mv[:, st, 0:1], rstd[:, st:st + 1],
                                                  ALU.subtract, ALU.mult).then_inc(s_xn, 1)
                            xn.up(4)
                        elif kind == "c_parts":
                            wait(dve, s_chi, chi.up())
                            dve.scalar_tensor_tensor(cp[:, 1], ct[:], X_UP, cp[:, 0], ALU.mult,
                                                     ALU.subtract).then_inc(s_clo, 1)
                        elif kind == "x":
                            for ec in range(C):
                                wait(dve, s_evac, evac.up())
                                low(ec, xp)
                        elif kind in "kq":
                            for eo in arg[0]:
                                rotate(eo)
                                if eo > 0:
                                    rope_sum(eo - 1)
                                if eo > 1:
                                    low(eo - 2, qkp)
                        elif kind in ("k_end", "q_end"):
                            rope_sum(3)
                            low(2, qkp)
                            low(3, qkp)
                        elif kind == "v":
                            evac.up(len(arg[0]))
                        elif kind == "xn2":
                            evac.up(4)
                        elif kind == "scores":
                            wait(dve, mc)
                            for pair in range(2):
                                for blocks in heads_blocks(pair, False):
                                    wait(dve, s_sfull, sfull.up())
                                    bank = sc[(sfull.n - 1) % 2]
                                    if blocks[0][1] == 1:
                                        last = dve.tensor_reduce(mx[:, 1, 2 * pair:2 * pair + 2],
                                                                 bank[:].rearrange("p (j t) -> p j t", j=2), AXX, ALU.max)
                                    else:
                                        for j, sbt, col in blocks:
                                            last = dve.tensor_reduce(mx[:, sbt, j:j + 1],
                                                                     bank[:, col:col + (sbt + 1) * P], AXX, ALU.max)
                                    last.then_inc(s_sread, 1)
                                    sread.up()
                            wait(dve, sread)
                            dve.tensor_scalar(mp[:, :, 0], mx[:], -1.0 / M_DOWN, None, ALU.mult).then_inc(s_m, 1)
                            wait(dve, s_m, mc.up())
                            dve.scalar_tensor_tensor(mp[:, :, 1], mx[:], -1.0 / M_DOWN, mp[:, :, 0],
                                                     ALU.mult, ALU.subtract).then_inc(s_m, 1)
                            mc.up()
                        elif kind == "rows":
                            wait(dve, s_sfull, sfull.up())
                            wait(dve, minn)
                            bank = sc[(sfull.n - 1) % 2]
                            dve.tensor_copy(mrow[:], bank[0:2 * HG, 0:S // 2].bitcast(F16)).then_inc(s_sread, 1)
                            sread.up()
                            minn.up(32)
                        elif kind == "ao_norm":
                            wait(dve, s_pvread, pvr.up(2))
                            dve.reciprocal(rden[:], rden[:]).then_inc(s_norm, 1)
                            wait(dve, s_norm, norm.up())
                            dve.tensor_tensor(att[:], att[:], rden[:], ALU.mult).then_inc(s_norm, 1)
                            norm.up()
                        elif kind == "ao_parts":
                            g = arg[0]
                            wait(dve, s_aohi, aohi.up())
                            dve.scalar_tensor_tensor(aop[t.par][:, 1, g], att[:], b_v[:, g:g + 1], aop[t.par][:, 0, g],
                                                     ALU.add, ALU.subtract).then_inc(s_aolo, 1)
                            aolo.up()
                        elif kind == "out":
                            for st in arg[0]:
                                wait(dve, s_evac, evac.up())
                                wait(dve, s_resb, resb.up())
                                dve.tensor_tensor(sum1[st % 2], sum1[st % 2], resid[st % 2], ALU.add).then_inc(s_x1, 1)
                                wait(dve, s_x1, x1c.up())
                                wait(dve, xn2c)
                                dve.bn_stats(stats2[:, st], sum1[st % 2]).then_inc(s_ln2, 1)
                                wait(dve, s_ln2, ln2.up(), past=s_past["dve"])
                                dve.bn_aggr(mv2[:, st], stats2[:, st]).then_inc(s_ln2, 1)
                                ln2.up()
                                if st > 0:
                                    top_x1(st - 1)
                                norm_x1(st)
                        elif kind == "out_end":
                            top_x1(3)
                            wait(dve, pk)
                            dve.tensor_tensor(peak[:], peak[:], peak_b[:], ALU.max).then_inc(s_peak, 1)
                            pk.up()

                run(dve, counts, turn)
                wait(dve, pk)

            @block.tensor
            def _(pe):
                evac, xn, lo, clo, kst, qst = (Count(s) for s in (s_evac, s_xn, s_lo, s_clo, s_kst, s_qst))
                sread, mc, minn, exp, pvr, aolo, xn2c = (Count(s) for s in (s_sread, s_m, s_min, s_exp, s_pvread, s_aolo, s_xn2))
                counts = [evac, xn, lo, clo, kst, qst, sread, mc, minn, exp, pvr, aolo, xn2c]
                pe.wait_ge(s_const, 12)
                pe.wait_ge(s_w, 160)
                pe.wait_ge(s_dc, 4)

                def next_bank():
                    evac.up()
                    wait(pe, s_evac, evac.value(2))
                    return proj[(evac.n - 1) % 2]

                def product(bank, left, right):
                    n = 0
                    for c in range(C):
                        for a, z in ((0, 0), (0, 1), (1, 0)):
                            last = pe.matmul(bank[:], left(a, c), right(z, c), start=n == 0, stop=n == 3 * C - 1)
                            n += 1
                    last.then_inc(s_full, 1)

                def turn(b, has_prev, has_next):
                    for kind, t, *arg in order(b, has_prev, has_next):
                        if kind == "x":
                            wait(pe, s_xn, xn.up(4))
                            for ec in range(C):
                                bank = next_bank()
                                for st in range(ST):
                                    last = pe.transpose(bank[:, st * P:(st + 1) * P], xt[:, st, ec * P:(ec + 1) * P], ident[:])
                                last.then_inc(s_full, 1)
                            lo.up(4)
                        elif kind == "k":
                            if arg[0][0] == 0:
                                wait(pe, s_clo, clo.up())
                            for eo in arg[0]:
                                cols = slice(eo * P, (eo + 1) * P)
                                product(next_bank(), lambda a, c: W["k"][:, a, c, cols], lambda z, c: cp[:, z, c])
                            lo.up(len(arg[0]))
                        elif kind == "q":
                            if arg[0][0] == 0:
                                wait(pe, s_lo, lo.value(4))
                            for eo in arg[0]:
                                cols = slice(eo * P, (eo + 1) * P)
                                product(next_bank(), lambda a, c: W["q"][:, a, c, cols], lambda z, c: xp[:, z, c])
                            lo.up(len(arg[0]))
                        elif kind == "v":
                            for tb in arg[0]:
                                cols = slice(tb * P, (tb + 1) * P)
                                product(next_bank(), lambda a, c: cp[:, a, c, cols], lambda z, c: W["v"][:, z, c])
                        elif kind == "scores":
                            g = arg[0]
                            if g == 0:
                                wait(pe, s_kst, kst.up(192))
                                wait(pe, s_qst, qst.up(192))
                            for pair in range(2):
                                for blocks in heads_blocks(pair, False):
                                    sread.up()
                                    wait(pe, s_sread, sread.value(2))
                                    bank = sc[(sread.n - 1) % 2]
                                    for j, sbt, col in blocks:
                                        w = (sbt + 1) * P
                                        pe.matmul(bank[:, col:col + w], qs[t.par][0:KROWS, g, j, sbt * P:w],
                                                  ks[t.par][0:KROWS, g, j, 0:w], start=True, stop=False)
                                        last = pe.matmul(bank[:, col + w - P:col + w], identb[:], mask_s[:],
                                                         start=False, stop=True)
                                    last.then_inc(s_sfull, 1)
                        elif kind == "rows":
                            wait(pe, s_m, mc.up(2))
                            sread.up()
                            wait(pe, s_sread, sread.value(2))
                            bank = sc[(sread.n - 1) % 2]
                            for st in range(ST):
                                last = pe.transpose(bank[0:2 * HG, st * P // 2:(st + 1) * P // 2].bitcast(F16),
                                                    mp[:, st].rearrange("p a j -> p (a j)"), ident16[:])
                            last.then_inc(s_sfull, 1)
                        elif kind == "exp":
                            g = arg[0]
                            wait(pe, s_min, minn.up(32))
                            for pair in range(2):
                                for blocks in heads_blocks(pair, True):
                                    exp.up()
                                    wait(pe, s_exp, exp.value(2))
                                    bank = sct[(exp.n - 1) % 2]
                                    for j, tb, col in blocks:
                                        w = S - tb * P
                                        pe.matmul(bank[:, col:col + w], ks[t.par][0:MROWS, g, j, tb * P:(tb + 1) * P],
                                                  qs[t.par][0:MROWS, g, j, tb * P:S], start=True, stop=False)
                                        last = pe.matmul(bank[:, col:col + P], identb[:], mask_t[:],
                                                         start=False, stop=True)
                                    last.then_inc(s_tfull, 1)
                        elif kind == "pv":
                            g = arg[0]
                            wait(pe, exp)
                            wait(pe, pvr)
                            where = {}
                            for pair in range(2):
                                for u, blocks in enumerate(heads_blocks(pair, True)):
                                    for j, tb, col in blocks:
                                        where[j, tb] = (pair * 5 + u, col)
                            for tb in range(ST):
                                w = S - tb * P
                                for dst in (ps_o, ps_d):
                                    for j in range(HG):
                                        u, col = where[j, tb]
                                        head = (HG * g + j) * D
                                        left = v[:, tb, head:head + D] if dst is ps_o else ones[:]
                                        last = pe.matmul(dst[j * D:(j + 1) * D, tb * P:S], left, pt[:, u, col:col + w],
                                                         start=tb == 0, stop=tb == ST - 1)
                            last.then_inc(s_pv, 1)
                            pvr.up(2)
                        elif kind == "ao_parts":
                            aolo.up()
                        elif kind == "out":
                            if arg[0][0] == 0:
                                wait(pe, aolo)
                            for st in arg[0]:
                                cols = slice(st * P, (st + 1) * P)
                                product(next_bank(), lambda a, c: aop[t.par][:, a, c, cols], lambda z, c: W["o"][:, z, c])
                        elif kind == "xn2":
                            wait(pe, s_xn2, xn2c.up(4))
                            for st in range(ST):
                                bank = next_bank()
                                for ec in range(C):
                                    last = pe.transpose(bank[:, ec * P:(ec + 1) * P], xt[:, st, ec * P:(ec + 1) * P], ident[:])
                                last.then_inc(s_full, 1)

                run(pe, counts, turn)


T = B
PIECES = 3
CH = IC // PIECES
CW = PIECES * S
RING = 6
RMAX = bass.bass_isa.ReduceOp.max
(X_MAX, X_S, X_INV, X_UNIT, G_MAX, G_S, G_INV, U_MAX, U_S, U_INV, F_MAX, F_UNIT, F_S, F_INV,
 O_MAX, O_UNIT, O_S, O_MUL, TOP, TMP, N_SCALARS) = range(21)


def tiles_in_pairs(eng, counts, growth, turn):
    turn(0, False)
    with eng.Fori(0, T // 2 - 2) as i:
        for c in counts:
            c.enter(i, growth[c.sem])
        turn(i * 2 + 2, False)
    for c in counts:
        c.leave(T // 2 - 2)
    turn(T - 2, True)


def three_pass_product(pe, bank, chunks, left, right):
    n = 0
    for c in range(chunks):
        for a, z in ((0, 0), (0, 1), (1, 0)):
            last = pe.matmul(bank, left(a, c), right(z, c), start=n == 0, stop=n == 3 * chunks - 1)
            n += 1
    return last


class Scalars:

    def __init__(self, dve, table, sem):
        self.dve, self.table, self.sem, self.n = dve, table, sem, 0

    def col(self, k):
        return self.table[:, k:k + 1]

    def after(self, ins):
        ins.then_inc(self.sem, 1)
        self.n += 1
        self.dve.wait_ge(self.sem, self.n)

    def quantisation(self, top, unit, scale, inverse):
        dve, col = self.dve, self.col
        if unit is None:
            self.after(dve.tensor_scalar(col(scale), col(top), 1.0 / QMAX_A, TINY, ALU.mult, ALU.max))
            self.after(dve.reciprocal(col(inverse), col(scale)))
            return
        self.after(dve.tensor_scalar(col(TMP), col(top), col(unit), 1.0 / QMAX_A, ALU.mult, ALU.mult))
        self.after(dve.tensor_scalar(col(scale), col(TMP), TINY, None, ALU.max))
        self.after(dve.reciprocal(col(TMP), col(scale)))
        self.after(dve.tensor_tensor(col(inverse), col(TMP), col(unit), ALU.mult))


def gate_stage(nc, wf, wf_parts, xn2T, x_int, g_raw, table, peak_x, peak_g, w_next):
    NB = 2 * 512 // BLOCK
    W_AT, W_DONE = (0, 3, 6), (2, 5, 8)
    with ExitStack() as ctx:
        def sb(n, s, d):
            return ctx.enter_context(nc.sbuf_tensor("g_" + n, s, d))

        def sem(n):
            return ctx.enter_context(nc.semaphore("g_" + n))

        w = sb("w", [P, IC, 2, C, P], F16)
        xn = [sb(f"xn{k}", [P, ST, C * P], F32) for k in range(2)]
        xi = [sb(f"xi{k}", [P, C, S], I16) for k in range(2)]
        xp = [sb(f"xp{k}", [P, 2, C, S], F16) for k in range(2)]
        stage = [sb(f"stage{k}", [P, PIECES, S], F32) for k in range(2)]
        top = sb("top", [P, 2 * CH], F32)
        bank = [ctx.enter_context(nc.psum_tensor(f"g_bank{k}", [P, S], F32)) for k in range(RING)]
        wraw = [sb(f"wraw{j}", [P, 2, 512], F32) for j in range(3)]
        wtop, winv = sb("wtop", [P, 3, NB], F32), sb("winv", [P, 3, NB], F32)
        wint = sb("wint", [P, 3, 2 * 512], I16)
        wdeq = [sb(f"wdeq{j}", [P, 2, 512], F32) for j in range(3)]
        ident = sb("ident", [P, P], F32)
        wbank = ctx.enter_context(nc.psum_tensor("g_wbank", [P, 2, 512], F32))
        s_w = [sem(f"w{c}") for c in range(CH)]
        s_id, s_wq, s_wt, s_whi, s_wlo = (sem(n) for n in ("id", "wquant", "wtransposed", "whi", "wlo"))
        s_wraw = [sem(f"wraw{j}") for j in range(3)]
        s_ready, s_max, s_sc = sem("ready"), sem("max"), sem("scalars")
        s_x = [sem(f"x{k}") for k in range(2)]
        s_xst = [sem(f"xst{k}") for k in range(2)]
        s_int, s_hi, s_lo = sem("int"), sem("hi"), sem("lo")
        s_full, s_evac, s_top, s_peak = sem("full"), sem("evac"), sem("top"), sem("peak")
        s_st = [sem(f"st{k}") for k in range(2)]
        growth = {s_int: 2, s_hi: 2, s_lo: 2, s_full: 2 * IC, s_evac: 2 * IC, s_top: 2 * CH, s_peak: 1,
                  s_wq: 15, s_wt: 3, s_whi: 6, s_wlo: 6, **{s: 32 for s in s_wraw},
                  **{s: 16 for s in s_x + s_xst}, **{s: 16 * CH for s in s_st}}
        s_past = {e: sem(f"past_{e}") for e in ("sp", "pool", "dve", "act")}

        with nc.Block() as block:
            @block.sync
            def _(sp):
                def sp_wait(*what):
                    wait(sp, *what, past=s_past["sp"])

                ints, lo, evac, wq = Count(s_int), Count(s_lo), Count(s_evac), Count(s_wq)

                def load_weights(j, tile):
                    for k in range(2):
                        sp.dma_start(wraw[j][:, k], wf[tile + k]).then_inc(s_wraw[j], 16)

                def load(k, t):
                    sp_wait(s_int, ints.value(1))
                    ints.up()
                    sp.dma_start(xn[k][:], xn2T[t]).then_inc(s_x[k], 16)

                load(0, 0)
                for c in range(CH):
                    pieces = slice(c * PIECES, (c + 1) * PIECES)
                    sp.dma_start(w[:, pieces].rearrange("p k a c n -> p k (a c n)"),
                                 wf_parts[pieces].rearrange("k p a n -> p k (a n)")).then_inc(s_w[c], 16)
                load(1, 1)
                for j in range(3):
                    load_weights(j, IC + 2 * j)

                def store_parts(k, t):
                    sp_wait(s_lo, lo.up())
                    sp.dma_start(x_int[t], xp[k][:]).then_inc(s_xst[k], 16)

                def turn(t, last):
                    for k in range(2):
                        for c in range(CH):
                            sp_wait(s_evac, evac.up(PIECES))
                            sp.dma_start(g_raw[t + k, c], stage[c % 2][:].rearrange("p a n -> p (a n)")
                                         ).then_inc(s_st[c % 2], 16)
                            if c == 0 and not last:
                                load(k, t + k + 2)
                            if c == 1 and not (last and k):
                                store_parts(1 - k, t + k + 1)
                            n = k * CH + c
                            if n - 1 in W_AT:
                                wq.up(5)
                                if not last:
                                    j = W_AT.index(n - 1)
                                    sp_wait(s_wq, wq.value(1))
                                    load_weights(j, t * 3 + (IC + 6 + 2 * j))

                store_parts(0, 0)
                tiles_in_pairs(sp, [ints, lo, evac, wq], growth, turn)
                for k in range(2):
                    sp.wait_ge(s_st[k], 16 * CH * T // 2)
                    sp.wait_ge(s_xst[k], 16 * T // 2)

            @block.gpsimd
            def _(pool):
                pool.memset(ident[:], 0.0).then_inc(s_id, 1)
                pool.wait_ge(s_id, 1)
                pool.affine_select(out=ident[:], in_=ident[:], compare_op=ALU.not_equal, fill=1.0, base=0,
                                   pattern=[[-1, P]], channel_multiplier=1).then_inc(s_id, 1)
                pool.wait_ge(s_ready, 1)
                pool.partition_all_reduce(table[:, X_MAX:X_MAX + 1], table[:, TOP:TOP + 1], P, RMAX).then_inc(s_max, 1)

            @block.scalar
            def _(act):
                ints, full, xst, st, tops = (Count(s_int), Count(s_full), [Count(s) for s in s_xst],
                                             [Count(s) for s in s_st], Count(s_top))

                def high(k):
                    wait(act, s_int, ints.up())
                    wait(act, full)
                    wait(act, xst[k])
                    xst[k].up(16)
                    act.activation(xp[k][:, 0], xi[k][:], ACT.Copy).then_inc(s_hi, 1)

                wt = Count(s_wt)

                def weights_high(t, j):
                    wait(act, s_wt, wt.up(), past=s_past["act"])
                    for k in range(2):
                        act.activation(w_next[:, t * 3 + (2 * j + k), 0].rearrange("p c n -> p (c n)"), wbank[:, k],
                                       ACT.Copy, scale=W_UP).then_inc(s_whi, 1)

                def turn(t, last):
                    for k in range(2):
                        for c in range(CH):
                            if c == 1 and not (last and k):
                                high(1 - k)
                            if k * CH + c in W_DONE:
                                weights_high(t, W_DONE.index(k * CH + c))
                            wait(act, st[c % 2])
                            wait(act, s_top, tops.value(1))
                            st[c % 2].up(16)
                            tops.up()
                            for j in range(PIECES):
                                wait(act, s_full, full.up())
                                act.activation(stage[c % 2][:, j], bank[(c * PIECES + j) % RING][:],
                                               ACT.Copy).then_inc(s_evac, 1)
                    weights_high(t, 2)

                high(0)
                tiles_in_pairs(act, [ints, full, *xst, *st, tops, wt], growth, turn)

            @block.vector
            def _(dve):
                sc = Scalars(dve, table, s_sc)
                x, hi, ints, evac, tops, peak, lo = ([Count(s) for s in s_x], Count(s_hi), Count(s_int), Count(s_evac),
                                                     Count(s_top), Count(s_peak), Count(s_lo))
                sc.after(dve.memset(peak_g[:], 0.0))
                dve.tensor_reduce(sc.col(TOP), peak_x[:], AXX, ALU.max).then_inc(s_ready, 1)
                dve.wait_ge(s_max, 1)
                sc.quantisation(X_MAX, None, X_S, X_INV)
                sc.after(dve.tensor_scalar(sc.col(X_UNIT), sc.col(X_S), 1.0 / W_UP, None, ALU.mult))

                def integers(k):
                    wait(dve, s_x[k], x[k].up(16))
                    wait(dve, s_lo, lo.value(1))
                    dve.tensor_scalar(xi[k][:].rearrange("p c (s n) -> p c s n", s=ST),
                                      xn[k][:].rearrange("p s (c n) -> p c s n", c=C),
                                      sc.col(X_INV), None, ALU.mult).then_inc(s_int, 1)
                    wait(dve, s_hi, hi.up())
                    dve.tensor_tensor(xp[k][:, 1], xi[k][:], xp[k][:, 0], ALU.subtract).then_inc(s_lo, 1)
                    lo.up()

                wq, wraw_in, whi, wlo = Count(s_wq), [Count(s) for s in s_wraw], Count(s_whi), Count(s_wlo)

                def weights(j):
                    wait(dve, s_wraw[j], wraw_in[j].up(32))
                    blocks = wraw[j][:].rearrange("p k (b c) -> p (k b) c", c=BLOCK)
                    dve.tensor_reduce(wtop[:, j], blocks, AXX, ALU.max, apply_absolute_value=True).then_inc(s_wq, 1)
                    wait(dve, s_wq, wq.up())
                    dve.tensor_scalar(wtop[:, j], wtop[:, j], 1.0 / QMAX_W, TINY, ALU.mult, ALU.max).then_inc(s_wq, 1)
                    wait(dve, s_wq, wq.up())
                    dve.reciprocal(winv[:, j], wtop[:, j]).then_inc(s_wq, 1)
                    wait(dve, s_wq, wq.up())
                    q = wint[:, j].rearrange("p (b c) -> p b c", c=BLOCK)
                    dve.tensor_tensor(q, blocks, winv[:, j].unsqueeze(2).to_broadcast([P, NB, BLOCK]),
                                      ALU.mult).then_inc(s_wq, 1)
                    wait(dve, s_wq, wq.up())
                    deq = wdeq[j][:].rearrange("p k (b c) -> p (k b) c", c=BLOCK)
                    dve.tensor_tensor(deq, q, wtop[:, j].unsqueeze(2).to_broadcast([P, NB, BLOCK]),
                                      ALU.mult).then_inc(s_wq, 1)
                    wq.up()

                def weights_low(t, j):
                    wait(dve, s_whi, whi.up(2))
                    for k in range(2):
                        hi_part, lo_part = (w_next[:, t * 3 + (2 * j + k), a].rearrange("p c n -> p (c n)") for a in range(2))
                        dve.scalar_tensor_tensor(lo_part, wbank[:, k], W_UP, hi_part,
                                                 ALU.mult, ALU.subtract).then_inc(s_wlo, 1)
                    wlo.up(2)

                def turn(t, last):
                    wait(dve, peak)
                    for k in range(2):
                        for c in range(CH):
                            if c == 1 and not (last and k):
                                integers(1 - k)
                            if k * CH + c in W_AT:
                                weights(W_AT.index(k * CH + c))
                            if k * CH + c in W_DONE:
                                weights_low(t, W_DONE.index(k * CH + c))
                            wait(dve, s_evac, evac.up(PIECES))
                            n = k * CH + c
                            dve.tensor_reduce(top[:, n:n + 1], stage[c % 2][:].rearrange("p a n -> p (a n)"), AXX,
                                              ALU.max, apply_absolute_value=True).then_inc(s_top, 1)
                            tops.up()
                    weights_low(t, 2)
                    wait(dve, tops)
                    dve.tensor_tensor(peak_g[:], peak_g[:], top[:], ALU.max).then_inc(s_peak, 1)
                    peak.up()

                integers(0)
                tiles_in_pairs(dve, [*x, hi, evac, tops, peak, lo, wq, *wraw_in, whi, wlo], growth, turn)
                wait(dve, peak)

            @block.tensor
            def _(pe):
                lo, evac, wq, wlo = Count(s_lo), Count(s_evac), Count(s_wq), Count(s_wlo)
                pe.wait_ge(s_id, 2)

                def transpose_weights(j):
                    wait(pe, s_wq, wq.up(5))
                    wait(pe, wlo)
                    wlo.up(2)
                    for k in range(2):
                        for c in range(C):
                            cols = slice(c * P, (c + 1) * P)
                            last = pe.transpose(wbank[:, k, cols], wdeq[j][:, k, cols], ident[:])
                    last.then_inc(s_wt, 1)

                def turn(t, last):
                    for k in range(2):
                        wait(pe, s_lo, lo.up())
                        for ic in range(IC):
                            if ic % PIECES == 0 and k * CH + ic // PIECES in W_DONE:
                                transpose_weights(W_DONE.index(k * CH + ic // PIECES))
                            if isinstance(t, int) and k == 0 and ic % PIECES == 0:
                                pe.wait_ge(s_w[ic // PIECES], 16)
                            evac.up()
                            wait(pe, s_evac, evac.value(RING))
                            three_pass_product(pe, bank[ic % RING][:], C, lambda a, c: w[:, ic, a, c],
                                               lambda z, c: xp[k][:, z, c]).then_inc(s_full, 1)
                    transpose_weights(2)

                tiles_in_pairs(pe, [lo, evac, wq, wlo], growth, turn)


def up_stage(nc, x_int, g_raw, u_raw, table, peak_g, peak_u, peak_f, gq, w):
    with ExitStack() as ctx:
        def sb(n, s, d):
            return ctx.enter_context(nc.sbuf_tensor("u_" + n, s, d))

        def sem(n):
            return ctx.enter_context(nc.semaphore("u_" + n))

        xp = [sb(f"xp{k}", [P, 2, C, S], F16) for k in range(2)]
        stage = [sb(f"stage{k}", [P, PIECES, S], F32) for k in range(2)]
        raw = [sb(f"raw{k}", [P, CW], F32) for k in range(2)]
        sig = [sb(f"sig{k}", [P, CW], F32) for k in range(2)]
        sigq = sb("sigq", [P, CW], U16)
        top = sb("top", [P, 2, 2 * CH], F32)
        bank = [ctx.enter_context(nc.psum_tensor(f"u_bank{k}", [P, S], F32)) for k in range(RING)]
        s_ready, s_max, s_sc, s_set = sem("ready"), sem("max"), sem("scalars"), sem("set")
        s_x = [sem(f"x{k}") for k in range(2)]
        s_g = [sem(f"g{k}") for k in range(2)]
        s_st = [sem(f"st{k}") for k in range(2)]
        s_full, s_evac, s_top, s_peak = sem("full"), sem("evac"), sem("top"), sem("peak")
        s_gq, s_sig, s_sigq, s_f, s_ftop = sem("gq"), sem("sig"), sem("sigq"), sem("f"), sem("ftop")
        growth = {s_full: 2 * IC, s_evac: 2 * IC, s_top: 2 * CH, s_peak: 2, s_gq: 2 * CH, s_sig: 2 * CH,
                  s_sigq: 2 * CH, s_f: 2 * CH, s_ftop: 2 * CH,
                  **{s: 16 for s in s_x}, **{s: 16 * CH for s in s_st + s_g}}
        s_past = {e: sem(f"past_{e}") for e in ("sp", "pool", "dve", "act")}

        with nc.Block() as block:
            @block.sync
            def _(sp):
                def sp_wait(*what):
                    wait(sp, *what, past=s_past["sp"])

                evac, gqc = Count(s_evac), Count(s_gq)

                def load_gate(t, c):
                    sp_wait(s_gq, gqc.value(1))
                    gqc.up()
                    sp.dma_start(raw[c % 2][:], g_raw[t, c]).then_inc(s_g[c % 2], 16)

                def turn(t, last):
                    for k in range(2):
                        for c in range(CH):
                            sp_wait(s_evac, evac.up(PIECES))
                            sp.dma_start(u_raw[t + k, c], stage[c % 2][:].rearrange("p a n -> p (a n)")
                                         ).then_inc(s_st[c % 2], 16)
                            if c == 0 and not (last and k):
                                sp.dma_start(xp[1 - k][:], x_int[t + k + 1]).then_inc(s_x[1 - k], 16)
                            if not (last and k and c + 2 >= CH):
                                load_gate(t + k + (c + 2) // CH, (c + 2) % CH)

                sp.dma_start(xp[0][:], x_int[0]).then_inc(s_x[0], 16)
                load_gate(0, 0)
                load_gate(0, 1)
                tiles_in_pairs(sp, [evac, gqc], growth, turn)
                for k in range(2):
                    sp.wait_ge(s_st[k], 16 * CH * T // 2)

            @block.gpsimd
            def _(pool):
                pool.wait_ge(s_ready, 1)
                pool.partition_all_reduce(table[:, G_MAX:G_MAX + 1], table[:, TOP:TOP + 1], P, RMAX).then_inc(s_max, 1)

            @block.scalar
            def _(act):
                full, tops, ftop, gqc = Count(s_full), Count(s_top), Count(s_ftop), Count(s_gq)
                st, g = [Count(s) for s in s_st], [Count(s) for s in s_g]
                act.wait_ge(s_set, 1)

                def turn(t, last):
                    for k in range(2):
                        for c in range(CH):
                            wait(act, st[c % 2])
                            wait(act, s_top, tops.value(1))
                            st[c % 2].up(16)
                            tops.up()
                            wait(act, s_g[c % 2], g[c % 2].up(16), past=s_past["act"])
                            ints = gq[:, t + k, c]
                            act.activation(ints, raw[c % 2][:], ACT.Copy,
                                           scale=table[:, G_INV:G_INV + 1]).then_inc(s_gq, 1)
                            for j in range(PIECES):
                                wait(act, s_full, full.up())
                                act.activation(stage[c % 2][:, j], bank[(c * PIECES + j) % RING][:],
                                               ACT.Copy).then_inc(s_evac, 1)
                            wait(act, s_gq, gqc.up())
                            wait(act, s_ftop, ftop.value(1), past=s_past["act"])
                            ftop.up()
                            act.activation(sig[c % 2][:], ints, ACT.Sigmoid,
                                           scale=table[:, G_S:G_S + 1]).then_inc(s_sig, 1)

                tiles_in_pairs(act, [full, tops, ftop, gqc, *st, *g], growth, turn)

            @block.vector
            def _(dve):
                sc = Scalars(dve, table, s_sc)
                evac, tops, peak, sigc, sigqc, f, ftop = (
                    Count(s) for s in (s_evac, s_top, s_peak, s_sig, s_sigq, s_f, s_ftop))
                sc.after(dve.memset(peak_u[:], 0.0))
                sc.after(dve.memset(peak_f[:], 0.0))
                dve.tensor_reduce(sc.col(TOP), peak_g[:], AXX, ALU.max).then_inc(s_ready, 1)
                dve.wait_ge(s_max, 1)
                sc.quantisation(G_MAX, X_UNIT, G_S, G_INV)
                dve.tensor_scalar(sc.col(F_UNIT), sc.col(G_S), 1.0 / 65536.0, None, ALU.mult).then_inc(s_set, 1)

                def turn(t, last):
                    wait(dve, peak)
                    for k in range(2):
                        for c in range(CH):
                            n = k * CH + c
                            wait(dve, s_evac, evac.up(PIECES))
                            dve.tensor_reduce(top[:, 0, n:n + 1], stage[c % 2][:].rearrange("p a n -> p (a n)"), AXX,
                                              ALU.max, apply_absolute_value=True).then_inc(s_top, 1)
                            tops.up()
                            wait(dve, s_sig, sigc.up())
                            wait(dve, f)
                            dve.tensor_scalar(sigq[:], sig[c % 2][:], 65536.0, None, ALU.mult).then_inc(s_sigq, 1)
                            wait(dve, s_sigq, sigqc.up())
                            dve.tensor_tensor(sig[c % 2][:], gq[:, t + k, c], sigq[:], ALU.mult).then_inc(s_f, 1)
                            wait(dve, s_f, f.up())
                            dve.tensor_reduce(top[:, 1, n:n + 1], sig[c % 2][:], AXX, ALU.max,
                                              apply_absolute_value=True).then_inc(s_ftop, 1)
                            ftop.up()
                    wait(dve, ftop)
                    dve.tensor_tensor(peak_u[:], peak_u[:], top[:, 0], ALU.max).then_inc(s_peak, 1)
                    dve.tensor_tensor(peak_f[:], peak_f[:], top[:, 1], ALU.max).then_inc(s_peak, 1)
                    peak.up(2)

                tiles_in_pairs(dve, [evac, tops, peak, sigc, sigqc, f, ftop], growth, turn)
                wait(dve, peak)

            @block.tensor
            def _(pe):
                x, evac = [Count(s) for s in s_x], Count(s_evac)

                def turn(t, last):
                    for k in range(2):
                        wait(pe, s_x[k], x[k].up(16))
                        for ic in range(IC):
                            evac.up()
                            wait(pe, s_evac, evac.value(RING))
                            three_pass_product(pe, bank[ic % RING][:], C, lambda a, c: w[:, ic, a, c],
                                               lambda z, c: xp[k][:, z, c]).then_inc(s_full, 1)

                tiles_in_pairs(pe, [*x, evac], growth, turn)


def peak_stage(nc, u_raw, table, peak_u, peak_f, peak_o, gq):
    with ExitStack() as ctx:
        def sb(n, s, d):
            return ctx.enter_context(nc.sbuf_tensor("p_" + n, s, d))

        def sem(n):
            return ctx.enter_context(nc.semaphore("p_" + n))

        sig = [sb(f"sig{k}", [P, CW], F32) for k in range(2)]
        sigq = [sb(f"sigq{k}", [P, CW], U16) for k in range(2)]
        raw = [sb(f"raw{k}", [P, CW], F32) for k in range(2)]
        uq = [sb(f"uq{k}", [P, CW], I16) for k in range(2)]
        prod = [sb(f"prod{k}", [P, CW], F32) for k in range(2)]
        top = sb("top", [P, 2 * CH], F32)
        s_ready, s_max, s_sc, s_set = sem("ready"), sem("max"), sem("scalars"), sem("set")
        s_u = [sem(f"u{k}") for k in range(2)]
        s_sig, s_sigq, s_f, s_fq, s_uq, s_o, s_top, s_peak = (
            sem(n) for n in ("sig", "sigq", "f", "fq", "uq", "o", "top", "peak"))
        growth = {**{s: 2 * CH for s in (s_sig, s_sigq, s_f, s_fq, s_uq, s_o, s_top)}, s_peak: 1,
                  **{s: 16 * CH for s in s_u}}
        s_past = {e: sem(f"past_{e}") for e in ("sp", "pool", "dve", "act")}

        with nc.Block() as block:
            @block.sync
            def _(sp):
                def sp_wait(*what):
                    wait(sp, *what, past=s_past["sp"])

                uqc = Count(s_uq)

                def turn(t, last):
                    for k in range(2):
                        for c in range(CH):
                            sp_wait(s_uq, uqc.value(1))
                            uqc.up()
                            sp.dma_start(raw[c % 2][:], u_raw[t + k, c]).then_inc(s_u[c % 2], 16)

                tiles_in_pairs(sp, [uqc], growth, turn)

            @block.gpsimd
            def _(pool):
                pool.wait_ge(s_ready, 1)
                pool.partition_all_reduce(table[:, U_MAX:U_MAX + 1], table[:, TOP:TOP + 1], P, RMAX).then_inc(s_max, 1)
                pool.wait_ge(s_ready, 2)
                pool.partition_all_reduce(table[:, F_MAX:F_MAX + 1], table[:, TOP:TOP + 1], P, RMAX).then_inc(s_max, 1)

            @block.scalar
            def _(act):
                f, fq, o, u, sigqc, sig_c = Count(s_f), Count(s_fq), Count(s_o), [Count(s) for s in s_u], Count(s_sigq), Count(s_sig)
                act.wait_ge(s_set, 1)

                def sigmoid(t, c):
                    wait(act, fq, past=s_past["act"])
                    act.activation(sig[c % 2][:], gq[:, t, c], ACT.Sigmoid,
                                   scale=table[:, G_S:G_S + 1]).then_inc(s_sig, 1)

                def up_integers(c):
                    wait(act, s_u[c % 2], u[c % 2].up(16))
                    wait(act, s_o, o.value(1))
                    o.up()
                    act.activation(uq[c % 2][:], raw[c % 2][:], ACT.Copy,
                                   scale=table[:, U_INV:U_INV + 1]).then_inc(s_uq, 1)

                def gate_integers(t, c):
                    wait(act, s_f, f.up(), past=s_past["act"])
                    act.activation(gq[:, t, c], sig[c % 2][:], ACT.Copy,
                                   scale=table[:, F_INV:F_INV + 1]).then_inc(s_fq, 1)
                    fq.up()

                def turn(t, last):
                    for n in range(2 * CH):
                        if not last or n < 2 * CH - 1:
                            sigmoid(t + (n + 1) // CH, (n + 1) % CH)
                        gate_integers(t + n // CH, n % CH)
                        up_integers(n % CH)

                sigmoid(0, 0)
                tiles_in_pairs(act, [f, fq, o, *u], growth, turn)

            @block.vector
            def _(dve):
                sc = Scalars(dve, table, s_sc)
                sc.after(dve.memset(peak_o[:], 0.0))
                dve.tensor_reduce(sc.col(TOP), peak_u[:], AXX, ALU.max).then_inc(s_ready, 1)
                dve.wait_ge(s_max, 1)
                sc.quantisation(U_MAX, X_UNIT, U_S, U_INV)
                dve.tensor_reduce(sc.col(TOP), peak_f[:], AXX, ALU.max).then_inc(s_ready, 1)
                dve.wait_ge(s_max, 2)
                sc.quantisation(F_MAX, F_UNIT, F_S, F_INV)
                dve.tensor_tensor(sc.col(O_UNIT), sc.col(F_S), sc.col(U_S), ALU.mult).then_inc(s_set, 1)
                sigc, f, fq, uqc, o, tops, peak, sigqc = (
                    Count(s) for s in (s_sig, s_f, s_fq, s_uq, s_o, s_top, s_peak, s_sigq))

                def gate(t, c):
                    wait(dve, s_sig, sigc.up())
                    wait(dve, s_f, f.value(1))
                    dve.tensor_scalar(sigq[c % 2][:], sig[c % 2][:], 65536.0, None, ALU.mult).then_inc(s_sigq, 1)

                def gate_product(t, c):
                    wait(dve, s_sigq, sigqc.up())
                    dve.tensor_tensor(sig[c % 2][:], gq[:, t, c], sigq[c % 2][:], ALU.mult).then_inc(s_f, 1)
                    f.up()

                def product(t, c):
                    wait(dve, s_fq, fq.up())
                    wait(dve, s_uq, uqc.up())
                    wait(dve, s_top, tops.value(1))
                    dve.tensor_tensor(prod[c % 2][:], gq[:, t, c], uq[c % 2][:], ALU.mult).then_inc(s_o, 1)

                def largest(n):
                    wait(dve, s_o, o.up())
                    dve.tensor_reduce(top[:, n:n + 1], prod[n % 2][:], AXX, ALU.max,
                                      apply_absolute_value=True).then_inc(s_top, 1)
                    tops.up()

                def turn(t, last):
                    wait(dve, peak)
                    for n in range(2 * CH):
                        ahead = not last or n < 2 * CH - 1
                        here, then = (t + n // CH, n % CH), (t + (n + 1) // CH, (n + 1) % CH)
                        if ahead:
                            gate(*then)
                        product(*here)
                        if ahead:
                            gate_product(*then)
                        largest(n)
                    wait(dve, tops)
                    dve.tensor_tensor(peak_o[:], peak_o[:], top[:], ALU.max).then_inc(s_peak, 1)
                    peak.up()

                gate(0, 0)
                gate_product(0, 0)
                tiles_in_pairs(dve, [sigc, f, fq, uqc, o, tops, peak, sigqc], growth, turn)
                wait(dve, peak)


def down_stage(nc, u_raw, x1, out, table, peak_o, gq, w):
    with ExitStack() as ctx:
        def sb(n, s, d):
            return ctx.enter_context(nc.sbuf_tensor("d_" + n, s, d))

        def sem(n):
            return ctx.enter_context(nc.semaphore("d_" + n))

        raw = [sb(f"raw{k}", [P, CW], F32) for k in range(2)]
        uq = [sb(f"uq{k}", [P, CW], I16) for k in range(2)]
        oi = [sb(f"oi{k}", [P, CW], I16) for k in range(2)]
        op = sb("op", [P, CH, 2, PIECES, S], F16)
        res = [sb(f"res{k}", [P, E], F32) for k in range(2)]
        bank = [ctx.enter_context(nc.psum_tensor(f"d_bank{k}", [P, E], F32)) for k in range(8)]
        s_ready, s_max, s_sc, s_set = sem("ready"), sem("max"), sem("scalars"), sem("set")
        s_u = [sem(f"u{k}") for k in range(2)]
        s_r = [sem(f"r{k}") for k in range(2)]
        s_out = [sem(f"out{k}") for k in range(2)]
        s_uq, s_oi, s_hi, s_lo, s_pass, s_full, s_y = (sem(n) for n in ("uq", "oi", "hi", "lo", "pass", "full", "y"))
        growth = {**{s: 2 * CH for s in (s_uq, s_oi, s_hi, s_lo)}, s_pass: 2 * (CH - 1), s_full: 2 * ST, s_y: 2 * ST,
                  **{s: 16 * CH for s in s_u}, **{s: 16 * ST for s in s_r + s_out}}
        s_past = {e: sem(f"past_{e}") for e in ("sp", "pool", "dve", "act")}

        with nc.Block() as block:
            @block.sync
            def _(sp):
                def sp_wait(*what):
                    wait(sp, *what, past=s_past["sp"])

                uqc, y = Count(s_uq), Count(s_y)
                out_c = [Count(s) for s in s_out]

                def load(t, c):
                    sp_wait(s_uq, uqc.value(1))
                    uqc.up()
                    sp.dma_start(raw[c % 2][:], u_raw[t, c]).then_inc(s_u[c % 2], 16)

                def chunks(t, last_tile):
                    for c in range(CH):
                        if not (last_tile and c == CH - 1):
                            load(t + (c + 1) // CH, (c + 1) % CH)

                def rows(t):
                    for st in range(ST):
                        sp_wait(out_c[st % 2])
                        out_c[st % 2].up(16)
                        sp.dma_start(res[st % 2][:], x1[t, st * P:(st + 1) * P, :]).then_inc(s_r[st % 2], 16)
                        sp_wait(s_y, y.up())
                        sp.dma_start(out[t, st * P:(st + 1) * P, :], res[st % 2][:]).then_inc(s_out[st % 2], 16)

                def turn(t, last):
                    for k in range(2):
                        if not (last and k):
                            chunks(t + k + 1, last)
                        rows(t + k)

                load(0, 0)
                chunks(0, False)
                tiles_in_pairs(sp, [uqc, y, *out_c], growth, turn)
                for c in out_c:
                    sp_wait(c)

            @block.gpsimd
            def _(pool):
                pool.wait_ge(s_ready, 1)
                pool.partition_all_reduce(table[:, O_MAX:O_MAX + 1], table[:, TOP:TOP + 1], P, RMAX).then_inc(s_max, 1)

            @block.scalar
            def _(act):
                u, oi_c, passed, full = [Count(s) for s in s_u], Count(s_oi), Count(s_pass), Count(s_full)

                def up_integers(c):
                    wait(act, s_u[c % 2], u[c % 2].up(16))
                    wait(act, oi_c)
                    act.activation(uq[c % 2][:], raw[c % 2][:], ACT.Copy,
                                   scale=table[:, U_INV:U_INV + 1]).then_inc(s_uq, 1)

                def high(c):
                    wait(act, s_oi, oi_c.up())
                    if c < CH - 1:
                        wait(act, s_pass, passed.value(CH - 2))
                        passed.up()
                    else:
                        wait(act, full)
                        full.up(ST)
                    act.activation(op[:, c, 0].rearrange("p a n -> p (a n)"), oi[c % 2][:], ACT.Copy).then_inc(s_hi, 1)

                def turn(t, last):
                    for k in range(2):
                        for c in range(CH):
                            if not (last and k and c == CH - 1):
                                up_integers((c + 1) % CH)
                            high(c)

                up_integers(0)
                tiles_in_pairs(act, [*u, oi_c, passed, full], growth, turn)

            @block.vector
            def _(dve):
                sc = Scalars(dve, table, s_sc)
                dve.tensor_reduce(sc.col(TOP), peak_o[:], AXX, ALU.max).then_inc(s_ready, 1)
                dve.wait_ge(s_max, 1)
                sc.quantisation(O_MAX, O_UNIT, O_S, O_MUL)
                sc.after(dve.tensor_scalar(sc.col(O_S), sc.col(O_S), 1.0 / W_UP, None, ALU.mult))
                uqc, hi, lo, full, r, y = (Count(s_uq), Count(s_hi), Count(s_lo), Count(s_full),
                                           [Count(s) for s in s_r], Count(s_y))

                def integers(t, c):
                    wait(dve, s_uq, uqc.up())
                    wait(dve, lo)
                    dve.scalar_tensor_tensor(oi[c % 2][:], gq[:, t, c], sc.col(O_MUL), uq[c % 2][:],
                                             ALU.mult, ALU.mult).then_inc(s_oi, 1)

                def chunks(t, last_tile):
                    for c in range(CH):
                        if not (last_tile and c == CH - 1):
                            integers(t + (c + 1) // CH, (c + 1) % CH)
                        wait(dve, s_hi, hi.up())
                        dve.tensor_tensor(op[:, c, 1].rearrange("p a n -> p (a n)"), oi[c % 2][:],
                                          op[:, c, 0].rearrange("p a n -> p (a n)"), ALU.subtract).then_inc(s_lo, 1)
                        lo.up()

                def rows(t):
                    for st in range(ST):
                        wait(dve, s_full, full.up())
                        wait(dve, s_r[st % 2], r[st % 2].up(16))
                        dve.scalar_tensor_tensor(res[st % 2][:], bank[(full.n - 1) % 8][:], sc.col(O_S),
                                                 res[st % 2][:], ALU.mult, ALU.add).then_inc(s_y, 1)
                        y.up()

                def turn(t, last):
                    for k in range(2):
                        if not (last and k):
                            chunks(t + k + 1, last)
                        rows(t + k)

                integers(0, 0)
                chunks(0, False)
                tiles_in_pairs(dve, [uqc, hi, lo, full, *r, y], growth, turn)

            @block.tensor
            def _(pe):
                lo, y = Count(s_lo), Count(s_y)

                def turn(t, last):
                    for k in range(2):
                        banks = [bank[k * ST + st] for st in range(ST)]
                        wait(pe, s_y, y.value(ST))
                        y.up(ST)
                        for c in range(CH):
                            wait(pe, s_lo, lo.up())
                            for st in range(ST):
                                cols = slice(st * P, (st + 1) * P)
                                for j in range(PIECES):
                                    ic = c * PIECES + j
                                    rows_of = slice(ic // C * C, ic // C * C + C)
                                    for a, z in ((0, 0), (0, 1), (1, 0)):
                                        last = pe.matmul(banks[st][:].rearrange("p (r n) -> p r n", r=C),
                                                         op[:, c, a, j, cols], w[:, rows_of, z, ic % C, :],
                                                         start=(c, j, a, z) == (0, 0, 0, 0),
                                                         stop=(c, j, a) == (CH - 1, PIECES - 1, 1))
                                if c == CH - 1:
                                    last.then_inc(s_full, 1)
                                elif st == ST - 1:
                                    last.then_inc(s_pass, 1)

                tiles_in_pairs(pe, [lo, y], growth, turn)


def block_program(nc, x, ctxT, wf, attn_w, b_qkv, b_o, rope, out):
    def scratch(name, shape, dtype):
        return nc.dram_tensor("scratch_" + name, shape, dtype, kind="Internal").ap()

    wf_parts = scratch("wf_parts", [IC, P, 2, 512], F16)
    wa_parts = scratch("wa_parts", [4, P, 2, C, E], F16)
    x1 = scratch("x1", [B, S, E], F32)
    xn2T = scratch("xn2T", [B, P, ST, C * P], F32)
    x_int = scratch("x_int", [T, P, 2, C, S], F16)
    g_raw = scratch("g_raw", [T, CH, P, CW], F32)
    u_raw = scratch("u_raw", [T, CH, P, CW], F32)
    with ExitStack() as ctx:
        def sb(name, shape, dtype):
            return ctx.enter_context(nc.sbuf_tensor(name, shape, dtype))

        peak_x = sb("peak_x", [P, ST], F32)
        weight_stage(nc, wf[0:IC].rearrange("(n k) p c -> n k p c", k=2), attn_w,
                     wf_parts.rearrange("(n k) p a c -> n k p a c", k=2), wa_parts)
        attention_stage(nc, x, ctxT, wa_parts, [b_qkv[0], b_qkv[1], b_qkv[2], b_o], rope, x1, xn2T, peak_x)
        table = sb("scalars", [P, N_SCALARS], F32)
        peak_g, peak_u, peak_f, peak_o = (sb(f"peak_{n}", [P, 2 * CH], F32) for n in "gufo")
        w_next = sb("w_up_down", [P, 2 * IC, 2, C, P], F16)
        gate_stage(nc, wf, wf_parts, xn2T, x_int, g_raw, table, peak_x, peak_g, w_next)
        gq = sb("gq", [P, T, CH, CW], I16)
        up_stage(nc, x_int, g_raw, u_raw, table, peak_g, peak_u, peak_f, gq, w_next[:, 0:IC])
        peak_stage(nc, u_raw, table, peak_u, peak_f, peak_o, gq)
        down_stage(nc, u_raw, x1, out, table, peak_o, gq, w_next[:, IC:2 * IC])


def rope_tables():
    inv = (np.float32(1.0) / np.float32(10000.0) ** (np.arange(0, D, 2, dtype=np.float32) / np.float32(D))).astype(np.float32)
    angle = inv[:, None] * np.arange(S, dtype=np.float32)[None, :]
    cos, sin = np.cos(angle), np.sin(angle)
    return np.stack([np.tile(cos, (2 * HG, 1)), np.tile(np.concatenate([-sin, sin]), (HG, 1))]).astype(np.float32)


def kernel(**inputs):
    import concourse.bacc as bacc
    from concourse.bass_utils import run_bass_kernel_spmd

    a = {k: np.asarray(v) for k, v in inputs.items()}
    down = a["L0_ffn_w_down"].reshape(C, P, IC // C, 512).transpose(2, 0, 1, 3).reshape(IC, P, 512)
    arrays = {
        "in_x": a["x"],
        "in_ctxT": a["ctx_1024"].transpose(0, 2, 1),
        "in_wf": np.concatenate([a["L0_ffn_w_gate"].reshape(IC, P, E), a["L0_ffn_w_up"].reshape(IC, P, E), down]),
        "in_attn_w": np.stack([a[f"L0_xattn_W{m}"].T.reshape(C, P, E).transpose(1, 0, 2) for m in "qkvo"]),
        "in_b_qkv": np.stack([a[f"L0_xattn_b{m}"].reshape(C, P).T for m in "qkv"]),
        "in_b_o": np.broadcast_to(a["L0_xattn_bo"], (P, E)),
        "in_rope": rope_tables(),
    }
    arrays = {k: np.ascontiguousarray(v) for k, v in arrays.items()}
    nc = bacc.Bacc("TRN2", target_bir_lowering=False, num_devices=1)
    args = [nc.dram_tensor(k, v.shape, mybir.dt.from_np(v.dtype), kind="ExternalInput").ap() for k, v in arrays.items()]
    out = nc.dram_tensor("out", (B, S, E), F32, kind="ExternalOutput").ap()
    block_program(nc, *args, out)
    result = run_bass_kernel_spmd(nc, [arrays], core_ids=[0])
    return result.results[0]["out"]
```

```python
from contextlib import ExitStack

import concourse.bass as bass
import numpy as np
from concourse import mybir
from concourse.alu_op_type import AluOpType as ALU

F32, F16, BF16 = mybir.dt.float32, mybir.dt.float16, mybir.dt.bfloat16
I16, U16 = mybir.dt.int16, mybir.dt.uint16
ACT = mybir.ActivationFunctionType
AXX = mybir.AxisListType.X

P = 128
B, S, E = 8, 512, 512
H, D = 16, 32
I = 1536
C = E // P
ST = S // P
HG = P // D
IC = I // P
BLOCK = 32
EPS = 1e-5
TINY = 1e-12
QMAX_W, QMAX_A = 7.0, 32767.0

X_UP = 16.0
W_UP = 256.0
QK_UP = 8.0
PROJ_DOWN = 1.0 / (X_UP * W_UP)
M_DOWN = 64.0
EXP_SCALE = 1.0 / (float(np.sqrt(D)) * QK_UP * QK_UP)
MASKED = -float(2.0 ** 100)
ROLE_Q = ("hi", "lo", "hi")
ROLE_K = ("hi", "hi", "lo")
KROWS = 3 * D
MROWS = KROWS + 2

PAIRS_LOOPED = 2


class Count:

    def __init__(self, sem):
        self.sem, self.n, self.turn, self.growth = sem, 0, None, 0

    def value(self, back=0):
        assert self.turn is None or self.n > back
        return self.n - back if self.turn is None else self.turn * self.growth + (self.n - back)

    def up(self, k=1):
        self.n += k
        return self.value()

    def enter(self, turn, growth):
        self.turn, self.growth, self.entered = turn, growth, self.n

    def leave(self, turns):
        assert self.n - self.entered == self.growth, (self.sem, self.n - self.entered, self.growth)
        self.turn, self.n = None, self.n + (turns - 1) * self.growth


def wait(eng, count_or_sem, value=None, past=None):
    sem = count_or_sem.sem if isinstance(count_or_sem, Count) else count_or_sem
    if value is None:
        value = count_or_sem.value()
    if not isinstance(value, int) or value > 0:
        eng.wait_ge(sem, value)
        if past and not isinstance(value, int):
            eng.sem_inc(past, 1)


class Batch:

    def __init__(self, c, turn=None):
        self.c, self.turn, self.par = c, turn, c % 2

    def index(self):
        return self.c if self.turn is None else self.turn * 2 + self.c

    def step(self, k):
        return Batch(self.c + k, self.turn)


def weight_stage(nc, wf, attn_w, wf_parts, W):
    N = IC // 2
    NB = 2 * 512 // BLOCK
    with ExitStack() as ctx:
        def sb(n, s, d):
            return ctx.enter_context(nc.sbuf_tensor("w_" + n, s, d))

        raw = [sb(f"raw{k}", [P, 2, 512], F32) for k in range(2)]
        top = sb("top", [P, 2, NB], F32)
        inv = sb("inv", [P, 2, NB], F32)
        ints = sb("ints", [P, 2, 2 * 512], I16)
        deq = [sb(f"deq{k}", [P, 2, 512], F32) for k in range(2)]
        parts = [sb(f"parts{k}", [P, 2, 2, 512], F16) for k in range(2)]
        ident = sb("ident", [P, P], F32)
        aw = [sb(f"aw{k}", [P, C, E], F32) for k in range(2)]
        bank = [ctx.enter_context(nc.psum_tensor(f"w_bank{k}", [P, 2, 512], F32)) for k in range(2)]

        def sem(n):
            return ctx.enter_context(nc.semaphore("w_" + n))

        s_in = [sem(f"in{k}") for k in range(2)]
        s_out = [sem(f"out{k}") for k in range(2)]
        s_q = sem("quant")
        s_t = sem("transposed")
        s_hi = sem("hi")
        s_lo = sem("lo")
        s_ain = [sem(f"ain{k}") for k in range(2)]
        s_ahi, s_alo = sem("ahi"), sem("alo")
        s_id = sem("id")

        with nc.Block() as block:
            @block.sync
            def _(sp):
                def load(k, n):
                    sp.dma_start(raw[k][:], wf[n].rearrange("k p c -> p k c")).then_inc(s_in[k], 16)

                def store(k, n):
                    sp.wait_ge(s_lo, n + 1)
                    sp.dma_start(wf_parts[n].rearrange("k p a c -> p k a c"), parts[k][:]).then_inc(s_out[k], 16)

                for m in range(4):
                    k = m % 2
                    if m >= 2:
                        sp.wait_ge(s_alo, m - 1)
                    sp.dma_start(aw[k][:], attn_w[m]).then_inc(s_ain[k], 16)
                load(0, 0)
                load(1, 1)
                with sp.Fori(0, N // 2 - 1) as i:
                    for k in range(2):
                        n = i * 2 + k
                        sp.wait_ge(s_q, n * 5 + 4)
                        load(k, n + 2)
                        store(k, n)
                for k in range(2):
                    store(k, N - 2 + k)
                for k in range(2):
                    sp.wait_ge(s_out[k], 16 * (N // 2))

            @block.gpsimd
            def _(pool):
                pool.memset(ident[:], 0.0).then_inc(s_id, 1)
                pool.wait_ge(s_id, 1)
                pool.affine_select(out=ident[:], in_=ident[:], compare_op=ALU.not_equal, fill=1.0, base=0,
                                   pattern=[[-1, P]], channel_multiplier=1).then_inc(s_id, 1)

            @block.scalar
            def _(act):
                for m in range(4):
                    act.wait_ge(s_ain[m % 2], 16 * (m // 2 + 1))
                    act.activation(W[m][:, 0], aw[m % 2][:], ACT.Copy, scale=W_UP).then_inc(s_ahi, 1)

                def pair(k, n, first):
                    act.wait_ge(s_t, n + 1)
                    if not first:
                        act.wait_ge(s_out[k], n * 8 - k * 8)
                    act.activation(parts[k][:, :, 0], bank[k][:], ACT.Copy, scale=W_UP).then_inc(s_hi, 1)

                pair(0, 0, True)
                pair(1, 1, True)
                with act.Fori(1, N // 2) as i:
                    for k in range(2):
                        pair(k, i * 2 + k, False)

            @block.vector
            def _(dve):
                for m in range(4):
                    dve.wait_ge(s_ahi, m + 1)
                    dve.scalar_tensor_tensor(W[m][:, 1], aw[m % 2][:], W_UP, W[m][:, 0],
                                             ALU.mult, ALU.subtract).then_inc(s_alo, 1)

                def quantise(k, n):
                    dve.wait_ge(s_in[k], n * 8 - k * 8 + 16)
                    blocks = raw[k][:].rearrange("p k (b c) -> p (k b) c", c=BLOCK)
                    dve.tensor_reduce(top[:, k], blocks, AXX, ALU.max, apply_absolute_value=True).then_inc(s_q, 1)
                    dve.wait_ge(s_q, n * 5 + 1)
                    dve.tensor_scalar(top[:, k], top[:, k], 1.0 / QMAX_W, TINY, ALU.mult, ALU.max).then_inc(s_q, 1)
                    dve.wait_ge(s_q, n * 5 + 2)
                    dve.reciprocal(inv[:, k], top[:, k]).then_inc(s_q, 1)
                    dve.wait_ge(s_q, n * 5 + 3)
                    q = ints[:, k].rearrange("p (b c) -> p b c", c=BLOCK)
                    dve.tensor_tensor(q, blocks, inv[:, k].unsqueeze(2).to_broadcast([P, NB, BLOCK]),
                                      ALU.mult).then_inc(s_q, 1)
                    dve.wait_ge(s_q, n * 5 + 4)
                    w = deq[k][:].rearrange("p k (b c) -> p (k b) c", c=BLOCK)
                    dve.tensor_tensor(w, q, top[:, k].unsqueeze(2).to_broadcast([P, NB, BLOCK]),
                                      ALU.mult).then_inc(s_q, 1)

                def low(k, n):
                    dve.wait_ge(s_hi, n + 1)
                    dve.scalar_tensor_tensor(parts[k][:, :, 1], bank[k][:], W_UP, parts[k][:, :, 0],
                                             ALU.mult, ALU.subtract).then_inc(s_lo, 1)

                quantise(0, 0)
                quantise(1, 1)
                low(0, 0)
                with dve.Fori(1, N // 2) as i:
                    quantise(0, i * 2)
                    low(1, i * 2 - 1)
                    quantise(1, i * 2 + 1)
                    low(0, i * 2)
                low(1, N - 1)

            @block.tensor
            def _(pe):
                pe.wait_ge(s_id, 2)

                def pair(k, n, first):
                    pe.wait_ge(s_q, n * 5 + 5)
                    if not first:
                        pe.wait_ge(s_lo, n - 1)
                    for t in range(2):
                        for c in range(C):
                            cols = slice(c * P, (c + 1) * P)
                            last = pe.transpose(bank[k][:, t, cols], deq[k][:, t, cols], ident[:])
                    last.then_inc(s_t, 1)

                pair(0, 0, True)
                pair(1, 1, True)
                with pe.Fori(1, N // 2) as i:
                    for k in range(2):
                        pair(k, i * 2 + k, False)


def attention_stage(nc, x, ctxT, weights, biases, rope, x1, xn2T, peak):
    with ExitStack() as ctx:
        def sb(n, s, d):
            return ctx.enter_context(nc.sbuf_tensor("a_" + n, s, d))

        def sem(n):
            return ctx.enter_context(nc.semaphore("a_" + n))

        W = dict(zip("qkvo", weights))
        b_q, b_k, b_v = (sb("b" + m, [P, C], F32) for m in "qkv")
        b_o = sb("bo", [P, E], F32)
        cos, sin = sb("cos", [P, S], F32), sb("sin", [P, S], F32)
        xt = sb("xt", [P, ST, E], F32)
        ct = sb("ct", [P, C, S], F32)
        sum1 = [ct[:, k] for k in range(2)]
        resid = [ct[:, 2 + k] for k in range(2)]
        xp = sb("xp", [P, 2, C, S], F16)
        cp = sb("cp", [P, 2, C, S], F16)
        tmp = sb("tmp", [P, 4, S], F32)
        rot = sb("rot", [P, 2, S], F32)
        qkp = sb("qkp", [P, 2, C, S], F16)
        qs = [sb(f"qs{k}", [P, C, HG, S], F16) for k in range(2)]
        ks = [sb(f"ks{k}", [P, C, HG, S], F16) for k in range(2)]
        v = sb("v", [P, ST, E], F32)
        pt = sb("pt", [P, 10, S], F32)
        rden, att = sb("rden", [P, S], F32), sb("att", [P, S], F32)
        aop = [sb(f"aop{k}", [P, 2, C, S], F16) for k in range(2)]
        mx = sb("mx", [P, ST, HG], F32)
        mp = sb("mp", [P, ST, 2, HG], F16)
        mrow = sb("mrow", [2 * HG, S], F16)
        stats, mv = sb("stats", [P, ST, 6], F32), sb("mv", [P, ST, 2], F32)
        rstd, power = sb("rstd", [P, ST], F32), sb("power", [P, ST], F32)
        stats2, mv2, rstd2 = sb("stats2", [P, ST, 6], F32), sb("mv2", [P, ST, 2], F32), sb("rstd2", [P, ST], F32)
        peak_b = sb("peakb", [P, ST], F32)
        ident = sb("ident", [P, P], F32)
        ident16, identb = sb("ident16", [P, P], F16), sb("identb", [P, P], BF16)
        mask_s, mask_t = sb("mask_s", [P, P], BF16), sb("mask_t", [P, P], BF16)
        ones = sb("ones", [P, D], F32)

        def ps(n, d=F32):
            return ctx.enter_context(nc.psum_tensor("a_" + n, [P, 512], d))

        proj = [ps(f"proj{k}") for k in range(2)]
        sc = [ps(f"sc{k}") for k in range(2)]
        sct = [ps(f"sct{k}") for k in range(2)]
        ps_o, ps_d = ps("o"), ps("d")

        s_const = sem("const")
        s_w, TABLES = sem("tables"), 6 * 16
        s_dc, s_rows = sem("dve_const"), sem("ks_rows")
        s_x, s_c = sem("x_in"), sem("c_in")
        s_ln = sem("ln_stats")
        s_rstd = sem("ln_rstd")
        s_xn = sem("xn")
        s_chi, s_clo = sem("c_hi"), sem("c_lo")
        s_full = sem("proj_full")
        s_evac = sem("proj_evac")
        s_rot = sem("rotated")
        s_cos, s_mul = sem("times_cos"), sem("rot_times_sin")
        s_sum = sem("rope_sum")
        s_hi, s_lo = sem("hi"), sem("lo")
        s_kst, s_qst = sem("k_stacked"), sem("q_stacked")
        s_sfull, s_sread = sem("sc_full"), sem("sc_read")
        s_m = sem("m_parts")
        s_min = sem("m_placed")
        s_tfull, s_exp = sem("sct_full"), sem("exp")
        s_pv, s_pvread, s_norm = sem("pv"), sem("pv_read"), sem("norm")
        s_aohi, s_aolo = sem("ao_hi"), sem("ao_lo")
        s_res, s_resb = [sem(f"resid_in{k}") for k in range(2)], sem("resid_bias")
        s_x1, s_ln2, s_rstd2, s_xn2, s_peak = sem("x1"), sem("ln2_stats"), sem("ln2_rstd"), sem("xn2"), sem("peak")
        s_x1out = [sem(f"x1_out{k}") for k in range(2)]
        s_xn2out = sem("xn2_out")

        growth = {
            s_x: 32, s_c: 32, s_ln: 16, s_rstd: 4, s_xn: 8, s_chi: 2, s_clo: 2, s_full: 48, s_evac: 48,
            s_rot: 16, s_cos: 16, s_mul: 16, s_sum: 16, s_hi: 24, s_lo: 24, s_kst: 384, s_qst: 384,
            s_sfull: 88, s_sread: 88, s_m: 16, s_min: 256, s_tfull: 80, s_exp: 80, s_pv: 8, s_pvread: 16,
            s_norm: 16, s_aohi: 8, s_aolo: 8, s_res[0]: 64, s_res[1]: 64, s_resb: 8, s_x1: 8, s_ln2: 16, s_rstd2: 16,
            s_xn2: 8, s_peak: 10, s_x1out[0]: 64, s_x1out[1]: 64, s_xn2out: 32,
        }

        def run(eng, counts, turn):
            turn(Batch(-2), False, False)
            turn(Batch(-1), False, True)
            turn(Batch(0), False, True)
            turn(Batch(1), True, True)
            with eng.Fori(0, PAIRS_LOOPED) as i:
                for c in counts:
                    c.enter(i, growth[c.sem])
                turn(Batch(2, i), True, True)
                turn(Batch(3, i), True, True)
            for c in counts:
                c.leave(PAIRS_LOOPED)
            turn(Batch(6), True, True)
            turn(Batch(7), True, False)
            turn(Batch(8), True, False)

        def order(b, has_prev, has_next):
            here, n, p, nn = 0 <= b.c < B, b.step(1), b.step(-1), b.step(2)
            has_next_but_one = b.turn is not None or b.c + 2 < B
            for step in (
                ("exp", b, 0, 0), ("scores", b, 1, 0), ("exp", b, 0, 1), ("scores", b, 1, 1), ("c_high", n),
                ("exp", b, 0, 2), ("scores", b, 1, 2), ("scores", b, 1, 3), ("x", n), ("exp", b, 0, 3),
                ("c_low", n), ("exp", b, 0, 4), ("scores", b, 1, 4), ("out", p, 0), ("rows", b, 1),
                ("out", p, 1), ("pv", b, 0), ("exp", b, 1, 0), ("scores", b, 2, 0), ("out", p, 2),
                ("exp", b, 1, 1), ("scores", b, 2, 1), ("out", p, 3), ("exp", b, 1, 2), ("scores", b, 2, 2),
                ("out_end", p), ("k", n, 0), ("k", n, 1), ("k", n, 2), ("scores", b, 2, 3), ("exp", b, 1, 3),
                ("exp", b, 1, 4), ("scores", b, 2, 4), ("rows", b, 2), ("ao_norm", b, 0), ("ao_parts", b, 0),
                ("pv", b, 1), ("exp", b, 2, 0), ("scores", b, 3, 0), ("exp", b, 2, 1), ("scores", b, 3, 1),
                ("k", n, 3), ("exp", b, 2, 2), ("k_end", n), ("q", n, 0), ("scores", b, 3, 2), ("xn2", p),
                ("exp", b, 2, 3), ("scores", b, 3, 3), ("exp", b, 2, 4), ("scores", b, 3, 4), ("q", n, 1),
                ("rows", b, 3), ("ao_norm", b, 1), ("load", nn), ("ao_parts", b, 1), ("q", n, 2),
                ("pv", b, 2), ("exp", b, 3, 0), ("ao_norm", b, 2), ("q", n, 3), ("exp", b, 3, 1),
                ("exp", b, 3, 2), ("ao_parts", b, 2), ("exp", b, 3, 3), ("exp", b, 3, 4), ("q_end", n),
                ("norm_x", nn), ("pv", b, 3), ("v", n, 0), ("v", n, 1), ("ao_norm", b, 3),
                ("scores", n, 0, 0), ("scores", n, 0, 1), ("ao_parts", b, 3), ("scores", n, 0, 2),
                ("v", n, 2), ("scores", n, 0, 3), ("scores", n, 0, 4), ("rows", n, 0), ("v", n, 3),
            ):
                if (step[1] is b and here or step[1] is n and has_next or step[1] is p and has_prev
                        or step[1] is nn and has_next_but_one):
                    yield step

        def heads_blocks(pair, transposed):
            a, z = 2 * pair, 2 * pair + 1
            if transposed:
                return [[(a, 0, 0)], [(a, 1, 0), (a, 3, 384)], [(z, 0, 0)], [(z, 1, 0), (z, 3, 384)],
                        [(a, 2, 0), (z, 2, 256)]]
            return [[(a, 3, 0)], [(a, 2, 0), (a, 0, 384)], [(z, 3, 0)], [(z, 2, 0), (z, 0, 384)],
                    [(a, 1, 0), (z, 1, 256)]]

        def two_units(i, transposed):
            return [(u, heads_blocks(u // 5, transposed)[u % 5]) for u in (2 * i, 2 * i + 1)]

        def stack(sp, dst, src, roles, s):
            for j in range(HG):
                for r, role in enumerate(roles):
                    sp.dma_start(dst[r * D:(r + 1) * D, :, j, :],
                                 src[j * D:(j + 1) * D, 0 if role == "hi" else 1, :, :]).then_inc(s, 16)
        s_past = {e: sem(f"past_{e}") for e in ("sp", "pool", "dve", "act")}

        with nc.Block() as block:
            @block.sync
            def _(sp):
                def sp_wait(*what):
                    wait(sp, *what, past=s_past["sp"])

                def load_tables():
                    for dst, src in ((b_q, biases[0]), (b_k, biases[1]), (b_v, biases[2]), (b_o, biases[3]),
                                     (cos, rope[0]), (sin, rope[1])):
                        sp.dma_start(dst[:], src).then_inc(s_w, 16)

                full, sread, x1c, lo = (Count(s) for s in (s_full, s_sread, s_x1, s_lo))
                evac, clo = Count(s_evac), Count(s_clo)
                x1out, xn2out = [Count(s) for s in s_x1out], Count(s_xn2out)
                counts = [full, sread, x1c, lo, evac, clo, *x1out, xn2out]

                def load_resid(t, st):
                    sp_wait(x1c)
                    sp.dma_start(resid[st % 2], x[t.index(), st * P:(st + 1) * P, :]).then_inc(s_res[st % 2], 16)

                def turn(b, has_prev, has_next):
                    for kind, t, *arg in order(b, has_prev, has_next):
                        if kind == "load":
                            sp_wait(full)
                            for c in x1out:
                                sp_wait(c)
                            sp_wait(xn2out)
                            sp.dma_start(xt[:], x[t.index()].rearrange("(s p) e -> p s e", p=P)).then_inc(s_x, 16)
                            sp_wait(clo)
                            sp.dma_start(ct[:], ctxT[t.index()].rearrange("(c p) t -> p c t", p=P)).then_inc(s_c, 16)
                            if t.turn is None and t.c == 0:
                                load_tables()
                        elif kind == "c_low":
                            clo.up()
                        elif kind == "x":
                            full.up(4), evac.up(4), lo.up(4)
                        elif kind in "kqv":
                            full.up(), evac.up()
                        elif kind == "k_end":
                            sp_wait(s_lo, lo.up(4))
                            stack(sp, ks[t.par], qkp, ROLE_K, s_kst)
                        elif kind == "q_end":
                            sp_wait(s_lo, lo.up(4))
                            stack(sp, qs[t.par], qkp, ROLE_Q, s_qst)
                        elif kind == "scores":
                            sread.up(2)
                        elif kind == "rows":
                            sp_wait(s_sread, sread.up())
                            for part in range(2):
                                sp.dma_start(qs[t.par][KROWS + part:KROWS + part + 1, arg[0], :, :],
                                             mrow[part * HG:(part + 1) * HG, :]).then_inc(s_min, 16)
                        elif kind == "out":
                            st = arg[0]
                            full.up(), evac.up()
                            if st == 0:
                                sp_wait(clo)
                                sp_wait(xn2out)
                                load_resid(t, 0)
                                load_resid(t, 1)
                            sp_wait(s_x1, x1c.up())
                            sp.dma_start(x1[t.index(), st * P:(st + 1) * P, :], sum1[st % 2]
                                         ).then_inc(s_x1out[st % 2], 16)
                            x1out[st % 2].up(16)
                            if st < 2:
                                load_resid(t, st + 2)
                        elif kind == "xn2":
                            full.up(ST)
                            sp_wait(s_evac, evac.up(ST))
                            sp.dma_start(xn2T[t.index()], ct[:]).then_inc(s_xn2out, 16)
                            xn2out.up(16)

                run(sp, counts, turn)
                for c in x1out:
                    sp_wait(c)
                sp_wait(xn2out)

            @block.gpsimd
            def _(pool):
                def pool_wait(*what):
                    wait(pool, *what, past=s_past["pool"])

                pool.memset(power[:], -0.5).then_inc(s_const, 1)
                pool.memset(ident[:], 0.0).then_inc(s_const, 1)
                pool.memset(ident16[:], 0.0).then_inc(s_const, 1)
                pool.memset(identb[:], 0.0).then_inc(s_const, 1)
                pool.memset(mask_s[:], 0.0).then_inc(s_const, 1)
                pool.memset(mask_t[:], 0.0).then_inc(s_const, 1)
                pool.memset(ones[:], 1.0).then_inc(s_const, 1)
                pool.wait_ge(s_const, 7)
                for t in (ident, ident16, identb):
                    pool.affine_select(out=t[:], in_=t[:], compare_op=ALU.not_equal, fill=1.0, base=0,
                                       pattern=[[-1, P]], channel_multiplier=1).then_inc(s_const, 1)
                pool.affine_select(out=mask_s[:], in_=mask_s[:], compare_op=ALU.is_ge, fill=MASKED, base=0,
                                   pattern=[[-1, P]], channel_multiplier=1).then_inc(s_const, 1)
                pool.affine_select(out=mask_t[:], in_=mask_t[:], compare_op=ALU.is_ge, fill=MASKED, base=0,
                                   pattern=[[1, P]], channel_multiplier=-1).then_inc(s_const, 1)
                ln, rotc, rstdc, ln2, rstd2c, xn1 = (
                    Count(s) for s in (s_ln, s_rot, s_rstd, s_ln2, s_rstd2, s_xn))
                res = [Count(s) for s in s_res]
                counts = [ln, rotc, rstdc, *res, ln2, rstd2c, xn1]

                def resid_bias(st):
                    pool_wait(s_res[st % 2], res[st % 2].up(16))
                    pool.tensor_tensor(resid[st % 2], resid[st % 2], b_o[:], ALU.add).then_inc(s_resb, 1)

                def turn(b, has_prev, has_next):
                    for kind, t, *arg in order(b, has_prev, has_next):
                        if kind == "norm_x":
                            pool_wait(s_ln, ln.up(8))
                            pool_wait(xn1)
                            pool.tensor_scalar(rstd[:], mv[:, :, 1], EPS, None, ALU.add).then_inc(s_rstd, 1)
                            pool_wait(s_rstd, rstdc.up())
                            pool.tensor_tensor(rstd[:], rstd[:], power[:], ALU.pow).then_inc(s_rstd, 1)
                            if b.c == -2:
                                two = float(np.array([M_DOWN, M_DOWN], np.float16).view(np.float32)[0])
                                pool.wait_ge(s_rstd, 2)
                                for k in range(2):
                                    pool.memset(ks[k][KROWS:P].rearrange("p c h s -> p (c h s)").bitcast(F32),
                                                two).then_inc(s_rows, 1)
                                    pool.wait_ge(s_rows, k + 1)
                            rstdc.up()
                            xn1.up(4)
                        elif kind in "kq":
                            eo = arg[0]
                            if b.c == -1 and kind == "k" and eo == 0:
                                pool.wait_ge(s_w, TABLES)
                            pool_wait(s_rot, rotc.up())
                            pool.tensor_tensor(rot[:, eo % 2], rot[:, eo % 2], sin[:], ALU.mult).then_inc(s_mul, 1)
                        elif kind == "out":
                            if arg[0] == 0:
                                resid_bias(0)
                                resid_bias(1)
                            for st in arg:
                                pool_wait(s_ln2, ln2.up(2))
                                pool.tensor_scalar(rstd2[:, st:st + 1], mv2[:, st, 1:2], EPS, None,
                                                   ALU.add).then_inc(s_rstd2, 1)
                                pool_wait(s_rstd2, rstd2c.up())
                                pool.tensor_tensor(rstd2[:, st:st + 1], rstd2[:, st:st + 1], power[:, 0:1],
                                                   ALU.pow).then_inc(s_rstd2, 1)
                                rstd2c.up()
                                if st < 2:
                                    resid_bias(st + 2)

                run(pool, counts, turn)

            @block.scalar
            def _(act):
                full, lo, xn2c, clo = (Count(s) for s in (s_full, s_lo, s_xn2, s_clo))
                tfull, pv, c_in, summ, norm, aolo = (Count(s) for s in (s_tfull, s_pv, s_c, s_sum, s_norm, s_aolo))
                kst, qst = Count(s_kst), Count(s_qst)
                x1out, xn2out = [Count(s) for s in s_x1out], Count(s_xn2out)
                counts = [full, lo, xn2c, clo, tfull, pv, c_in, summ, norm, aolo, kst, qst, *x1out, xn2out]

                def high(item):
                    wait(act, s_sum, summ.up())
                    act.activation(qkp[:, 0, item], tmp[:, item], ACT.Copy).then_inc(s_hi, 1)

                def turn(b, has_prev, has_next):
                    for kind, t, *arg in order(b, has_prev, has_next):
                        if kind == "c_high":
                            wait(act, s_c, c_in.up(16))
                            wait(act, full)
                            act.activation(cp[:, 0], ct[:], ACT.Copy, scale=X_UP).then_inc(s_chi, 1)
                        elif kind == "c_low":
                            clo.up()
                        elif kind == "x":
                            for ec in range(C):
                                wait(act, s_full, full.up())
                                wait(act, s_lo, lo.value(3))
                                act.activation(xp[:, 0, ec], proj[(full.n - 1) % 2][:], ACT.Copy, scale=X_UP).then_inc(s_hi, 1)
                                act.activation(tmp[:, ec], proj[(full.n - 1) % 2][:], ACT.Copy, scale=X_UP).then_inc(s_evac, 1)
                                lo.up()
                        elif kind in "kq":
                            bias = b_k if kind == "k" else b_q
                            if b.c == -1 and kind == "k" and arg[0] == 0:
                                act.wait_ge(s_dc, 4)
                            for eo in arg:
                                wait(act, s_full, full.up())
                                wait(act, s_lo, lo.value(3))
                                act.activation(tmp[:, eo], proj[(full.n - 1) % 2][:], ACT.Identity, bias=bias[:, eo:eo + 1],
                                               scale=PROJ_DOWN * QK_UP).then_inc(s_evac, 1)
                                lo.up()
                                if eo == 2:
                                    wait(act, qst if kind == "k" else kst)
                                if eo >= 2:
                                    high(eo - 2)
                        elif kind in ("k_end", "q_end"):
                            high(2)
                            high(3)
                            (kst if kind == "k_end" else qst).up(192)
                        elif kind == "v":
                            for tb in arg:
                                wait(act, s_full, full.up())
                                act.activation(v[:, tb], proj[(full.n - 1) % 2][:], ACT.Copy, scale=PROJ_DOWN * X_UP).then_inc(s_evac, 1)
                        elif kind == "exp":
                            for u, _ in two_units(arg[1], True):
                                wait(act, s_tfull, tfull.up())
                                if u == 0:
                                    wait(act, pv)
                                act.activation(pt[:, u], sct[u % 2][:], ACT.Exp, scale=EXP_SCALE).then_inc(s_exp, 1)
                        elif kind == "pv":
                            wait(act, s_pv, pv.up())
                            wait(act, aolo)
                            act.activation(att[:], ps_o[:], ACT.Copy).then_inc(s_pvread, 1)
                            act.activation(rden[:], ps_d[:], ACT.Copy).then_inc(s_pvread, 1)
                        elif kind == "ao_parts":
                            g = arg[0]
                            wait(act, s_norm, norm.up(2))
                            act.activation(aop[t.par][:, 0, g], att[:], ACT.Identity,
                                           bias=b_v[:, g:g + 1]).then_inc(s_aohi, 1)
                            aolo.up()
                        elif kind == "out":
                            for st in arg:
                                wait(act, s_full, full.up())
                                wait(act, clo)
                                if st == 0:
                                    wait(act, xn2out)
                                wait(act, x1out[st % 2])
                                if st >= 2:
                                    wait(act, s_xn2, xn2c.value(1))
                                act.activation(sum1[st % 2], proj[(full.n - 1) % 2][:], ACT.Copy,
                                               scale=PROJ_DOWN).then_inc(s_evac, 1)
                                x1out[st % 2].up(16)
                                xn2c.up()
                        elif kind == "xn2":
                            for st in range(ST):
                                wait(act, s_full, full.up())
                                for c in x1out:
                                    wait(act, c)
                                act.activation(ct[:, st], proj[(full.n - 1) % 2][:], ACT.Copy).then_inc(s_evac, 1)
                            xn2out.up(16)

                run(act, counts, turn)

            @block.vector
            def _(dve):
                x_in, rstdc, ln, xn = Count(s_x), Count(s_rstd), Count(s_ln), Count(s_xn)
                hi, evac, mul, summ, rotc = Count(s_hi), Count(s_evac), Count(s_mul), Count(s_sum), Count(s_rot)
                chi, lo, sfull, sread, mc, minn = (Count(s) for s in (s_chi, s_lo, s_sfull, s_sread, s_m, s_min))
                pvr, norm, aohi, resb = Count(s_pvread), Count(s_norm), Count(s_aohi), Count(s_resb)
                cosc, aolo = Count(s_cos), Count(s_aolo)
                x1c, ln2, rstd2c, xn2c, pk = Count(s_x1), Count(s_ln2), Count(s_rstd2), Count(s_xn2), Count(s_peak)
                counts = [x_in, rstdc, ln, xn, hi, evac, mul, summ, rotc, chi, lo, sfull, sread, mc, minn,
                          pvr, norm, aohi, resb, x1c, ln2, rstd2c, xn2c, pk, aolo, cosc]
                dve.memset(peak[:], 0.0).then_inc(s_dc, 1)

                def rotate(item):
                    wait(dve, s_evac, evac.up())
                    wait(dve, summ, past=s_past["dve"])
                    dve.stream_shuffle(rot[:, item % 2], tmp[:, item % 4],
                                       [(d + D // 2) % D for d in range(D)]).then_inc(s_rot, 1)
                    rotc.up()
                    wait(dve, s_rot, rotc.value())
                    dve.tensor_tensor(tmp[:, item % 4], tmp[:, item % 4], cos[:], ALU.mult).then_inc(s_cos, 1)

                def rope_sum(item):
                    wait(dve, s_cos, cosc.up())
                    wait(dve, s_mul, mul.up())
                    dve.tensor_tensor(tmp[:, item % 4], tmp[:, item % 4], rot[:, item % 2], ALU.add).then_inc(s_sum, 1)
                    summ.up()

                def low(item, dst):
                    wait(dve, s_hi, hi.up())
                    dve.tensor_tensor(dst[:, 1, item % 4], tmp[:, item % 4], dst[:, 0, item % 4],
                                      ALU.subtract).then_inc(s_lo, 1)
                    lo.up()

                def norm_x1(st):
                    wait(dve, s_rstd2, rstd2c.up(2))
                    dve.tensor_scalar(xt[:, st], sum1[st % 2], mv2[:, st, 0:1], rstd2[:, st:st + 1],
                                      ALU.subtract, ALU.mult).then_inc(s_xn2, 1)
                    xn2c.up()

                def top_x1(st):
                    wait(dve, s_xn2, xn2c.value())
                    wait(dve, s_peak, pk.value())
                    dve.tensor_reduce(peak_b[:, st:st + 1], xt[:, st], AXX, ALU.max,
                                      apply_absolute_value=True).then_inc(s_peak, 1)
                    pk.up()

                def turn(b, has_prev, has_next):
                    for kind, t, *arg in order(b, has_prev, has_next):
                        if kind == "norm_x":
                            wait(dve, s_x, x_in.up(16))
                            wait(dve, xn)
                            for st in range(ST):
                                dve.bn_stats(stats[:, st], xt[:, st]).then_inc(s_ln, 1)
                            for st in range(ST):
                                wait(dve, s_ln, ln.up(), past=s_past["dve"])
                                dve.bn_aggr(mv[:, st], stats[:, st]).then_inc(s_ln, 1)
                            ln.up(4)
                            wait(dve, s_rstd, rstdc.up(2))
                            for st in range(ST):
                                dve.tensor_scalar(xt[:, st], xt[:, st], mv[:, st, 0:1], rstd[:, st:st + 1],
                                                  ALU.subtract, ALU.mult).then_inc(s_xn, 1)
                            xn.up(4)
                        elif kind == "c_low":
                            wait(dve, s_chi, chi.up())
                            dve.scalar_tensor_tensor(cp[:, 1], ct[:], X_UP, cp[:, 0], ALU.mult,
                                                     ALU.subtract).then_inc(s_clo, 1)
                        elif kind == "x":
                            for ec in range(C):
                                wait(dve, s_evac, evac.up())
                                low(ec, xp)
                        elif kind in "kq":
                            if b.c == -1 and kind == "k" and arg[0] == 0:
                                dve.wait_ge(s_w, TABLES)
                                for bias, up in ((b_q, QK_UP), (b_k, QK_UP), (b_v, X_UP)):
                                    dve.tensor_scalar(bias[:], bias[:], up, None, ALU.mult).then_inc(s_dc, 1)
                            for eo in arg:
                                rotate(eo)
                                if eo > 0:
                                    rope_sum(eo - 1)
                                if eo > 1:
                                    low(eo - 2, qkp)
                        elif kind in ("k_end", "q_end"):
                            rope_sum(3)
                            low(2, qkp)
                            low(3, qkp)
                        elif kind == "v":
                            evac.up()
                        elif kind == "xn2":
                            evac.up(4)
                        elif kind == "scores":
                            if arg[1] == 0:
                                wait(dve, mc)
                            for u, blocks in two_units(arg[1], False):
                                wait(dve, s_sfull, sfull.up())
                                bank = sc[(sfull.n - 1) % 2]
                                if blocks[0][1] == 1:
                                    pair = u // 5
                                    last = dve.tensor_reduce(mx[:, 1, 2 * pair:2 * pair + 2],
                                                             bank[:].rearrange("p (j t) -> p j t", j=2), AXX, ALU.max)
                                else:
                                    for j, sbt, col in blocks:
                                        last = dve.tensor_reduce(mx[:, sbt, j:j + 1],
                                                                 bank[:, col:col + (sbt + 1) * P], AXX, ALU.max)
                                last.then_inc(s_sread, 1)
                                sread.up()
                            if arg[1] == 4:
                                wait(dve, sread)
                                dve.tensor_scalar(mp[:, :, 0], mx[:], -1.0 / M_DOWN, None, ALU.mult).then_inc(s_m, 1)
                                wait(dve, s_m, mc.up())
                                dve.scalar_tensor_tensor(mp[:, :, 1], mx[:], -1.0 / M_DOWN, mp[:, :, 0],
                                                         ALU.mult, ALU.subtract).then_inc(s_m, 1)
                                mc.up()
                        elif kind == "rows":
                            wait(dve, s_sfull, sfull.up())
                            wait(dve, minn)
                            bank = sc[(sfull.n - 1) % 2]
                            dve.tensor_copy(mrow[:], bank[0:2 * HG, 0:S // 2].bitcast(F16)).then_inc(s_sread, 1)
                            sread.up()
                            minn.up(32)
                        elif kind == "ao_norm":
                            wait(dve, s_pvread, pvr.up(2))
                            dve.reciprocal(rden[:], rden[:]).then_inc(s_norm, 1)
                            wait(dve, s_norm, norm.up())
                            dve.tensor_tensor(att[:], att[:], rden[:], ALU.mult).then_inc(s_norm, 1)
                            norm.up()
                        elif kind == "ao_parts":
                            g = arg[0]
                            wait(dve, s_aohi, aohi.up())
                            dve.scalar_tensor_tensor(aop[t.par][:, 1, g], att[:], b_v[:, g:g + 1], aop[t.par][:, 0, g],
                                                     ALU.add, ALU.subtract).then_inc(s_aolo, 1)
                            aolo.up()
                        elif kind == "out":
                            for st in arg:
                                wait(dve, s_evac, evac.up())
                                wait(dve, s_resb, resb.up())
                                dve.tensor_tensor(sum1[st % 2], sum1[st % 2], resid[st % 2], ALU.add).then_inc(s_x1, 1)
                                wait(dve, s_x1, x1c.up())
                                wait(dve, xn2c)
                                dve.bn_stats(stats2[:, st], sum1[st % 2]).then_inc(s_ln2, 1)
                                wait(dve, s_ln2, ln2.up(), past=s_past["dve"])
                                dve.bn_aggr(mv2[:, st], stats2[:, st]).then_inc(s_ln2, 1)
                                ln2.up()
                                if st > 0:
                                    norm_x1(st - 1)
                                if st > 1:
                                    top_x1(st - 2)
                        elif kind == "out_end":
                            norm_x1(3)
                            top_x1(2)
                            top_x1(3)
                            wait(dve, pk)
                            dve.tensor_tensor(peak[:], peak[:], peak_b[:], ALU.max).then_inc(s_peak, 1)
                            pk.up()

                run(dve, counts, turn)
                wait(dve, pk)

            @block.tensor
            def _(pe):
                evac, xn, lo, clo, kst, qst = (Count(s) for s in (s_evac, s_xn, s_lo, s_clo, s_kst, s_qst))
                sread, mc, minn, exp, pvr, aolo, xn2c = (Count(s) for s in (s_sread, s_m, s_min, s_exp, s_pvread, s_aolo, s_xn2))
                counts = [evac, xn, lo, clo, kst, qst, sread, mc, minn, exp, pvr, aolo, xn2c]
                pe.wait_ge(s_const, 12)

                def next_bank():
                    evac.up()
                    wait(pe, s_evac, evac.value(2))
                    return proj[(evac.n - 1) % 2]

                def product(bank, left, right):
                    n = 0
                    for c in range(C):
                        for a, z in ((0, 0), (0, 1), (1, 0)):
                            last = pe.matmul(bank[:], left(a, c), right(z, c), start=n == 0, stop=n == 3 * C - 1)
                            n += 1
                    last.then_inc(s_full, 1)

                def turn(b, has_prev, has_next):
                    for kind, t, *arg in order(b, has_prev, has_next):
                        if kind == "x":
                            wait(pe, s_xn, xn.up(4))
                            for ec in range(C):
                                bank = next_bank()
                                for st in range(ST):
                                    last = pe.transpose(bank[:, st * P:(st + 1) * P], xt[:, st, ec * P:(ec + 1) * P], ident[:])
                                last.then_inc(s_full, 1)
                            lo.up(4)
                        elif kind == "k":
                            if arg[0] == 0:
                                wait(pe, s_clo, clo.up())
                            for eo in arg:
                                cols = slice(eo * P, (eo + 1) * P)
                                product(next_bank(), lambda a, c: W["k"][:, a, c, cols], lambda z, c: cp[:, z, c])
                            lo.up()
                        elif kind == "q":
                            if arg[0] == 0:
                                wait(pe, s_lo, lo.value(4))
                            for eo in arg:
                                cols = slice(eo * P, (eo + 1) * P)
                                product(next_bank(), lambda a, c: W["q"][:, a, c, cols], lambda z, c: xp[:, z, c])
                            lo.up()
                        elif kind == "v":
                            for tb in arg:
                                cols = slice(tb * P, (tb + 1) * P)
                                product(next_bank(), lambda a, c: cp[:, a, c, cols], lambda z, c: W["v"][:, z, c])
                        elif kind == "scores":
                            g, i = arg
                            if g == 0 and i == 0:
                                if b.c == -1:
                                    pe.wait_ge(s_rows, 2)
                                wait(pe, s_kst, kst.up(192))
                                wait(pe, s_qst, qst.up(192))
                            for _, blocks in two_units(i, False):
                                sread.up()
                                wait(pe, s_sread, sread.value(2))
                                bank = sc[(sread.n - 1) % 2]
                                for j, sbt, col in blocks:
                                    w = (sbt + 1) * P
                                    pe.matmul(bank[:, col:col + w], qs[t.par][0:KROWS, g, j, sbt * P:w],
                                              ks[t.par][0:KROWS, g, j, 0:w], start=True, stop=False)
                                    last = pe.matmul(bank[:, col + w - P:col + w], identb[:], mask_s[:],
                                                     start=False, stop=True)
                                last.then_inc(s_sfull, 1)
                        elif kind == "rows":
                            wait(pe, s_m, mc.up(2))
                            sread.up()
                            wait(pe, s_sread, sread.value(2))
                            bank = sc[(sread.n - 1) % 2]
                            for st in range(ST):
                                last = pe.transpose(bank[0:2 * HG, st * P // 2:(st + 1) * P // 2].bitcast(F16),
                                                    mp[:, st].rearrange("p a j -> p (a j)"), ident16[:])
                            last.then_inc(s_sfull, 1)
                        elif kind == "exp":
                            g, i = arg
                            if i == 0:
                                wait(pe, s_min, minn.up(32))
                            for _, blocks in two_units(i, True):
                                exp.up()
                                wait(pe, s_exp, exp.value(2))
                                bank = sct[(exp.n - 1) % 2]
                                for j, tb, col in blocks:
                                    w = S - tb * P
                                    pe.matmul(bank[:, col:col + w], ks[t.par][0:MROWS, g, j, tb * P:(tb + 1) * P],
                                              qs[t.par][0:MROWS, g, j, tb * P:S], start=True, stop=False)
                                    last = pe.matmul(bank[:, col:col + P], identb[:], mask_t[:],
                                                     start=False, stop=True)
                                last.then_inc(s_tfull, 1)
                        elif kind == "pv":
                            g = arg[0]
                            wait(pe, exp)
                            wait(pe, pvr)
                            where = {}
                            for pair in range(2):
                                for u, blocks in enumerate(heads_blocks(pair, True)):
                                    for j, tb, col in blocks:
                                        where[j, tb] = (pair * 5 + u, col)
                            for tb in range(ST):
                                w = S - tb * P
                                for dst in (ps_o, ps_d):
                                    for j in range(HG):
                                        u, col = where[j, tb]
                                        head = (HG * g + j) * D
                                        left = v[:, tb, head:head + D] if dst is ps_o else ones[:]
                                        last = pe.matmul(dst[j * D:(j + 1) * D, tb * P:S], left, pt[:, u, col:col + w],
                                                         start=tb == 0, stop=tb == ST - 1)
                            last.then_inc(s_pv, 1)
                            pvr.up(2)
                        elif kind == "ao_parts":
                            aolo.up()
                        elif kind == "out":
                            if arg[0] == 0:
                                wait(pe, aolo)
                            for st in arg:
                                cols = slice(st * P, (st + 1) * P)
                                product(next_bank(), lambda a, c: aop[t.par][:, a, c, cols], lambda z, c: W["o"][:, z, c])
                        elif kind == "xn2":
                            wait(pe, s_xn2, xn2c.up(4))
                            for st in range(ST):
                                bank = next_bank()
                                for ec in range(C):
                                    last = pe.transpose(bank[:, ec * P:(ec + 1) * P], xt[:, st, ec * P:(ec + 1) * P], ident[:])
                                last.then_inc(s_full, 1)

                run(pe, counts, turn)


T = B
PIECES = 3
CH = IC // PIECES
CW = PIECES * S
RING = 6
RMAX = bass.bass_isa.ReduceOp.max
(X_MAX, X_S, X_INV, X_UNIT, G_MAX, G_S, G_INV, U_MAX, U_S, U_INV, F_MAX, F_UNIT, F_S, F_INV,
 O_MAX, O_UNIT, O_S, O_MUL, TOP, TMP, N_SCALARS) = range(21)


def tiles_in_pairs(eng, counts, growth, turn):
    turn(0, False)
    with eng.Fori(0, T // 2 - 2) as i:
        for c in counts:
            c.enter(i, growth[c.sem])
        turn(i * 2 + 2, False)
    for c in counts:
        c.leave(T // 2 - 2)
    turn(T - 2, True)


def three_pass_product(pe, bank, chunks, left, right):
    n = 0
    for c in range(chunks):
        for a, z in ((0, 0), (0, 1), (1, 0)):
            last = pe.matmul(bank, left(a, c), right(z, c), start=n == 0, stop=n == 3 * chunks - 1)
            n += 1
    return last


class Scalars:

    def __init__(self, dve, table, sem):
        self.dve, self.table, self.sem, self.n = dve, table, sem, 0

    def col(self, k):
        return self.table[:, k:k + 1]

    def after(self, ins):
        ins.then_inc(self.sem, 1)
        self.n += 1
        self.dve.wait_ge(self.sem, self.n)

    def quantisation(self, top, unit, scale, inverse):
        dve, col = self.dve, self.col
        if unit is None:
            self.after(dve.tensor_scalar(col(scale), col(top), 1.0 / QMAX_A, TINY, ALU.mult, ALU.max))
            self.after(dve.reciprocal(col(inverse), col(scale)))
            return
        self.after(dve.tensor_scalar(col(TMP), col(top), col(unit), 1.0 / QMAX_A, ALU.mult, ALU.mult))
        self.after(dve.tensor_scalar(col(scale), col(TMP), TINY, None, ALU.max))
        self.after(dve.reciprocal(col(TMP), col(scale)))
        self.after(dve.tensor_tensor(col(inverse), col(TMP), col(unit), ALU.mult))


def gate_stage(nc, wf, wf_parts, xn2T, x_int, g_raw, table, peak_x, peak_g, w_next):
    NB = 2 * 512 // BLOCK
    W_AT, W_DONE = (0, 3, 6), (2, 5, 8)
    with ExitStack() as ctx:
        def sb(n, s, d):
            return ctx.enter_context(nc.sbuf_tensor("g_" + n, s, d))

        def sem(n):
            return ctx.enter_context(nc.semaphore("g_" + n))

        w = sb("w", [P, IC, 2, C, P], F16)
        xn = [sb(f"xn{k}", [P, ST, C * P], F32) for k in range(2)]
        xi = [sb(f"xi{k}", [P, C, S], I16) for k in range(2)]
        xp = [sb(f"xp{k}", [P, 2, C, S], F16) for k in range(2)]
        stage = [sb(f"stage{k}", [P, PIECES, S], F32) for k in range(2)]
        top = sb("top", [P, 2 * CH], F32)
        bank = [ctx.enter_context(nc.psum_tensor(f"g_bank{k}", [P, S], F32)) for k in range(RING)]
        wraw = [sb(f"wraw{j}", [P, 2, 512], F32) for j in range(3)]
        wtop, winv = sb("wtop", [P, 3, NB], F32), sb("winv", [P, 3, NB], F32)
        wint = sb("wint", [P, 3, 2 * 512], I16)
        wdeq = [sb(f"wdeq{j}", [P, 2, 512], F32) for j in range(3)]
        ident = sb("ident", [P, P], F32)
        wbank = ctx.enter_context(nc.psum_tensor("g_wbank", [P, 2, 512], F32))
        s_w = [sem(f"w{c}") for c in range(CH)]
        s_id, s_wq, s_wt, s_whi, s_wlo = (sem(n) for n in ("id", "wquant", "wtransposed", "whi", "wlo"))
        s_wraw = [sem(f"wraw{j}") for j in range(3)]
        s_ready, s_max, s_sc = sem("ready"), sem("max"), sem("scalars")
        s_x = [sem(f"x{k}") for k in range(2)]
        s_xst = [sem(f"xst{k}") for k in range(2)]
        s_int, s_hi, s_lo = sem("int"), sem("hi"), sem("lo")
        s_full, s_evac, s_top, s_peak = sem("full"), sem("evac"), sem("top"), sem("peak")
        s_st = [sem(f"st{k}") for k in range(2)]
        growth = {s_int: 2, s_hi: 2, s_lo: 2, s_full: 2 * IC, s_evac: 2 * IC, s_top: 2 * CH, s_peak: 1,
                  s_wq: 15, s_wt: 3, s_whi: 6, s_wlo: 6, **{s: 32 for s in s_wraw},
                  **{s: 16 for s in s_x + s_xst}, **{s: 16 * CH for s in s_st}}
        s_past = {e: sem(f"past_{e}") for e in ("sp", "pool", "dve", "act")}

        with nc.Block() as block:
            @block.sync
            def _(sp):
                def sp_wait(*what):
                    wait(sp, *what, past=s_past["sp"])

                ints, lo, evac, wq = Count(s_int), Count(s_lo), Count(s_evac), Count(s_wq)

                def load_weights(j, tile):
                    for k in range(2):
                        sp.dma_start(wraw[j][:, k], wf[tile + k]).then_inc(s_wraw[j], 16)

                def load(k, t):
                    sp_wait(s_int, ints.value(1))
                    ints.up()
                    sp.dma_start(xn[k][:], xn2T[t]).then_inc(s_x[k], 16)

                load(0, 0)
                for c in range(CH):
                    pieces = slice(c * PIECES, (c + 1) * PIECES)
                    sp.dma_start(w[:, pieces].rearrange("p k a c n -> p k (a c n)"),
                                 wf_parts[pieces].rearrange("k p a n -> p k (a n)")).then_inc(s_w[c], 16)
                load(1, 1)
                for j in range(3):
                    load_weights(j, IC + 2 * j)

                def store_parts(k, t):
                    sp_wait(s_lo, lo.up())
                    sp.dma_start(x_int[t], xp[k][:]).then_inc(s_xst[k], 16)

                def turn(t, last):
                    for k in range(2):
                        for c in range(CH):
                            sp_wait(s_evac, evac.up(PIECES))
                            sp.dma_start(g_raw[t + k, c], stage[c % 2][:].rearrange("p a n -> p (a n)")
                                         ).then_inc(s_st[c % 2], 16)
                            if c == 0 and not last:
                                load(k, t + k + 2)
                            if c == 1 and not (last and k):
                                store_parts(1 - k, t + k + 1)
                            n = k * CH + c
                            if n - 1 in W_AT:
                                wq.up(5)
                                if not last:
                                    j = W_AT.index(n - 1)
                                    sp_wait(s_wq, wq.value(1))
                                    load_weights(j, t * 3 + (IC + 6 + 2 * j))

                store_parts(0, 0)
                tiles_in_pairs(sp, [ints, lo, evac, wq], growth, turn)
                for k in range(2):
                    sp.wait_ge(s_st[k], 16 * CH * T // 2)
                    sp.wait_ge(s_xst[k], 16 * T // 2)

            @block.gpsimd
            def _(pool):
                pool.memset(ident[:], 0.0).then_inc(s_id, 1)
                pool.wait_ge(s_id, 1)
                pool.affine_select(out=ident[:], in_=ident[:], compare_op=ALU.not_equal, fill=1.0, base=0,
                                   pattern=[[-1, P]], channel_multiplier=1).then_inc(s_id, 1)
                pool.wait_ge(s_ready, 1)
                pool.partition_all_reduce(table[:, X_MAX:X_MAX + 1], table[:, TOP:TOP + 1], P, RMAX).then_inc(s_max, 1)

            @block.scalar
            def _(act):
                ints, full, xst, st, tops = (Count(s_int), Count(s_full), [Count(s) for s in s_xst],
                                             [Count(s) for s in s_st], Count(s_top))

                def high(k):
                    wait(act, s_int, ints.up())
                    wait(act, full)
                    wait(act, xst[k])
                    xst[k].up(16)
                    act.activation(xp[k][:, 0], xi[k][:], ACT.Copy).then_inc(s_hi, 1)

                wt = Count(s_wt)

                def weights_high(t, j):
                    wait(act, s_wt, wt.up(), past=s_past["act"])
                    for k in range(2):
                        act.activation(w_next[:, t * 3 + (2 * j + k), 0].rearrange("p c n -> p (c n)"), wbank[:, k],
                                       ACT.Copy, scale=W_UP).then_inc(s_whi, 1)

                def turn(t, last):
                    for k in range(2):
                        for c in range(CH):
                            if c == 1 and not (last and k):
                                high(1 - k)
                            if k * CH + c in W_DONE:
                                weights_high(t, W_DONE.index(k * CH + c))
                            wait(act, st[c % 2])
                            wait(act, s_top, tops.value(1))
                            st[c % 2].up(16)
                            tops.up()
                            for j in range(PIECES):
                                wait(act, s_full, full.up())
                                act.activation(stage[c % 2][:, j], bank[(c * PIECES + j) % RING][:],
                                               ACT.Copy).then_inc(s_evac, 1)
                    weights_high(t, 2)

                high(0)
                tiles_in_pairs(act, [ints, full, *xst, *st, tops, wt], growth, turn)

            @block.vector
            def _(dve):
                sc = Scalars(dve, table, s_sc)
                x, hi, ints, evac, tops, peak, lo = ([Count(s) for s in s_x], Count(s_hi), Count(s_int), Count(s_evac),
                                                     Count(s_top), Count(s_peak), Count(s_lo))
                sc.after(dve.memset(peak_g[:], 0.0))
                dve.tensor_reduce(sc.col(TOP), peak_x[:], AXX, ALU.max).then_inc(s_ready, 1)
                dve.wait_ge(s_max, 1)
                sc.quantisation(X_MAX, None, X_S, X_INV)
                sc.after(dve.tensor_scalar(sc.col(X_UNIT), sc.col(X_S), 1.0 / W_UP, None, ALU.mult))

                def integers(k):
                    wait(dve, s_x[k], x[k].up(16))
                    wait(dve, s_lo, lo.value(1))
                    dve.tensor_scalar(xi[k][:].rearrange("p c (s n) -> p c s n", s=ST),
                                      xn[k][:].rearrange("p s (c n) -> p c s n", c=C),
                                      sc.col(X_INV), None, ALU.mult).then_inc(s_int, 1)
                    wait(dve, s_hi, hi.up())
                    dve.tensor_tensor(xp[k][:, 1], xi[k][:], xp[k][:, 0], ALU.subtract).then_inc(s_lo, 1)
                    lo.up()

                wq, wraw_in, whi, wlo = Count(s_wq), [Count(s) for s in s_wraw], Count(s_whi), Count(s_wlo)

                def weights(j):
                    wait(dve, s_wraw[j], wraw_in[j].up(32))
                    blocks = wraw[j][:].rearrange("p k (b c) -> p (k b) c", c=BLOCK)
                    dve.tensor_reduce(wtop[:, j], blocks, AXX, ALU.max, apply_absolute_value=True).then_inc(s_wq, 1)
                    wait(dve, s_wq, wq.up())
                    dve.tensor_scalar(wtop[:, j], wtop[:, j], 1.0 / QMAX_W, TINY, ALU.mult, ALU.max).then_inc(s_wq, 1)
                    wait(dve, s_wq, wq.up())
                    dve.reciprocal(winv[:, j], wtop[:, j]).then_inc(s_wq, 1)
                    wait(dve, s_wq, wq.up())
                    q = wint[:, j].rearrange("p (b c) -> p b c", c=BLOCK)
                    dve.tensor_tensor(q, blocks, winv[:, j].unsqueeze(2).to_broadcast([P, NB, BLOCK]),
                                      ALU.mult).then_inc(s_wq, 1)
                    wait(dve, s_wq, wq.up())
                    deq = wdeq[j][:].rearrange("p k (b c) -> p (k b) c", c=BLOCK)
                    dve.tensor_tensor(deq, q, wtop[:, j].unsqueeze(2).to_broadcast([P, NB, BLOCK]),
                                      ALU.mult).then_inc(s_wq, 1)
                    wq.up()

                def weights_low(t, j):
                    wait(dve, s_whi, whi.up(2))
                    for k in range(2):
                        hi_part, lo_part = (w_next[:, t * 3 + (2 * j + k), a].rearrange("p c n -> p (c n)") for a in range(2))
                        dve.scalar_tensor_tensor(lo_part, wbank[:, k], W_UP, hi_part,
                                                 ALU.mult, ALU.subtract).then_inc(s_wlo, 1)
                    wlo.up(2)

                def turn(t, last):
                    wait(dve, peak)
                    for k in range(2):
                        for c in range(CH):
                            if c == 1 and not (last and k):
                                integers(1 - k)
                            if k * CH + c in W_AT:
                                weights(W_AT.index(k * CH + c))
                            if k * CH + c in W_DONE:
                                weights_low(t, W_DONE.index(k * CH + c))
                            wait(dve, s_evac, evac.up(PIECES))
                            n = k * CH + c
                            dve.tensor_reduce(top[:, n:n + 1], stage[c % 2][:].rearrange("p a n -> p (a n)"), AXX,
                                              ALU.max, apply_absolute_value=True).then_inc(s_top, 1)
                            tops.up()
                    weights_low(t, 2)
                    wait(dve, tops)
                    dve.tensor_tensor(peak_g[:], peak_g[:], top[:], ALU.max).then_inc(s_peak, 1)
                    peak.up()

                integers(0)
                tiles_in_pairs(dve, [*x, hi, evac, tops, peak, lo, wq, *wraw_in, whi, wlo], growth, turn)
                wait(dve, peak)

            @block.tensor
            def _(pe):
                lo, evac, wq, wlo = Count(s_lo), Count(s_evac), Count(s_wq), Count(s_wlo)
                pe.wait_ge(s_id, 2)

                def transpose_weights(j):
                    wait(pe, s_wq, wq.up(5))
                    wait(pe, wlo)
                    wlo.up(2)
                    for k in range(2):
                        for c in range(C):
                            cols = slice(c * P, (c + 1) * P)
                            last = pe.transpose(wbank[:, k, cols], wdeq[j][:, k, cols], ident[:])
                    last.then_inc(s_wt, 1)

                def turn(t, last):
                    for k in range(2):
                        wait(pe, s_lo, lo.up())
                        for ic in range(IC):
                            if ic % PIECES == 0 and k * CH + ic // PIECES in W_DONE:
                                transpose_weights(W_DONE.index(k * CH + ic // PIECES))
                            if isinstance(t, int) and k == 0 and ic % PIECES == 0:
                                pe.wait_ge(s_w[ic // PIECES], 16)
                            evac.up()
                            wait(pe, s_evac, evac.value(RING))
                            three_pass_product(pe, bank[ic % RING][:], C, lambda a, c: w[:, ic, a, c],
                                               lambda z, c: xp[k][:, z, c]).then_inc(s_full, 1)
                    transpose_weights(2)

                tiles_in_pairs(pe, [lo, evac, wq, wlo], growth, turn)


def up_stage(nc, x_int, g_raw, u_raw, table, peak_g, peak_u, peak_f, gq, w):
    N = T * CH

    def gate_steps(m):
        ends = N * 9 // 16
        if m < ends:
            return [(0, g) for g in range(m * N // ends, (m + 1) * N // ends)]
        return [(1, g) for g in range((m - ends) * N // (N - ends), (m + 1 - ends) * N // (N - ends))]

    with ExitStack() as ctx:
        def sb(n, s, d):
            return ctx.enter_context(nc.sbuf_tensor("u_" + n, s, d))

        def sem(n):
            return ctx.enter_context(nc.semaphore("u_" + n))

        xp = [sb(f"xp{k}", [P, 2, C, S], F16) for k in range(2)]
        stage = [sb(f"stage{k}", [P, PIECES, S], F32) for k in range(2)]
        raw = [sb(f"raw{k}", [P, CW], F32) for k in range(2)]
        sig = [sb(f"sig{k}", [P, CW], F32) for k in range(2)]
        sigq = sb("sigq", [P, CW], U16)
        size = sb("size", [P, CW], I16)
        bank = [ctx.enter_context(nc.psum_tensor(f"u_bank{k}", [P, S], F32)) for k in range(RING)]
        s_ready, s_max, s_sc, s_set = sem("ready"), sem("max"), sem("scalars"), sem("set")
        s_x = [sem(f"x{k}") for k in range(2)]
        s_g = [sem(f"g{k}") for k in range(2)]
        s_st = [sem(f"st{k}") for k in range(2)]
        s_full, s_evac, s_top = sem("full"), sem("evac"), sem("top")
        s_gq, s_size, s_sig, s_sigq, s_f, s_ftop, s_fq = (
            sem(n) for n in ("gq", "size", "sig", "sigq", "f", "ftop", "fq"))
        growth = {s_full: 2 * IC, s_evac: 2 * IC, **{s: 16 for s in s_x}}

        with nc.Block() as block:
            @block.sync
            def _(sp):
                gqc = Count(s_gq)

                def load_gate(g):
                    wait(sp, s_gq, gqc.value(1))
                    gqc.up()
                    sp.dma_start(raw[g % 2][:], g_raw[g // CH, g % CH]).then_inc(s_g[g % 2], 16)

                sp.dma_start(xp[0][:], x_int[0]).then_inc(s_x[0], 16)
                load_gate(0)
                load_gate(1)
                for m in range(N):
                    t, c = m // CH, m % CH
                    sp.wait_ge(s_evac, PIECES * (m + 1))
                    sp.dma_start(u_raw[t, c], stage[c % 2][:].rearrange("p a n -> p (a n)")).then_inc(s_st[c % 2], 16)
                    if c == 0 and t + 1 < T:
                        sp.dma_start(xp[(t + 1) % 2][:], x_int[t + 1]).then_inc(s_x[(t + 1) % 2], 16)
                    for last_pass, g in gate_steps(m):
                        if not last_pass and g + 2 < N:
                            load_gate(g + 2)
                for k in range(2):
                    sp.wait_ge(s_st[k], 16 * CH * T // 2)

            @block.gpsimd
            def _(pool):
                pool.wait_ge(s_ready, 1)
                pool.partition_all_reduce(table[:, G_MAX:G_MAX + 1], table[:, TOP:TOP + 1], P, RMAX).then_inc(s_max, 1)
                pool.wait_ge(s_ready, 2)
                pool.partition_all_reduce(table[:, F_MAX:F_MAX + 1], table[:, TOP:TOP + 1], P, RMAX).then_inc(s_max, 1)

            @block.scalar
            def _(act):
                act.wait_ge(s_set, 1)

                def sigmoid(g):
                    act.activation(sig[g % 2][:], gq[:, g // CH, g % CH], ACT.Sigmoid,
                                   scale=table[:, G_S:G_S + 1]).then_inc(s_sig, 1)

                def second_integers(g):
                    act.wait_ge(s_f, N // 2 + g + 1)
                    act.activation(gq[:, g // CH, g % CH], sig[g % 2][:], ACT.Copy,
                                   scale=table[:, F_INV:F_INV + 1]).then_inc(s_fq, 1)

                for m in range(N):
                    if m >= 2:
                        act.wait_ge(s_st[m % 2], 16 * (m // 2))
                        act.wait_ge(s_top, m - 1)
                    for j in range(PIECES):
                        act.wait_ge(s_full, m * PIECES + j + 1)
                        act.activation(stage[m % 2][:, j], bank[(m * PIECES + j) % RING][:],
                                       ACT.Copy).then_inc(s_evac, 1)
                    for last_pass, g in gate_steps(m):
                        if not last_pass:
                            act.wait_ge(s_g[g % 2], 16 * (g // 2 + 1))
                            act.activation(gq[:, g // CH, g % CH], raw[g % 2][:], ACT.Copy,
                                           scale=table[:, G_INV:G_INV + 1]).then_inc(s_gq, 1)
                            act.wait_ge(s_gq, g + 1)
                            if g >= 2:
                                act.wait_ge(s_ftop, g - 1)
                            if g % 2 == 0:
                                act.activation(size[:], gq[:, g // CH, g % CH], ACT.Abs).then_inc(s_size, 1)
                            sigmoid(g)
                            continue
                        if g == 0:
                            act.wait_ge(s_set, 2)
                        if g >= 2:
                            act.wait_ge(s_fq, g - 1)
                        sigmoid(g)
                        if g >= 1:
                            second_integers(g - 1)
                second_integers(N - 1)

            @block.vector
            def _(dve):
                sc = Scalars(dve, table, s_sc)
                dve.tensor_reduce(sc.col(TOP), peak_g[:], AXX, ALU.max).then_inc(s_ready, 1)
                dve.wait_ge(s_max, 1)
                sc.quantisation(G_MAX, X_UNIT, G_S, G_INV)
                dve.tensor_scalar(sc.col(F_UNIT), sc.col(G_S), 1.0 / 65536.0, None, ALU.mult).then_inc(s_set, 1)

                f = Count(s_f)
                for m in range(N):
                    dve.wait_ge(s_evac, PIECES * (m + 1))
                    dve.tensor_reduce(peak_u[:, m:m + 1], stage[m % 2][:].rearrange("p a n -> p (a n)"), AXX,
                                      ALU.max, apply_absolute_value=True).then_inc(s_top, 1)
                    for last_pass, g in gate_steps(m):
                        n = last_pass * N + g
                        if last_pass and g == 0:
                            dve.wait_ge(s_ftop, N)
                            dve.tensor_reduce(sc.col(TOP), peak_f[:], AXX, ALU.max).then_inc(s_ready, 1)
                            dve.wait_ge(s_max, 2)
                            dve.wait_ge(s_set, 1)
                            sc.quantisation(F_MAX, F_UNIT, F_S, F_INV)
                            dve.tensor_scalar(sc.col(TMP), sc.col(F_S), 1.0, None, ALU.mult).then_inc(s_set, 1)
                        dve.wait_ge(s_sig, n + 1)
                        if last_pass:
                            wait(dve, f)
                        elif g > 0:
                            dve.wait_ge(s_ftop, g)
                        dve.tensor_scalar(sigq[:], sig[g % 2][:], 65536.0, None, ALU.mult).then_inc(s_sigq, 1)
                        dve.wait_ge(s_sigq, n + 1)
                        if not last_pass and g % 2 == 0:
                            dve.wait_ge(s_size, g // 2 + 1)
                            dve.tensor_tensor_reduce(sig[g % 2][:], size[:], sigq[:], 1.0, 0.0, ALU.mult, ALU.max,
                                                     accum_out=peak_f[:, g:g + 1]).then_inc(s_ftop, 1)
                            continue
                        dve.tensor_tensor(sig[g % 2][:], gq[:, g // CH, g % CH], sigq[:], ALU.mult).then_inc(s_f, 1)
                        f.up()
                        if not last_pass:
                            wait(dve, f)
                            dve.tensor_reduce(peak_f[:, g:g + 1], sig[g % 2][:], AXX, ALU.max,
                                              apply_absolute_value=True).then_inc(s_ftop, 1)

            @block.tensor
            def _(pe):
                x, evac = [Count(s) for s in s_x], Count(s_evac)

                def turn(t, last):
                    for k in range(2):
                        wait(pe, s_x[k], x[k].up(16))
                        for ic in range(IC):
                            evac.up()
                            wait(pe, s_evac, evac.value(RING))
                            three_pass_product(pe, bank[ic % RING][:], C, lambda a, c: w[:, ic, a, c],
                                               lambda z, c: xp[k][:, z, c]).then_inc(s_full, 1)

                tiles_in_pairs(pe, [*x, evac], growth, turn)


def peak_stage(nc, u_raw, table, peak_u, peak_o, gq):
    with ExitStack() as ctx:
        def sb(n, s, d):
            return ctx.enter_context(nc.sbuf_tensor("p_" + n, s, d))

        def sem(n):
            return ctx.enter_context(nc.semaphore("p_" + n))

        raw = [sb(f"raw{k}", [P, CW], F32) for k in range(2)]
        uq = [sb(f"uq{k}", [P, CW], I16) for k in range(2)]
        fq = [sb(f"fq{k}", [P, CW], I16) for k in range(2)]
        prod = [sb(f"prod{k}", [P, CW], F32) for k in range(2)]
        top = sb("top", [P, 2 * CH], F32)
        s_ready, s_max, s_sc, s_set = sem("ready"), sem("max"), sem("scalars"), sem("set")
        s_u = [sem(f"u{k}") for k in range(2)]
        s_fq, s_uq, s_top, s_peak = (sem(n) for n in ("fq", "uq", "top", "peak"))
        growth = {**{s: 2 * CH for s in (s_fq, s_uq, s_top)}, s_peak: 1, **{s: 16 * CH for s in s_u}}
        s_past = {e: sem(f"past_{e}") for e in ("sp", "dve", "act")}

        with nc.Block() as block:
            @block.sync
            def _(sp):
                uqc = Count(s_uq)

                def turn(t, last):
                    for k in range(2):
                        for c in range(CH):
                            wait(sp, s_uq, uqc.value(1), past=s_past["sp"])
                            uqc.up()
                            sp.dma_start(raw[c % 2][:], u_raw[t + k, c]).then_inc(s_u[c % 2], 16)

                tiles_in_pairs(sp, [uqc], growth, turn)

            @block.gpsimd
            def _(pool):
                pool.wait_ge(s_ready, 1)
                pool.partition_all_reduce(table[:, U_MAX:U_MAX + 1], table[:, TOP:TOP + 1], P, RMAX).then_inc(s_max, 1)

            @block.scalar
            def _(act):
                tops, u = Count(s_top), [Count(s) for s in s_u]
                act.wait_ge(s_set, 1)

                def turn(t, last):
                    for n in range(2 * CH):
                        wait(act, s_top, tops.value(1), past=s_past["act"])
                        tops.up()
                        act.activation(fq[n % 2][:], gq[:, t + n // CH, n % CH], ACT.Abs).then_inc(s_fq, 1)
                        wait(act, s_u[n % 2], u[n % 2].up(16))
                        act.activation(uq[n % 2][:], raw[n % 2][:], ACT.Abs,
                                       scale=table[:, U_INV:U_INV + 1]).then_inc(s_uq, 1)

                tiles_in_pairs(act, [tops, *u], growth, turn)

            @block.vector
            def _(dve):
                sc = Scalars(dve, table, s_sc)
                sc.after(dve.memset(peak_o[:], 0.0))
                dve.tensor_reduce(sc.col(TOP), peak_u[:], AXX, ALU.max).then_inc(s_ready, 1)
                dve.wait_ge(s_max, 1)
                sc.quantisation(U_MAX, X_UNIT, U_S, U_INV)
                dve.tensor_tensor(sc.col(O_UNIT), sc.col(F_S), sc.col(U_S), ALU.mult).then_inc(s_set, 1)
                fqc, uqc, tops, peak = (Count(s) for s in (s_fq, s_uq, s_top, s_peak))

                def turn(t, last):
                    wait(dve, peak)
                    for n in range(2 * CH):
                        wait(dve, s_fq, fqc.up())
                        wait(dve, s_uq, uqc.up())
                        wait(dve, s_top, tops.value(1), past=s_past["dve"])
                        dve.tensor_tensor_reduce(prod[n % 2][:], fq[n % 2][:], uq[n % 2][:], 1.0, 0.0, ALU.mult,
                                                 ALU.max, accum_out=top[:, n:n + 1]).then_inc(s_top, 1)
                        tops.up()
                    wait(dve, tops)
                    dve.tensor_tensor(peak_o[:], peak_o[:], top[:], ALU.max).then_inc(s_peak, 1)
                    peak.up()

                tiles_in_pairs(dve, [fqc, uqc, tops, peak], growth, turn)
                wait(dve, peak)


def down_stage(nc, u_raw, x1, out, table, peak_o, gq, w):
    with ExitStack() as ctx:
        def sb(n, s, d):
            return ctx.enter_context(nc.sbuf_tensor("d_" + n, s, d))

        def sem(n):
            return ctx.enter_context(nc.semaphore("d_" + n))

        raw = [sb(f"raw{k}", [P, CW], F32) for k in range(2)]
        uq = [sb(f"uq{k}", [P, CW], I16) for k in range(2)]
        oi = [sb(f"oi{k}", [P, CW], I16) for k in range(2)]
        op = sb("op", [P, CH, 2, PIECES, S], F16)
        res = [sb(f"res{k}", [P, E], F32) for k in range(2)]
        bank = [ctx.enter_context(nc.psum_tensor(f"d_bank{k}", [P, E], F32)) for k in range(8)]
        s_ready, s_max, s_sc, s_set = sem("ready"), sem("max"), sem("scalars"), sem("set")
        s_u = [sem(f"u{k}") for k in range(2)]
        s_r = [sem(f"r{k}") for k in range(2)]
        s_out = [sem(f"out{k}") for k in range(2)]
        s_uq, s_oi, s_hi, s_lo, s_pass, s_full, s_y = (sem(n) for n in ("uq", "oi", "hi", "lo", "pass", "full", "y"))
        growth = {**{s: 2 * CH for s in (s_uq, s_oi, s_hi, s_lo)}, s_pass: 2 * (CH - 1), s_full: 2 * ST, s_y: 2 * ST,
                  **{s: 16 * CH for s in s_u}, **{s: 16 * ST for s in s_r + s_out}}
        s_past = {e: sem(f"past_{e}") for e in ("sp", "pool", "dve", "act")}

        with nc.Block() as block:
            @block.sync
            def _(sp):
                def sp_wait(*what):
                    wait(sp, *what, past=s_past["sp"])

                uqc, y = Count(s_uq), Count(s_y)
                out_c = [Count(s) for s in s_out]

                def load(t, c):
                    sp_wait(s_uq, uqc.value(1))
                    uqc.up()
                    sp.dma_start(raw[c % 2][:], u_raw[t, c]).then_inc(s_u[c % 2], 16)

                def chunks(t, last_tile):
                    for c in range(CH):
                        if not (last_tile and c == CH - 1):
                            load(t + (c + 1) // CH, (c + 1) % CH)

                def rows(t):
                    for st in range(ST):
                        sp_wait(out_c[st % 2])
                        out_c[st % 2].up(16)
                        sp.dma_start(res[st % 2][:], x1[t, st * P:(st + 1) * P, :]).then_inc(s_r[st % 2], 16)
                        sp_wait(s_y, y.up())
                        sp.dma_start(out[t, st * P:(st + 1) * P, :], res[st % 2][:]).then_inc(s_out[st % 2], 16)

                def turn(t, last):
                    for k in range(2):
                        if not (last and k):
                            chunks(t + k + 1, last)
                        rows(t + k)

                load(0, 0)
                chunks(0, False)
                tiles_in_pairs(sp, [uqc, y, *out_c], growth, turn)
                for c in out_c:
                    sp_wait(c)

            @block.gpsimd
            def _(pool):
                pool.wait_ge(s_ready, 1)
                pool.partition_all_reduce(table[:, O_MAX:O_MAX + 1], table[:, TOP:TOP + 1], P, RMAX).then_inc(s_max, 1)

            @block.scalar
            def _(act):
                u, oi_c, passed, full = [Count(s) for s in s_u], Count(s_oi), Count(s_pass), Count(s_full)

                def up_integers(c):
                    wait(act, s_u[c % 2], u[c % 2].up(16))
                    wait(act, oi_c)
                    act.activation(uq[c % 2][:], raw[c % 2][:], ACT.Copy,
                                   scale=table[:, U_INV:U_INV + 1]).then_inc(s_uq, 1)

                def high(c):
                    wait(act, s_oi, oi_c.up())
                    if c < CH - 1:
                        wait(act, s_pass, passed.value(CH - 2))
                        passed.up()
                    else:
                        wait(act, full)
                        full.up(ST)
                    act.activation(op[:, c, 0].rearrange("p a n -> p (a n)"), oi[c % 2][:], ACT.Copy).then_inc(s_hi, 1)

                def turn(t, last):
                    for k in range(2):
                        for c in range(CH):
                            if not (last and k and c == CH - 1):
                                up_integers((c + 1) % CH)
                            high(c)

                up_integers(0)
                tiles_in_pairs(act, [*u, oi_c, passed, full], growth, turn)

            @block.vector
            def _(dve):
                sc = Scalars(dve, table, s_sc)
                dve.tensor_reduce(sc.col(TOP), peak_o[:], AXX, ALU.max).then_inc(s_ready, 1)
                dve.wait_ge(s_max, 1)
                sc.quantisation(O_MAX, O_UNIT, O_S, O_MUL)
                sc.after(dve.tensor_scalar(sc.col(O_S), sc.col(O_S), 1.0 / W_UP, None, ALU.mult))
                uqc, hi, lo, full, r, y = (Count(s_uq), Count(s_hi), Count(s_lo), Count(s_full),
                                           [Count(s) for s in s_r], Count(s_y))

                def integers(t, c):
                    wait(dve, s_uq, uqc.up())
                    wait(dve, lo)
                    dve.scalar_tensor_tensor(oi[c % 2][:], gq[:, t, c], sc.col(O_MUL), uq[c % 2][:],
                                             ALU.mult, ALU.mult).then_inc(s_oi, 1)

                def chunks(t, last_tile):
                    for c in range(CH):
                        if not (last_tile and c == CH - 1):
                            integers(t + (c + 1) // CH, (c + 1) % CH)
                        wait(dve, s_hi, hi.up())
                        dve.tensor_tensor(op[:, c, 1].rearrange("p a n -> p (a n)"), oi[c % 2][:],
                                          op[:, c, 0].rearrange("p a n -> p (a n)"), ALU.subtract).then_inc(s_lo, 1)
                        lo.up()

                def rows(t):
                    for st in range(ST):
                        wait(dve, s_full, full.up())
                        wait(dve, s_r[st % 2], r[st % 2].up(16))
                        dve.scalar_tensor_tensor(res[st % 2][:], bank[(full.n - 1) % 8][:], sc.col(O_S),
                                                 res[st % 2][:], ALU.mult, ALU.add).then_inc(s_y, 1)
                        y.up()

                def turn(t, last):
                    for k in range(2):
                        if not (last and k):
                            chunks(t + k + 1, last)
                        rows(t + k)

                integers(0, 0)
                chunks(0, False)
                tiles_in_pairs(dve, [uqc, hi, lo, full, *r, y], growth, turn)

            @block.tensor
            def _(pe):
                lo, y = Count(s_lo), Count(s_y)

                def turn(t, last):
                    for k in range(2):
                        banks = [bank[k * ST + st] for st in range(ST)]
                        wait(pe, s_y, y.value(ST))
                        y.up(ST)
                        for c in range(CH):
                            wait(pe, s_lo, lo.up())
                            for st in range(ST):
                                cols = slice(st * P, (st + 1) * P)
                                for j in range(PIECES):
                                    ic = c * PIECES + j
                                    rows_of = slice(ic // C * C, ic // C * C + C)
                                    for a, z in ((0, 0), (0, 1), (1, 0)):
                                        last = pe.matmul(banks[st][:].rearrange("p (r n) -> p r n", r=C),
                                                         op[:, c, a, j, cols], w[:, rows_of, z, ic % C, :],
                                                         start=(c, j, a, z) == (0, 0, 0, 0),
                                                         stop=(c, j, a) == (CH - 1, PIECES - 1, 1))
                                if c == CH - 1:
                                    last.then_inc(s_full, 1)
                                elif st == ST - 1:
                                    last.then_inc(s_pass, 1)

                tiles_in_pairs(pe, [lo, y], growth, turn)


def block_program(nc, x, ctxT, wf, attn_w, b_qkv, b_o, rope, out):
    def scratch(name, shape, dtype):
        return nc.dram_tensor("scratch_" + name, shape, dtype, kind="Internal").ap()

    wf_parts = scratch("wf_parts", [IC, P, 2, 512], F16)
    x1 = scratch("x1", [B, S, E], F32)
    xn2T = scratch("xn2T", [B, P, ST, C * P], F32)
    x_int = scratch("x_int", [T, P, 2, C, S], F16)
    g_raw = scratch("g_raw", [T, CH, P, CW], F32)
    u_raw = scratch("u_raw", [T, CH, P, CW], F32)
    with ExitStack() as ctx:
        def sb(name, shape, dtype):
            return ctx.enter_context(nc.sbuf_tensor(name, shape, dtype))

        peak_x = sb("peak_x", [P, ST], F32)
        with ExitStack() as until_ffn:
            W = [until_ffn.enter_context(nc.sbuf_tensor("W" + m, [P, 2, C, E], F16)) for m in "qkvo"]
            weight_stage(nc, wf[0:IC].rearrange("(n k) p c -> n k p c", k=2), attn_w,
                         wf_parts.rearrange("(n k) p a c -> n k p a c", k=2), W)
            attention_stage(nc, x, ctxT, W, [b_qkv[0], b_qkv[1], b_qkv[2], b_o], rope, x1, xn2T, peak_x)
        table = sb("scalars", [P, N_SCALARS], F32)
        peak_g, peak_o = (sb(f"peak_{n}", [P, 2 * CH], F32) for n in "go")
        peak_u, peak_f = (sb(f"peak_{n}", [P, T * CH], F32) for n in "uf")
        w_next = sb("w_up_down", [P, 2 * IC, 2, C, P], F16)
        gate_stage(nc, wf, wf_parts, xn2T, x_int, g_raw, table, peak_x, peak_g, w_next)
        gq = sb("gq", [P, T, CH, CW], I16)
        up_stage(nc, x_int, g_raw, u_raw, table, peak_g, peak_u, peak_f, gq, w_next[:, 0:IC])
        peak_stage(nc, u_raw, table, peak_u, peak_o, gq)
        down_stage(nc, u_raw, x1, out, table, peak_o, gq, w_next[:, IC:2 * IC])


def rope_tables():
    inv = (np.float32(1.0) / np.float32(10000.0) ** (np.arange(0, D, 2, dtype=np.float32) / np.float32(D))).astype(np.float32)
    angle = inv[:, None] * np.arange(S, dtype=np.float32)[None, :]
    cos, sin = np.cos(angle), np.sin(angle)
    return np.stack([np.tile(cos, (2 * HG, 1)), np.tile(np.concatenate([-sin, sin]), (HG, 1))]).astype(np.float32)


def kernel(**inputs):
    import concourse.bacc as bacc
    from concourse.bass_utils import run_bass_kernel_spmd

    a = {k: np.asarray(v) for k, v in inputs.items()}
    down = a["L0_ffn_w_down"].reshape(C, P, IC // C, 512).transpose(2, 0, 1, 3).reshape(IC, P, 512)
    arrays = {
        "in_x": a["x"],
        "in_ctxT": a["ctx_1024"].transpose(0, 2, 1),
        "in_wf": np.concatenate([a["L0_ffn_w_gate"].reshape(IC, P, E), a["L0_ffn_w_up"].reshape(IC, P, E), down]),
        "in_attn_w": np.stack([a[f"L0_xattn_W{m}"].T.reshape(C, P, E).transpose(1, 0, 2) for m in "qkvo"]),
        "in_b_qkv": np.stack([a[f"L0_xattn_b{m}"].reshape(C, P).T for m in "qkv"]),
        "in_b_o": np.broadcast_to(a["L0_xattn_bo"], (P, E)),
        "in_rope": rope_tables(),
    }
    arrays = {k: np.ascontiguousarray(v) for k, v in arrays.items()}
    nc = bacc.Bacc("TRN2", target_bir_lowering=False, num_devices=1)
    args = [nc.dram_tensor(k, v.shape, mybir.dt.from_np(v.dtype), kind="ExternalInput").ap() for k, v in arrays.items()]
    out = nc.dram_tensor("out", (B, S, E), F32, kind="ExternalOutput").ap()
    block_program(nc, *args, out)
    result = run_bass_kernel_spmd(nc, [arrays], core_ids=[0])
    return result.results[0]["out"]
```
